# Optimizing a Trainium2 kernel written in Bass

```python
import numpy as np
import jax
import jax.numpy as jnp

def _softmax(x, axis=-1):
    return jax.nn.softmax(x, axis=axis)

def _gelu(x):
    return jax.nn.gelu(x, approximate=True)

def _silu(x):
    return jax.nn.silu(x)

def _sigmoid(x):
    return jax.nn.sigmoid(x)

def _layernorm(x, axis=-1, eps=1e-05):
    m = jnp.mean(x, axis=axis, keepdims=True)
    v = jnp.var(x, axis=axis, keepdims=True)
    return (x - m) / jnp.sqrt(v + eps)

def _scatter_add(tgt, idx, src, axis=0):
    return tgt.at[idx].add(src)

def _segment_sum(src, seg, n):
    return jax.ops.segment_sum(src, seg, n)
kernel_name = 'mk_vit_tower_postln_d2_tok_img768_r4_dd375f'

def setup_inputs(seed: int=0):
    np.random.seed(seed)
    _w = jnp.asarray

    def _rec_inputs():
        import jax
        import jax.numpy as jnp
        _rk = jax.random.key(seed)
        x = jax.random.uniform(jax.random.fold_in(_rk, 1), (16, 3, 96, 96), jnp.float32, 0.0, 1)
        return x
    x = _rec_inputs()

    def _L0_tok_setup():
        import jax, jax.numpy as jnp
        import numpy as np
        B, C, H, W, P, D = (32, 3, 96, 96, 16, 192)
        N = H // P * (W // P)
        key = jax.random.key(seed)
        k0, k1, k2, k3 = jax.random.split(key, 4)
        x = jax.random.uniform(k0, (B, C, H, W), dtype=jnp.float32)
        proj_w = jax.random.normal(k1, (D, P * P * C), dtype=jnp.float32) * 0.02
        proj_b = jnp.zeros((D,), jnp.float32)
        cls_token = jax.random.normal(k2, (1, 1, D), dtype=jnp.float32)
        pos_embedding = jax.random.normal(k3, (1, N + 1, D), dtype=jnp.float32)
        return {'x': x, 'proj_w': proj_w, 'proj_b': proj_b, 'cls_token': cls_token, 'pos_embedding': pos_embedding}
    _L0_tok_all = _L0_tok_setup()
    _L0_tok_in = {k: v for k, v in _L0_tok_all.items() if k in ('proj_w', 'proj_b', 'cls_token', 'pos_embedding')}
    del _L0_tok_all

    def _L0_attn_setup():
        import jax, jax.numpy as jnp
        import numpy as np
        D_MODEL = 192
        N_HEADS = 12
        D_HEAD = D_MODEL // N_HEADS
        B, T = (2, 1024)

        def _split_heads(t):
            Bc, Tc, _ = t.shape
            return t.reshape(Bc, Tc, N_HEADS, D_HEAD).transpose(0, 2, 1, 3)
        key = jax.random.key(seed)
        ks = jax.random.split(key, 9)
        s = 1.0 / np.sqrt(D_MODEL)
        x = jax.random.normal(ks[0], (B, T, D_MODEL), dtype=jnp.float32)
        Wq = jax.random.uniform(ks[1], (D_MODEL, D_MODEL), jnp.float32, -s, s)
        Wk = jax.random.uniform(ks[2], (D_MODEL, D_MODEL), jnp.float32, -s, s)
        Wv = jax.random.uniform(ks[3], (D_MODEL, D_MODEL), jnp.float32, -s, s)
        Wo = jax.random.uniform(ks[4], (D_MODEL, D_MODEL), jnp.float32, -s, s)
        bq = jax.random.uniform(ks[5], (D_MODEL,), jnp.float32, -s, s)
        bk = jax.random.uniform(ks[6], (D_MODEL,), jnp.float32, -s, s)
        bv = jax.random.uniform(ks[7], (D_MODEL,), jnp.float32, -s, s)
        bo = jax.random.uniform(ks[8], (D_MODEL,), jnp.float32, -s, s)
        return {'x': x, 'Wq': Wq, 'bq': bq, 'Wk': Wk, 'bk': bk, 'Wv': Wv, 'bv': bv, 'Wo': Wo, 'bo': bo}
    _L0_attn_all = _L0_attn_setup()
    _L0_attn_in = {k: v for k, v in _L0_attn_all.items() if k in ('Wq', 'bq', 'Wk', 'bk', 'Wv', 'bv', 'Wo', 'bo')}
    del _L0_attn_all

    def _L0_ffn_setup():
        import jax, jax.numpy as jnp
        import numpy as np
        B, L, D, H, F = (4, 512, 192, 12, 768)
        ROUTE_FRAC = 0.15
        LN_EPS = 1e-05

        def _ln(x, g, b):
            m = jnp.mean(x, axis=-1, keepdims=True)
            v = jnp.mean((x - m) ** 2, axis=-1, keepdims=True)
            return (x - m) * jax.lax.rsqrt(v + LN_EPS) * g + b
        key = jax.random.key(seed)
        ks = jax.random.split(key, 20)
        s = 0.02
        return {'hidden_states': jax.random.normal(ks[0], (B, L, D), dtype=jnp.float32), 'g1': jnp.ones((D,), jnp.float32), 'b1': jnp.zeros((D,), jnp.float32), 'g2': jnp.ones((D,), jnp.float32), 'b2': jnp.zeros((D,), jnp.float32), 'Wr': jax.random.normal(ks[1], (D,), jnp.float32) * s, 'br': jnp.zeros((), jnp.float32), 'Wq': jax.random.normal(ks[2], (D, D), jnp.float32) * s, 'bq': jnp.zeros((D,), jnp.float32), 'Wk': jax.random.normal(ks[3], (D, D), jnp.float32) * s, 'bk': jnp.zeros((D,), jnp.float32), 'Wv': jax.random.normal(ks[4], (D, D), jnp.float32) * s, 'bv': jnp.zeros((D,), jnp.float32), 'Wo': jax.random.normal(ks[5], (D, D), jnp.float32) * s, 'bo': jnp.zeros((D,), jnp.float32), 'Wm': jax.random.normal(ks[6], (D, D), jnp.float32) * s, 'bm': jnp.zeros((D,), jnp.float32), 'W1': jax.random.normal(ks[7], (D, F), jnp.float32) * s, 'bf1': jnp.zeros((F,), jnp.float32), 'W2': jax.random.normal(ks[8], (F, D), jnp.float32) * s, 'bf2': jnp.zeros((D,), jnp.float32)}
    _L0_ffn_all = _L0_ffn_setup()
    _L0_ffn_in = {k: v for k, v in _L0_ffn_all.items() if k in ('g1', 'b1', 'g2', 'b2', 'Wr', 'br', 'Wq', 'bq', 'Wk', 'bk', 'Wv', 'bv', 'Wo', 'bo', 'Wm', 'bm', 'W1', 'bf1', 'W2', 'bf2')}
    del _L0_ffn_all

    def _L1_attn_setup():
        import jax, jax.numpy as jnp
        import numpy as np
        NB_REF = 10
        HEADS = 12
        STEPS = 3
        TAU = 0.5
        LN_EPS = 1e-05
        COS_EPS = 1e-08

        def _encoder(z, fc1_w, fc1_b, fc2_w, fc2_b):
            h = jax.nn.gelu(z @ fc1_w + fc1_b, approximate=False)
            return h @ fc2_w + fc2_b

        def _layernorm(z, g, b):
            mu = jnp.mean(z, axis=-1, keepdims=True)
            var = jnp.mean(jnp.square(z - mu), axis=-1, keepdims=True)
            return (z - mu) * jax.lax.rsqrt(var + LN_EPS) * g + b

        def _projector_mask(x, ref, fc1_w, fc1_b, fc2_w, fc2_b):
            ex = _encoder(x, fc1_w, fc1_b, fc2_w, fc2_b)
            er = _encoder(ref, fc1_w, fc1_b, fc2_w, fc2_b)
            nx = jnp.maximum(jnp.linalg.norm(ex, axis=-1), COS_EPS)
            nr = jnp.maximum(jnp.linalg.norm(er, axis=-1), COS_EPS)
            cos = jnp.einsum('bne,rne->bnr', ex, er) / (nx[:, :, None] * nr.T[None])
            c = (jnp.mean(cos, axis=2) + 1.0) / 2.0
            return (0.5 + 0.5 * jnp.tanh(25.0 * (c - TAU)))[:, :, None]

        def _diffuser(x, ref, qv_w, k_w, proj_w, proj_b, ln_g, ln_b):
            B, N, C = x.shape
            hd = C // HEADS
            scale = hd ** (-0.5)
            k = (ref @ k_w).reshape(NB_REF, N, HEADS, hd).transpose(0, 2, 1, 3)
            for _ in range(STEPS):
                qv = (x @ qv_w).reshape(B, N, 2, HEADS, hd).transpose(2, 0, 3, 1, 4)
                q, v = (qv[0], qv[1])
                attn = jnp.einsum('bhnd,rhmd->brhnm', q, k) * scale
                attn = jnp.einsum('brhnm,brhkm->brhnk', attn, attn)
                o = jnp.einsum('brhnk,bhkd->brhnd', attn, v)
                o = o.reshape(B, NB_REF, N, C)
                x = jnp.mean(o.transpose(0, 2, 3, 1), axis=-1)
                x = _layernorm(x @ proj_w + proj_b, ln_g, ln_b)
            return x
        key = jax.random.key(seed)
        ks = jax.random.split(key, 11)
        D, B, N = (192, 8, 197)
        s = 0.02
        return {'x': jax.random.normal(ks[0], (B + NB_REF, N, D), jnp.float32), 'qv_w': jax.random.normal(ks[1], (D, 2 * D), jnp.float32) * s, 'k_w': jax.random.normal(ks[2], (D, D), jnp.float32) * s, 'proj_w': jax.random.normal(ks[3], (D, D), jnp.float32) * s, 'proj_b': jnp.zeros((D,), jnp.float32), 'ln_g': jnp.ones((D,), jnp.float32), 'ln_b': jnp.zeros((D,), jnp.float32), 'fc1_w': jax.random.normal(ks[4], (D, D // 4), jnp.float32) * s, 'fc1_b': jnp.zeros((D // 4,), jnp.float32), 'fc2_w': jax.random.normal(ks[5], (D // 4, D // 8), jnp.float32) * s, 'fc2_b': jnp.zeros((D // 8,), jnp.float32)}
    _L1_attn_all = _L1_attn_setup()
    _L1_attn_in = {k: v for k, v in _L1_attn_all.items() if k in ('qv_w', 'k_w', 'proj_w', 'proj_b', 'ln_g', 'ln_b', 'fc1_w', 'fc1_b', 'fc2_w', 'fc2_b')}
    del _L1_attn_all

    def _L1_ffn_setup():
        import jax, jax.numpy as jnp
        import numpy as np
        B, S, D = (2, 256, 192)
        NF, NR, R, DS, K = (128, 128, 128, 64, 4)

        @jax.checkpoint
        def feature_fn(x, neurons, weights):
            all_h = jnp.einsum('bsd,ndr->bsnr', x, neurons)
            return jnp.einsum('bsnr,bsn->bsr', all_h, weights)

        @jax.checkpoint
        def restore_fn(h, neurons, weights):
            all_out = jnp.einsum('bsr,nrd->bsnd', h, neurons)
            return jnp.einsum('bsnd,bsn->bsd', all_out, weights)

        def topk_sparsify(weights, k):
            topk_vals, topk_idx = jax.lax.top_k(weights, k)
            N = weights.shape[-1]
            one_hot_mask = jax.nn.one_hot(topk_idx, N, dtype=weights.dtype)
            sparse = (one_hot_mask * topk_vals[..., jnp.newaxis]).sum(axis=-2)
            sparse = sparse / (sparse.sum(axis=-1, keepdims=True) + 1e-08)
            return (sparse, topk_idx)
        key = jax.random.key(seed)
        ks = jax.random.split(key, 8)
        x = jax.random.normal(ks[0], (B, S, D), jnp.float32)
        f_know = jax.random.normal(ks[1], (NF, D, R), jnp.float32) * 0.02
        r_know = jax.random.normal(ks[2], (NR, R, D), jnp.float32) * 0.02
        W_fk = jax.random.normal(ks[3], (D, DS), jnp.float32) * 0.02
        b_fk = jnp.zeros((DS,), jnp.float32)
        W_rk = jax.random.normal(ks[4], (D, DS), jnp.float32) * 0.02
        b_rk = jnp.zeros((DS,), jnp.float32)
        emb_fk = jax.random.normal(ks[5], (NF, DS), jnp.float32) * 0.02
        emb_rk = jax.random.normal(ks[6], (NR, DS), jnp.float32) * 0.02
        return {'x': x, 'f_know': f_know, 'r_know': r_know, 'W_fk': W_fk, 'b_fk': b_fk, 'W_rk': W_rk, 'b_rk': b_rk, 'emb_fk': emb_fk, 'emb_rk': emb_rk}
    _L1_ffn_all = _L1_ffn_setup()
    _L1_ffn_in = {k: v for k, v in _L1_ffn_all.items() if k in ('f_know', 'r_know', 'W_fk', 'b_fk', 'W_rk', 'b_rk', 'emb_fk', 'emb_rk')}
    del _L1_ffn_all
    return {'x': x, 'L0_tok_proj_w': _L0_tok_in['proj_w'], 'L0_tok_proj_b': _L0_tok_in['proj_b'], 'L0_tok_cls_token': _L0_tok_in['cls_token'], 'L0_tok_pos_embedding': _L0_tok_in['pos_embedding'], 'L0_attn_Wq': _L0_attn_in['Wq'], 'L0_attn_bq': _L0_attn_in['bq'], 'L0_attn_Wk': _L0_attn_in['Wk'], 'L0_attn_bk': _L0_attn_in['bk'], 'L0_attn_Wv': _L0_attn_in['Wv'], 'L0_attn_bv': _L0_attn_in['bv'], 'L0_attn_Wo': _L0_attn_in['Wo'], 'L0_attn_bo': _L0_attn_in['bo'], 'L0_ffn_g1': _L0_ffn_in['g1'], 'L0_ffn_b1': _L0_ffn_in['b1'], 'L0_ffn_g2': _L0_ffn_in['g2'], 'L0_ffn_b2': _L0_ffn_in['b2'], 'L0_ffn_Wr': _L0_ffn_in['Wr'], 'L0_ffn_br': _L0_ffn_in['br'], 'L0_ffn_Wq': _L0_ffn_in['Wq'], 'L0_ffn_bq': _L0_ffn_in['bq'], 'L0_ffn_Wk': _L0_ffn_in['Wk'], 'L0_ffn_bk': _L0_ffn_in['bk'], 'L0_ffn_Wv': _L0_ffn_in['Wv'], 'L0_ffn_bv': _L0_ffn_in['bv'], 'L0_ffn_Wo': _L0_ffn_in['Wo'], 'L0_ffn_bo': _L0_ffn_in['bo'], 'L0_ffn_Wm': _L0_ffn_in['Wm'], 'L0_ffn_bm': _L0_ffn_in['bm'], 'L0_ffn_W1': _L0_ffn_in['W1'], 'L0_ffn_bf1': _L0_ffn_in['bf1'], 'L0_ffn_W2': _L0_ffn_in['W2'], 'L0_ffn_bf2': _L0_ffn_in['bf2'], 'L1_attn_qv_w': _L1_attn_in['qv_w'], 'L1_attn_k_w': _L1_attn_in['k_w'], 'L1_attn_proj_w': _L1_attn_in['proj_w'], 'L1_attn_proj_b': _L1_attn_in['proj_b'], 'L1_attn_ln_g': _L1_attn_in['ln_g'], 'L1_attn_ln_b': _L1_attn_in['ln_b'], 'L1_attn_fc1_w': _L1_attn_in['fc1_w'], 'L1_attn_fc1_b': _L1_attn_in['fc1_b'], 'L1_attn_fc2_w': _L1_attn_in['fc2_w'], 'L1_attn_fc2_b': _L1_attn_in['fc2_b'], 'L1_ffn_f_know': _L1_ffn_in['f_know'], 'L1_ffn_r_know': _L1_ffn_in['r_know'], 'L1_ffn_W_fk': _L1_ffn_in['W_fk'], 'L1_ffn_b_fk': _L1_ffn_in['b_fk'], 'L1_ffn_W_rk': _L1_ffn_in['W_rk'], 'L1_ffn_b_rk': _L1_ffn_in['b_rk'], 'L1_ffn_emb_fk': _L1_ffn_in['emb_fk'], 'L1_ffn_emb_rk': _L1_ffn_in['emb_rk']}

def reference(x, L0_tok_proj_w, L0_tok_proj_b, L0_tok_cls_token, L0_tok_pos_embedding, L0_attn_Wq, L0_attn_bq, L0_attn_Wk, L0_attn_bk, L0_attn_Wv, L0_attn_bv, L0_attn_Wo, L0_attn_bo, L0_ffn_g1, L0_ffn_b1, L0_ffn_g2, L0_ffn_b2, L0_ffn_Wr, L0_ffn_br, L0_ffn_Wq, L0_ffn_bq, L0_ffn_Wk, L0_ffn_bk, L0_ffn_Wv, L0_ffn_bv, L0_ffn_Wo, L0_ffn_bo, L0_ffn_Wm, L0_ffn_bm, L0_ffn_W1, L0_ffn_bf1, L0_ffn_W2, L0_ffn_bf2, L1_attn_qv_w, L1_attn_k_w, L1_attn_proj_w, L1_attn_proj_b, L1_attn_ln_g, L1_attn_ln_b, L1_attn_fc1_w, L1_attn_fc1_b, L1_attn_fc2_w, L1_attn_fc2_b, L1_ffn_f_know, L1_ffn_r_know, L1_ffn_W_fk, L1_ffn_b_fk, L1_ffn_W_rk, L1_ffn_b_rk, L1_ffn_emb_fk, L1_ffn_emb_rk):
    import jax
    import jax.numpy as jnp

    def _L0_tok_ref(x, proj_w, proj_b, cls_token, pos_embedding):
        import jax, jax.numpy as jnp
        import numpy as np
        B, C, H, W, P, D = (32, 3, 96, 96, 16, 192)
        N = H // P * (W // P)
        b, c, h, w = x.shape
        hp, wp = (h // P, w // P)
        patches = x.reshape(b, c, hp, P, wp, P).transpose(0, 2, 4, 1, 3, 5).reshape(b, hp * wp, c * P * P)
        tok = jnp.einsum('bnk,dk->bnd', patches, proj_w) + proj_b
        cls = jnp.broadcast_to(cls_token, (b, 1, cls_token.shape[-1]))
        z0 = jnp.concatenate([cls, tok], axis=1) + pos_embedding
        return z0

    def _L0_attn_ref(x, Wq, bq, Wk, bk, Wv, bv, Wo, bo):
        import jax, jax.numpy as jnp
        import numpy as np
        D_MODEL = 192
        N_HEADS = 12
        D_HEAD = D_MODEL // N_HEADS
        B, T = (2, 1024)

        def _split_heads(t):
            Bc, Tc, _ = t.shape
            return t.reshape(Bc, Tc, N_HEADS, D_HEAD).transpose(0, 2, 1, 3)
        scale = D_HEAD ** (-0.5)
        Q = _split_heads(x @ Wq.T + bq)
        K = _split_heads(x @ Wk.T + bk)
        V = _split_heads(x @ Wv.T + bv)
        scores = jnp.einsum('bhqd,bhkd->bhqk', Q, K) * scale
        attn = jax.nn.softmax(scores, axis=-1)
        out = jnp.einsum('bhqk,bhkd->bhqd', attn, V)
        out = out.transpose(0, 2, 1, 3).reshape(x.shape[0], x.shape[1], D_MODEL)
        return out @ Wo.T + bo

    def _L0_ffn_ref(hidden_states, g1, b1, g2, b2, Wr, br, Wq, bq, Wk, bk, Wv, bv, Wo, bo, Wm, bm, W1, bf1, W2, bf2):
        import jax, jax.numpy as jnp
        import numpy as np
        B, L, D, H, F = (4, 512, 192, 12, 768)
        ROUTE_FRAC = 0.15
        LN_EPS = 1e-05

        def _ln(x, g, b):
            m = jnp.mean(x, axis=-1, keepdims=True)
            v = jnp.mean((x - m) ** 2, axis=-1, keepdims=True)
            return (x - m) * jax.lax.rsqrt(v + LN_EPS) * g + b
        b, l, d = hidden_states.shape
        dh = d // H
        normed = _ln(hidden_states, g1, b1)
        scores = jax.nn.sigmoid(jnp.einsum('bld,d->bl', normed, Wr) + br)
        k = max(1, int(round(ROUTE_FRAC * l)))
        _, idx = jax.lax.top_k(-scores, k)
        attn_mask = jnp.zeros((b, l), bool).at[jnp.arange(b)[:, None], idx].set(True)
        q = (normed @ Wq + bq).reshape(b, l, H, dh)
        kk = (normed @ Wk + bk).reshape(b, l, H, dh)
        v = (normed @ Wv + bv).reshape(b, l, H, dh)
        logits = jnp.einsum('blhd,bmhd->bhlm', q, kk) / jnp.sqrt(jnp.float32(dh))
        probs = jax.nn.softmax(logits, axis=-1)
        ctx = jnp.einsum('bhlm,bmhd->blhd', probs, v).reshape(b, l, d)
        attn_out = ctx @ Wo + bo
        w = scores / (jnp.sum(scores, axis=1, keepdims=True) + 1e-06)
        pooled = jnp.einsum('bl,bld->bd', w, normed)
        mix_out = (normed + scores[..., None] * pooled[:, None, :]) @ Wm + bm
        merged = jnp.where(attn_mask[..., None], attn_out, mix_out)
        h = hidden_states + merged
        n2 = _ln(h, g2, b2)
        ffn = jax.nn.gelu(n2 @ W1 + bf1, approximate=False) @ W2 + bf2
        return h + ffn

    def _L1_attn_ref(x, qv_w, k_w, proj_w, proj_b, ln_g, ln_b, fc1_w, fc1_b, fc2_w, fc2_b):
        import jax, jax.numpy as jnp
        import numpy as np
        NB_REF = 10
        HEADS = 12
        STEPS = 3
        TAU = 0.5
        LN_EPS = 1e-05
        COS_EPS = 1e-08

        def _encoder(z, fc1_w, fc1_b, fc2_w, fc2_b):
            h = jax.nn.gelu(z @ fc1_w + fc1_b, approximate=False)
            return h @ fc2_w + fc2_b

        def _layernorm(z, g, b):
            mu = jnp.mean(z, axis=-1, keepdims=True)
            var = jnp.mean(jnp.square(z - mu), axis=-1, keepdims=True)
            return (z - mu) * jax.lax.rsqrt(var + LN_EPS) * g + b

        def _projector_mask(x, ref, fc1_w, fc1_b, fc2_w, fc2_b):
            ex = _encoder(x, fc1_w, fc1_b, fc2_w, fc2_b)
            er = _encoder(ref, fc1_w, fc1_b, fc2_w, fc2_b)
            nx = jnp.maximum(jnp.linalg.norm(ex, axis=-1), COS_EPS)
            nr = jnp.maximum(jnp.linalg.norm(er, axis=-1), COS_EPS)
            cos = jnp.einsum('bne,rne->bnr', ex, er) / (nx[:, :, None] * nr.T[None])
            c = (jnp.mean(cos, axis=2) + 1.0) / 2.0
            return (0.5 + 0.5 * jnp.tanh(25.0 * (c - TAU)))[:, :, None]

        def _diffuser(x, ref, qv_w, k_w, proj_w, proj_b, ln_g, ln_b):
            B, N, C = x.shape
            hd = C // HEADS
            scale = hd ** (-0.5)
            k = (ref @ k_w).reshape(NB_REF, N, HEADS, hd).transpose(0, 2, 1, 3)
            for _ in range(STEPS):
                qv = (x @ qv_w).reshape(B, N, 2, HEADS, hd).transpose(2, 0, 3, 1, 4)
                q, v = (qv[0], qv[1])
                attn = jnp.einsum('bhnd,rhmd->brhnm', q, k) * scale
                attn = jnp.einsum('brhnm,brhkm->brhnk', attn, attn)
                o = jnp.einsum('brhnk,bhkd->brhnd', attn, v)
                o = o.reshape(B, NB_REF, N, C)
                x = jnp.mean(o.transpose(0, 2, 3, 1), axis=-1)
                x = _layernorm(x @ proj_w + proj_b, ln_g, ln_b)
            return x
        xm, ref = (x[:-NB_REF], jax.lax.stop_gradient(x[-NB_REF:]))
        correct_m = _projector_mask(xm, ref, fc1_w, fc1_b, fc2_w, fc2_b)
        corrected = _diffuser(xm * correct_m, ref, qv_w, k_w, proj_w, proj_b, ln_g, ln_b)
        out = correct_m * corrected + (1.0 - correct_m) * xm
        return jnp.concatenate((out, ref), axis=0)

    def _L1_ffn_ref(x, f_know, r_know, W_fk, b_fk, W_rk, b_rk, emb_fk, emb_rk):
        import jax, jax.numpy as jnp
        import numpy as np
        B, S, D = (2, 256, 192)
        NF, NR, R, DS, K = (128, 128, 128, 64, 4)

        @jax.checkpoint
        def feature_fn(x, neurons, weights):
            all_h = jnp.einsum('bsd,ndr->bsnr', x, neurons)
            return jnp.einsum('bsnr,bsn->bsr', all_h, weights)

        @jax.checkpoint
        def restore_fn(h, neurons, weights):
            all_out = jnp.einsum('bsr,nrd->bsnd', h, neurons)
            return jnp.einsum('bsnd,bsn->bsd', all_out, weights)

        def topk_sparsify(weights, k):
            topk_vals, topk_idx = jax.lax.top_k(weights, k)
            N = weights.shape[-1]
            one_hot_mask = jax.nn.one_hot(topk_idx, N, dtype=weights.dtype)
            sparse = (one_hot_mask * topk_vals[..., jnp.newaxis]).sum(axis=-2)
            sparse = sparse / (sparse.sum(axis=-1, keepdims=True) + 1e-08)
            return (sparse, topk_idx)
        emb_fk_n = emb_fk / (jnp.linalg.norm(emb_fk, axis=-1, keepdims=True) + 1e-08)
        emb_rk_n = emb_rk / (jnp.linalg.norm(emb_rk, axis=-1, keepdims=True) + 1e-08)
        logits_fk = jnp.einsum('bsd,nd->bsn', x @ W_fk + b_fk, emb_fk_n)
        logits_rk = jnp.einsum('bsd,nd->bsn', x @ W_rk + b_rk, emb_rk_n)
        w_fk, _ = topk_sparsify(jax.nn.softmax(logits_fk, axis=-1), K)
        w_rk, _ = topk_sparsify(jax.nn.softmax(logits_rk, axis=-1), K)
        h = feature_fn(x, f_know, w_fk)
        out = restore_fn(h, r_know, w_rk)
        return out
    h = _L0_tok_ref(x, L0_tok_proj_w, L0_tok_proj_b, L0_tok_cls_token, L0_tok_pos_embedding)
    h = _layernorm(h + _L0_attn_ref(h, L0_attn_Wq, L0_attn_bq, L0_attn_Wk, L0_attn_bk, L0_attn_Wv, L0_attn_bv, L0_attn_Wo, L0_attn_bo), axis=-1)
    h = _layernorm(h + _L0_ffn_ref(h, L0_ffn_g1, L0_ffn_b1, L0_ffn_g2, L0_ffn_b2, L0_ffn_Wr, L0_ffn_br, L0_ffn_Wq, L0_ffn_bq, L0_ffn_Wk, L0_ffn_bk, L0_ffn_Wv, L0_ffn_bv, L0_ffn_Wo, L0_ffn_bo, L0_ffn_Wm, L0_ffn_bm, L0_ffn_W1, L0_ffn_bf1, L0_ffn_W2, L0_ffn_bf2), axis=-1)
    h = _layernorm(h + _L1_attn_ref(h, L1_attn_qv_w, L1_attn_k_w, L1_attn_proj_w, L1_attn_proj_b, L1_attn_ln_g, L1_attn_ln_b, L1_attn_fc1_w, L1_attn_fc1_b, L1_attn_fc2_w, L1_attn_fc2_b), axis=-1)
    h = _layernorm(h + _L1_ffn_ref(h, L1_ffn_f_know, L1_ffn_r_know, L1_ffn_W_fk, L1_ffn_b_fk, L1_ffn_W_rk, L1_ffn_b_rk, L1_ffn_emb_fk, L1_ffn_emb_rk), axis=-1)
    return h

_drawn_inputs = setup_inputs


def setup_inputs(seed=0):
    import zlib

    import numpy as np

    out = dict(_drawn_inputs(seed))
    spreads = {'L0_tok_proj_b': (0.0, 0.1),
     'L0_ffn_g1': (1.0, 0.2),
     'L0_ffn_b1': (0.0, 0.439),
     'L0_ffn_g2': (1.0, 0.6),
     'L0_ffn_b2': (0.0, 0.8),
     'L0_ffn_bq': (0.0, 0.8),
     'L0_ffn_bk': (0.0, 0.8),
     'L0_ffn_bv': (0.0, 0.8),
     'L0_ffn_bo': (0.0, 0.412),
     'L0_ffn_bm': (0.0, 0.1),
     'L0_ffn_bf1': (0.0, 0.509),
     'L0_ffn_bf2': (0.0, 0.1),
     'L1_attn_proj_b': (0.0, 0.1),
     'L1_attn_ln_g': (1.0, 0.2),
     'L1_attn_ln_b': (0.0, 0.1),
     'L1_attn_fc1_b': (0.0, 0.1),
     'L1_attn_fc2_b': (0.0, 0.1),
     'L1_ffn_b_fk': (0.0, 0.647),
     'L1_ffn_b_rk': (0.0, 0.633)}
    factors = {'L0_attn_bq': 8.0,
     'L0_attn_bk': 8.0,
     'L0_ffn_Wq': 8.0,
     'L0_ffn_Wk': 8.0,
     'L0_ffn_Wv': 8.0,
     'L0_ffn_Wo': 7.791,
     'L1_ffn_f_know': 3.625,
     'L1_ffn_r_know': 3.587,
     'L1_ffn_W_fk': 3.702,
     'L1_ffn_W_rk': 3.725,
     'L1_ffn_emb_fk': 3.643,
     'L1_ffn_emb_rk': 3.662}
    for name, (base, spread) in spreads.items():
        noise = np.random.default_rng([zlib.crc32(name.encode()), seed]).standard_normal(out[name].shape)
        drawn = base * np.exp(spread * noise) if base else spread * noise
        out[name] = jnp.asarray(drawn.astype(out[name].dtype))
    for name, factor in factors.items():
        out[name] = (out[name] * factor).astype(out[name].dtype)
    return out
```

```python
from contextlib import ExitStack

import numpy as np

import concourse.bass as bass
from concourse import mybir

ALU = mybir.AluOpType
ACT = mybir.ActivationFunctionType
AX = mybir.AxisListType.X
F32 = mybir.dt.float32
BF16 = mybir.dt.bfloat16
I32 = mybir.dt.int32
U32 = mybir.dt.uint32

P = 128
NB, NT, D = 16, 37, 192
T = NB * NT
HALF = D // 2
HEADS, DH = 12, 16
GROUPS, GF = 4, 3 * DH
TT = 3 * NT
TILES = -(-NB // 3)
PAD = TILES * TT
LAST = T - (TILES - 1) * TT
CH = T // 2
F = 768
ENC1, ENC2 = 48, 24
XM = 6
XT_ = XM * NT
REFS = NB - XM
ROUTED = 6
EPS = 1e-5
NN, R, TOPK = 128, 128, 4
PAIRS = T * TOPK
SLOT = 64
EXTRA = (PAIRS - NN) // SLOT + 1
TRASH = PAIRS + SLOT
PCOLS = TRASH + SLOT
PTILES = -(-PAIRS // P)
PLAST = PAIRS - (PTILES - 1) * P
SENTINEL = 3e38
HID_BANKS = [(t, min(t + 4, PTILES)) for t in range(0, PTILES, 4)]
OUT_BANKS = [(t, min(t + 2, PTILES)) for t in range(0, PTILES, 2)]

_WIDTHS = [("ident", P), ("same", TT), ("earlier", TT), ("upto", TT), ("spread", 3 * TT), ("vmask", GF), ("headof", 6),
           ("imageof", 3), ("headblock", HALF), ("before", P), ("sametoken", TT), ("steps64", 10), ("slots", EXTRA),
           ("slots64", EXTRA), ("neuron", 1)]
CONST = {}
_at = 0
for _name, _w in _WIDTHS:
    CONST[_name] = (_at, _w)
    _at += _w
NCONST = _at


def constants():
    p, c = np.arange(P)[:, None], np.arange(3 * TT)[None]
    t, u = c[:, :TT], c[:, :P]
    e = np.arange(EXTRA)[None]
    parts = {
        "ident": p == u,
        "same": p // NT == t // NT,
        "earlier": (p // NT == t // NT) & (t < p),
        "upto": p <= t,
        "spread": np.concatenate([p == NT * b + t % NT for b in range(3)], axis=1),
        "vmask": p // NT == c[:, :GF] // DH,
        "headof": p // DH == c[:, :6],
        "imageof": p // NT == c[:, :3],
        "headblock": p // DH == c[:, :HALF] // DH,
        "before": p < u,
        "sametoken": p % NT == t % NT,
        "steps64": SLOT * (1 + np.arange(10))[None] + 0 * p,
        "slots": e + 0 * p,
        "slots64": SLOT * (e + 1) - TRASH + 0 * p,
        "neuron": p,
    }
    return np.concatenate([np.asarray(parts[n], np.float32) for n, _ in _WIDTHS], axis=1)


G1, B1, G2, B2, LNG, LNB, TOKB, CLS, POS = 0, 2, 4, 6, 8, 10, 12, 14, 16
FC1B = POS + 2 * NT
NVEC = FC1B + 1
QV, KW, FC1, ROUTE = 0, 2 * D, 3 * D, 3 * D + ENC1
NDIFF = ROUTE + P
MIXW, RW = 3 * D, 4 * D
NATT2 = RW + TT


def vit_tower(nc, dram, out):
    with ExitStack() as ctx:
        def sb(name, shape, dt=F32):
            return ctx.enter_context(nc.sbuf_tensor(name, shape, dt))

        def sem(name):
            return ctx.enter_context(nc.semaphore(name))

        ps = ctx.enter_context(nc.psum_tensor("ps", [P, 8, 512], F32))

        def carve(base, shapes, start=0):
            views = []
            for rows, *dims in shapes:
                size = int(np.prod(dims))
                view = base[0:rows, start:start + size]
                names = "abc"[:len(dims)]
                if len(dims) > 1:
                    view = view.rearrange(f"p ({' '.join(names)}) -> p {' '.join(names)}", **dict(zip(names, dims)))
                views.append(view)
                start += size
            assert start <= base.shape[1], (start, base.shape)
            return views

        cst = sb("cst", [P, NCONST])
        vec = sb("vec", [HALF, NVEC])
        early = sb("early", [P, 4 * 8 * 2 * R])
        main = sb("main", [P, 29014])

        def const(name, rows=P):
            a, w = CONST[name]
            return cst[0:rows, a:a + w]

        ident = const("ident")

        patches, token_w = carve(early, [(P, 6, NB * (NT - 1)), (P, 6, D)])
        (hid,) = carve(early, [(P, 6, PAD)])

        xt = [sb(f"xt{n}", [HALF + 1, 2, PAD]) for n in range(3)]
        xt += xt[0:2]
        posb = sb("posb", [HALF, 2, NT])
        h1 = sb("h1", [TT, TILES, D])
        zln = sb("zln", [TT, TILES, D])
        n1 = sb("n1", [TT, TILES, D])
        h2 = sb("h2", [TT, TILES, D])
        hs = sb("hs", [TT, TILES, D])
        stats = sb("stats", [TT, TILES, 6])
        mv = sb("mv", [TT, TILES, 2])
        rstd = sb("rstd", [TT, TILES])
        power = sb("power", [TT, TILES])
        (w_a, w_b, wo_a, wo_b, w1, w2, qt, kt, kx, vtok, vx, shifted, probs, probsT, ctxT, h0, mixT, zb, sig) = carve(
            main, [(HALF + 1, 2, 3 * D), (HALF + 1, 2, NATT2), (P, 2, D), (P, 2, D), (HALF, 2, F), (P, 6, D),
                   (HALF, 2, T + 64 - NT), (HALF, 2, T), (HALF, 2, 6, T), (TT, TILES, D), (TT, NB, GROUPS, 64),
                   (P, 2, HEADS * NT), (P, 2, HEADS * NT), (TT, 2, 4 * P), (P, 2, PAD), (TT, TILES, D),
                   (HALF + 1, 2, PAD), (TT, PAD), (HALF, T)])
        attn_w, attn_wo = [w_a, w_b], [wo_a, wo_b]
        hp = h0
        weighed = kt
        smax = sb("smax", [P, 2, HEADS])
        ssum = sb("ssum", [P, 2, HEADS])
        sinv = sb("sinv", [P, 2, HEADS])
        sigsum = sb("sigsum", [HALF, NB])
        pooled = sb("pooled", [HALF, 2, NB])
        zcol = sb("zcol", [TT, TILES])
        below = sb("below", [TT, 2, TILES])
        takes = sb("takes", [TT, 2, TILES])
        scratch = zln[:].rearrange("p i d -> p (i d)")[:, 0:8 * P].rearrange("p (a b) -> p a b", b=P)
        b1 = sb("b1", [P, 6])
        b2 = sb("b2", [1, D])
        ones = sb("ones", [P, P])
        diff_w = sb("diff_w", [HALF + 1, 2, NDIFF])
        proj_w = sb("proj_w", [P, 3, D])
        diff_ln = sb("diff_ln", [TT, 2, D])
        enc_w2 = sb("enc_w2", [65, ENC2])
        (enc1, code, code2, ksb, gram, qtok, vmask, mblock, gmask, qd, xd, od, refsum) = carve(
            main, [(65, PAD), (TT, TILES, ENC2), (TT, TILES, ENC2), (TT, 4, D), (HALF, 2, HALF), (TT, 2, D),
                   (TT, 2, 3, D), (HALF, 2, XM, HALF), (HALF, 2, XM, HALF), (HALF, 2, XT_), (HALF + 1, 2, XT_),
                   (P, 3, XT_), (TT, ENC2)], start=14000)
        norm2 = sb("norm2", [TT, TILES])
        (feature_ring,) = carve(early, [(HALF, 4, 8, 2 * R)])
        (restore_ring,) = carve(early, [(P, 4, 8, D)])
        (xg, yg, hg, rows, logit, kept, expo, keyT, emb_block, count_wide, extra_f, extra_r, sel_f32, place) = carve(
            main, [(HALF, 2, PCOLS), (HALF, 2, PCOLS), (P, PCOLS), (P, PTILES, D), (TT, 2 * TILES, NN + 4),
                   (TT, 2 * TILES, NN + 4), (TT, 2 * TILES, NN), (P, PAD), (P, 2 * NN), (P, 2, TT), (HALF, 4, 2 * R),
                   (P, 4, D), (TT, TILES * NN), (TT, 2 * TILES, NN)])
        (got_h,) = carve(main, [(TT, TILES, TOPK, R)], start=2 * PCOLS)
        (got_y,) = carve(main, [(TT, TILES, TOPK, D)])
        chosen = sel_f32.bitcast(BF16).rearrange("p (q n) -> p q n", n=NN)
        mixed_h = hs[:, :, 0:R]
        emb = sb("emb", [P, 2, 64])
        emb2 = sb("emb2", [P, 2, 64])
        emb_n = sb("emb_n", [P, 2])
        half_p = sb("half_p", [P, 2])
        ones_bf = sb("ones_bf", [P, TT], BF16)
        upto_bf = sb("upto_bf", [TT, TT], BF16)
        top8 = sb("top8", [TT, 2 * TILES, 8])
        slot8 = sb("slot8", [TT, 2 * TILES, 8])
        slot = sb("slot", [TT, 2 * TILES, TOPK], U32)
        weight = sb("weight", [TT, 2 * TILES, TOPK])
        esum = sb("esum", [TT, 2 * TILES])
        counts = sb("counts", [P, 4])
        over = sb("over", [P, 2, 10])
        first = sb("first", [P, 4])
        reach = sb("reach", [P, 2])
        owns = sb("owns", [P, 3, EXTRA])
        table_f = sb("table_f", [P, 2, 2, EXTRA])
        table = sb("table", [1, 2, NN + 2 * EXTRA], I32)
        alike = sb("alike", [TT, 2])
        gate = sb("gate", [TT, 2, 2])

        xs = nc.dram_tensor("xs", (PAIRS, D), F32, kind="Internal").ap()
        hsd = nc.dram_tensor("hsd", (PAIRS, R), F32, kind="Internal").ap()
        hxs = nc.dram_tensor("hxs", (PAIRS, R), F32, kind="Internal").ap()
        ysd = nc.dram_tensor("ysd", (PAIRS, D), F32, kind="Internal").ap()
        in_const, in_vec, in_tok, in_w1, in_w2 = (sem(f"in_{n}") for n in ("const", "vec", "tok", "w1", "w2"))
        ready = sem("ready")
        dve_chain = sem("dve_chain")
        pool_chain = sem("pool_chain")
        tok_ps, tok_xt, h0_ps, h0_sb = sem("tok_ps"), sem("tok_xt"), sem("h0_ps"), sem("h0_sb")
        qk_ps, q_sb, k_sb, kx_sb = sem("qk_ps"), sem("q_sb"), sem("k_sb"), sem("kx_sb")
        v_ps, v_sb, vrep_ps, vx_sb = sem("v_ps"), sem("v_sb"), sem("vrep_ps"), sem("vx_sb")
        score_ps, score_used, exped, prob_sb = sem("score_ps"), sem("score_used"), sem("exped"), sem("prob_sb")
        probT_ps, probT_sb, ctx_ps, ctx_sb = sem("probT_ps"), sem("probT_sb"), sem("ctx_ps"), sem("ctx_sb")
        sum_rdy, inv_rdy = sem("sum_rdy"), sem("inv_rdy")
        att_ps = sem("att_ps")
        var_rdy, rstd_rdy = sem("var_rdy"), sem("rstd_rdy")
        ln_out = sem("ln_out")
        stored = sem("stored")
        in_ffn = sem("in_ffn")
        pads_rdy = sem("pads_rdy")
        turn_ps, xt_rdy = sem("turn_ps"), sem("xt_rdy")
        z_ps, z_sb, e_sb = sem("z_ps"), sem("z_sb"), sem("e_sb")
        sig_rdy, weighed_rdy, pooled_rdy, mixT_rdy = sem("sig_rdy"), sem("weighed_rdy"), sem("pooled_rdy"), sem("mixT_rdy")
        mix_ps, merged = sem("mix_ps"), sem("merged")
        in_diff, buf_rdy = sem("in_diff"), sem("buf_rdy")
        enc1_ps, enc1_sb, enc2_ps, norm_rdy, inorm_rdy = (sem(f"enc_{n}") for n in ("a", "b", "c", "d", "e"))
        code_rdy, refsum_ps, alike_rdy, tanh_rdy = sem("code_rdy"), sem("refsum_ps"), sem("alike_rdy"), sem("tanh_rdy")
        gated = sem("gated")
        k_ref_ps, k_ref_sb, gram_ps, gram_sb = sem("k_ref_ps"), sem("k_ref_sb"), sem("gram_ps"), sem("gram_sb")
        xd_ps, xd_sb, qv_ps, qd_ps, qtok_sb, qd_sb, vmask_sb = (sem(f"diff_{n}") for n in "abcdefg")
        qtok_ps = sem("qtok_ps")
        m_ps, m_sb, gm_ps, gm_sb, o_ps, o_sb_act, o_sb_dve, proj_ps = (sem(f"diff_{n}") for n in "hijklmno")
        in_emb, emb2_rdy, emb_root, emb_rdy, embT_ps, emb_sb = (sem(f"emb_{n}") for n in "abcdef")
        bf_rdy, moe_buf = sem("bf_rdy"), sem("moe_buf")
        key_ps, key_sb, logit_ps, logit_sb, chosen_rdy, count_ps, count_rdy, first_ps = (sem(f"route_{n}") for n in "abcdefgh")
        shift_rdy, expo_rdy, place_ps, slot_rdy, table_in, table_ps, table_rdy, weight_rdy = (
            sem(f"route_{n}") for n in "ijklmnop")
        place_used = sem("place_used")
        rows_in = [sem(f"rows_in{j}") for j in range(4)]
        scattered, turned_ps, turned_sb, backed_ps, backed_sb, stored_rows, gathered = (
            sem(f"pairs_{n}") for n in "abcdefg")
        ring_in = [[sem(f"ring{st}_{j}") for j in range(4)] for st in range(2)]
        extra_in = [[sem(f"extra{st}_{j}") for j in range(4)] for st in range(2)]
        product, taken = [sem("product0"), sem("product1")], [sem("taken0"), sem("taken1")]
        combined = sem("combined")
        hid_ps, hid_sb, ffn_ps, hs_rdy = sem("hid_ps"), sem("hid_sb"), sem("ffn_ps"), sem("hs_rdy")
        block = ctx.enter_context(nc.Block())

        def folded(i, j):
            to = od[32 * (j % 4):32 * (j % 4) + DH, j // 4, TT * i:TT * (i + 1)].rearrange("p (b n) -> p b n", b=3)
            return to, ps[0:DH, 3 * i:3 * i + 3, j:HEADS * NT:HEADS]

        PAIRS_OF_IMAGES = NB // 2

        @block.sync
        def _(sp):
            sp.dma_start(token_w[:], dram["token_w"]).then_inc(in_tok, 16)
            sp.dma_start(patches[:], dram["patches"]).then_inc(in_tok, 16)
            sp.dma_start(cst[:], dram["constants"]).then_inc(in_const, 16)
            sp.dma_start(vec[:], dram["vectors"]).then_inc(in_vec, 16)
            sp.dma_start(attn_w[0][:], dram["attn1_w"]).then_inc(in_w1, 16)
            sp.dma_start(attn_wo[0][:], dram["attn1_wo"]).then_inc(in_w1, 16)
            sp.dma_start(attn_w[1][:], dram["attn2_w"]).then_inc(in_w2, 16)
            sp.dma_start(attn_wo[1][:], dram["attn2_wo"]).then_inc(in_w2, 16)
            sp.dma_start(emb[:], dram["emb"]).then_inc(in_emb, 16)
            for t, n in ((w1, "ffn_w1"), (b1, "ffn_b1"), (w2, "ffn_w2"), (b2, "ffn_b2")):
                sp.dma_start(t[:], dram[n]).then_inc(in_ffn, 16)
            for t, n in ((diff_w, "diff_w"), (proj_w, "proj_w"), (diff_ln, "diff_ln"), (enc_w2, "enc_w2")):
                sp.dma_start(t[:], dram[n]).then_inc(in_diff, 16)
            sp.wait_ge(ffn_ps, 3)
            for j in range(4):
                sp.dma_start(feature_ring[:, j], dram["feature_w"][:, 8 * j:8 * j + 8, :]).then_inc(ring_in[0][j], 16)

            def tiles_of(d, a, b):
                return d[P * a:P * b, :].rearrange("(t p) f -> p t f", p=P)

            def pairs_in(st, d, width):
                sp.wait_ge(scattered, 16 * TOPK * TILES * (st + 1))
                for j in range(3):
                    sp.dma_start(rows[:, 6 * j:6 * j + 6, 0:width], tiles_of(d, 6 * j, 6 * j + 6)).then_inc(rows_in[j], 16)
                sp.dma_start(rows[0:PLAST, PTILES - 1, 0:width], d[P * (PTILES - 1):PAIRS, :]).then_inc(rows_in[3], 16)

            regs = [sp.alloc_register(f"sp_neuron{j}") for j in range(4)]

            def neurons(st, w, ring, extra):
                sp.wait_ge(table_rdy, 1)

                def further(i, wait):
                    sp.load(regs, table[0:1, st, bass.ds(NN + EXTRA + 4 * i, 4)])
                    for j in range(4):
                        n = sp.snap(regs[j], min_val=0, max_val=NN - 1)
                        if wait:
                            sp.wait_ge(product[st], 4 * i + j - 3)
                        sp.dma_start(extra[:, j, :], w[:, bass.ds(n, 1), :].rearrange("p o f -> p (o f)")).then_inc(
                            extra_in[st][j], 16)

                further(0, False)
                with sp.Fori(1, EXTRA // 4) as i:
                    further(i, True)
                with sp.Fori(1, NN // 32) as i:
                    for j in range(4):
                        sp.wait_ge(product[st], 32 * i + 8 * j + (EXTRA - 24))
                        sp.dma_start(ring[:, j], w[:, bass.ds(32 * i + 8 * j, 8), :]).then_inc(ring_in[st][j], 16)

            def pairs_back(st, d, width, parts):
                for n, (a, b) in enumerate(parts):
                    sp.wait_ge(backed_sb, (0, 5)[st] + n + 1)
                    last = b == PTILES
                    if b - last > a:
                        sp.dma_start(tiles_of(d, a, b - last), rows[:, a:b - last, 0:width]).then_inc(stored_rows, 16)
                    if last:
                        sp.dma_start(d[P * (PTILES - 1):PAIRS, :], rows[0:PLAST, PTILES - 1, 0:width]).then_inc(stored_rows, 16)

            pairs_in(0, xs, D)
            neurons(0, dram["feature_w"], feature_ring, extra_f)
            sp.wait_ge(product[0], EXTRA + NN)
            for j in range(4):
                sp.dma_start(restore_ring[:, j], dram["restore_w"][:, 8 * j:8 * j + 8, :]).then_inc(ring_in[1][j], 16)
            pairs_back(0, hsd, R, HID_BANKS)
            pairs_in(1, hxs, R)
            neurons(1, dram["restore_w"], restore_ring, extra_r)
            pairs_back(1, ysd, D, OUT_BANKS)
            flat = out.rearrange("b n d -> (b n) d")
            for i in range(TILES):
                n = TT if i < TILES - 1 else LAST
                sp.wait_ge(ln_out, 4 * TILES + 6 + TILES + i + 1)
                sp.dma_start(flat[TT * i:TT * i + n, :], hs[0:n, i, :]).then_inc(stored, 16)
            sp.wait_ge(stored, 16 * TILES)

        @block.gpsimd
        def _(pool):
            steps = [0]

            def link(ins):
                steps[0] += 1
                ins.then_inc(pool_chain, 1)
                pool.wait_ge(pool_chain, steps[0])

            for x in xt[0:3]:
                nc.gpsimd.memset(x[:, :, T:PAD], 0.0)
            nc.gpsimd.memset(qt[:, :, T:], 0.0)
            nc.gpsimd.memset(vx[:], 0.0)
            nc.gpsimd.memset(ctxT[:], 1.0)
            nc.gpsimd.memset(zb[:, T:PAD], 0.0)
            nc.gpsimd.memset(mixT[:, :, T:PAD], 0.0)
            nc.gpsimd.memset(ones[:], 1.0)
            nc.gpsimd.memset(half_p[:], 0.5)
            link(nc.gpsimd.memset(power[:], -0.5))
            for x in (*xt[0:3], mixT):
                ins = nc.gpsimd.memset(x[HALF:HALF + 1, :, :], 1.0)
            ins.then_inc(ready, 1)

            def softmax_products(a):
                for p in range(PAIRS_OF_IMAGES):
                    n = a * PAIRS_OF_IMAGES + p
                    pool.wait_ge(inv_rdy, n + 1)
                    if n >= 2:
                        pool.wait_ge(probT_ps, n - 1)
                    e = shifted[:, n % 2, :].rearrange("p (h k) -> p h k", h=HEADS)
                    nc.gpsimd.tensor_tensor(
                        probs[:, n % 2, :].rearrange("p (h k) -> p h k", h=HEADS), e,
                        sinv[:, n % 2, :].unsqueeze(2).to_broadcast([P, HEADS, NT]), ALU.mult).then_inc(prob_sb, 1)

            def root(n, tiles=TILES):
                pool.wait_ge(var_rdy, n + 1)
                nc.gpsimd.tensor_tensor(rstd[:, 0:tiles], rstd[:, 0:tiles], power[:, 0:tiles],
                                        ALU.pow).then_inc(rstd_rdy, 1)

            pool.wait_ge(in_const, 16)
            pool.wait_ge(ready, 1)
            link(nc.gpsimd.tensor_copy(ones_bf[:], ones[:, 0:TT]))
            nc.gpsimd.tensor_copy(upto_bf[:], const("upto", TT)).then_inc(bf_rdy, 1)
            pool.wait_ge(emb2_rdy, 1)
            pool.wait_ge(bf_rdy, 1)
            nc.gpsimd.tensor_tensor(emb_n[:], emb_n[:], half_p[:], ALU.pow).then_inc(emb_root, 1)
            softmax_products(0)
            root(0)
            root(1)
            nc.gpsimd.memset(hid[:, :, T:PAD], 0.0).then_inc(pads_rdy, 1)
            pool.wait_ge(sig_rdy, 1)
            pool.wait_ge(xt_rdy, 3)
            nc.gpsimd.tensor_tensor(weighed[:], xt[1][0:HALF, :, 0:T], sig[:].unsqueeze(1).to_broadcast([HALF, 2, T]),
                                    ALU.mult).then_inc(weighed_rdy, 1)
            softmax_products(1)
            pool.wait_ge(pooled_rdy, 1)
            for m in range(2):
                ins = nc.gpsimd.tensor_tensor(
                    weighed[:, m, :].rearrange("p (b t) -> p b t", b=NB), sig[:].rearrange("p (b t) -> p b t", b=NB),
                    pooled[:, m, :].unsqueeze(2).to_broadcast([HALF, NB, NT]), ALU.mult)
            link(ins)
            nc.gpsimd.tensor_tensor(mixT[0:HALF, :, 0:T], weighed[:], xt[1][0:HALF, :, 0:T],
                                    ALU.add).then_inc(mixT_rdy, 1)
            root(2)
            pool.wait_ge(merged, TILES)
            nc.gpsimd.tensor_tensor(hs[:], h1[:], hp[:], ALU.add).then_inc(hs_rdy, 1)
            pool.wait_ge(hs_rdy, 1)
            pool.wait_ge(ffn_ps, 1)
            link(nc.gpsimd.memset(enc1[:], 1.0))
            link(nc.gpsimd.memset(xd[HALF:HALF + 1, :, :], 1.0))
            ins = nc.gpsimd.memset(od[:], 1.0)
            ins.then_inc(buf_rdy, 1)
            pool.wait_ge(buf_rdy, 1)
            root(3)
            pool.wait_ge(norm_rdy, 1)
            nc.gpsimd.tensor_tensor(norm2[:], norm2[:], power[:], ALU.pow).then_inc(inorm_rdy, 1)
            for s in range(3):
                root(4 + s, 2)
            pool.wait_ge(xd_sb, 3)
            nc.gpsimd.memset(emb_block[:], 0.0)
            link(nc.gpsimd.memset(keyT[:, T:PAD], 0.0))
            nc.gpsimd.memset(logit[:, :, NN:NN + 4], SENTINEL).then_inc(moe_buf, 1)
            root(7)
            rows_of = [TT if i < TILES - 1 else LAST for i in range(TILES)]

            def scatter(st, src, d):
                pool.wait_ge(slot_rdy, st + 1)
                for i, n in enumerate(rows_of):
                    if st == 1:
                        pool.wait_ge(combined, i + 1)
                    for k in range(TOPK):
                        nc.gpsimd.indirect_dma_start(
                            out=d[:, :], out_offset=bass.IndirectOffsetOnAxis(ap=slot[0:n, 2 * i + st, k:k + 1], axis=0),
                            in_=src[0:n, i, :], in_offset=None).then_inc(scattered, 16)

            def gather(st, dst, d, stores):
                pool.wait_ge(stored_rows, 16 * stores)
                for i, n in enumerate(rows_of):
                    for k in range(TOPK):
                        nc.gpsimd.indirect_dma_start(
                            out=dst[0:n, i, k, :], out_offset=None, in_=d[:, :],
                            in_offset=bass.IndirectOffsetOnAxis(ap=slot[0:n, 2 * i + st, k:k + 1], axis=0)).then_inc(gathered, 16)

            pool.wait_ge(table_rdy, 1)
            link(nc.gpsimd.memset(xg[:, :, PAIRS:PCOLS], 0.0))
            nc.gpsimd.memset(hg[:, PAIRS:PCOLS], 0.0).then_inc(moe_buf, 1)
            pool.wait_ge(ln_out, 4 * TILES + 6 + TILES)
            scatter(0, h1, xs)
            gather(0, got_h, hsd, 6)
            scatter(1, mixed_h, hxs)
            gather(1, got_y, ysd, 16)
            root(8)

        @block.tensor
        def _(pe):
            def mm(dst, lhs, rhs, start=True, stop=True):
                return nc.tensor.matmul(dst, lhs, rhs, start=start, stop=stop)

            def projected(dst, w, x):
                mm(dst, w[0:HALF + 1, 0], x[0:HALF + 1, 0], stop=False)
                return mm(dst, w[0:HALF, 1], x[0:HALF, 1], start=False)

            def tokens():
                pe.wait_ge(in_tok, 32)
                for m in range(2):
                    for c in range(2):
                        for k in range(6):
                            ins = mm(ps[0:HALF, 2 * m + c, 0:8 * (NT - 1)], token_w[:, k, HALF * m:HALF * (m + 1)],
                                     patches[:, k, 8 * (NT - 1) * c:8 * (NT - 1) * (c + 1)], k == 0, k == 5)
                        ins.then_inc(tok_ps, 1)

            def turn_h0():
                pe.wait_ge(tok_xt, 5)
                pe.wait_ge(in_const, 16)
                for i in range(TILES):
                    for m in range(2):
                        ins = nc.tensor.transpose(
                            ps[0:TT, 4 + i // 2, D * (i % 2) + HALF * m:D * (i % 2) + HALF * (m + 1)],
                            xt[0][0:HALF, m, TT * i:TT * (i + 1)], ident[0:HALF, 0:HALF])
                    if i % 2:
                        ins.then_inc(h0_ps, 1)

            def turn_to_features(n, src, bank, need):
                for i in range(TILES):
                    pe.wait_ge(ln_out, need + i + 1)
                    for m in range(2):
                        at = TT * (2 * m + i % 2)
                        ins = nc.tensor.transpose(ps[0:HALF, bank + i // 2, at:at + TT],
                                                  src[:, i, HALF * m:HALF * (m + 1)], ident[0:TT, 0:TT])
                    if i % 2:
                        ins.then_inc(turn_ps, 1)

            def routing_logits(c):
                if c == 0:
                    pe.wait_ge(q_sb, 8)
                else:
                    pe.wait_ge(e_sb, 1)
                projected(ps[0:TT, 3, 0:CH], attn_w[1][:, :, RW:RW + TT],
                          xt[1][:, :, CH * c:CH * (c + 1)]).then_inc(z_ps, 1)

            def mix():
                for i in range(TILES):
                    if i == 0:
                        pe.wait_ge(mixT_rdy, 1)
                    ins = projected(ps[0:TT, 3 + i // 2, D * (i % 2):D * (i % 2 + 1)], mixT[:, :, TT * i:TT * (i + 1)],
                                    attn_w[1][:, :, MIXW:MIXW + D])
                    if i % 2:
                        ins.then_inc(mix_ps, 1)

            def feed_forward():
                pe.wait_ge(in_ffn, 64)
                pe.wait_ge(xt_rdy, 6)
                for k in range(6):
                    for c in range(2):
                        q = 2 * k + c
                        if q >= 4:
                            pe.wait_ge(hid_sb, q - 3)
                        bank = 3 + q % 4
                        mm(ps[:, bank, 0:CH], w1[:, 0, P * k:P * (k + 1)], xt[2][0:HALF, 0, CH * c:CH * (c + 1)],
                           stop=False)
                        mm(ps[:, bank, 0:CH], w1[:, 1, P * k:P * (k + 1)], xt[2][0:HALF, 1, CH * c:CH * (c + 1)],
                           start=False).then_inc(hid_ps, 1)
                pe.wait_ge(hid_sb, 12)
                pe.wait_ge(pads_rdy, 1)
                for i in range(TILES):
                    dst = ps[0:TT, i // 2, D * (i % 2):D * (i % 2 + 1)]
                    mm(dst, ones[0:1, 0:TT], b2[:], stop=False)
                    for k in range(6):
                        ins = mm(dst, hid[:, k, TT * i:TT * (i + 1)], w2[:, k, :], False, k == 5)
                    if i % 2:
                        ins.then_inc(ffn_ps, 1)

            def attention(a):
                w, x = attn_w[a], xt[a]
                pe.wait_ge((in_w1, in_w2)[a], 32)
                for which in range(2):
                    if which == 1 and a == 0:
                        pe.wait_ge(h0_sb, 3)
                        pe.wait_ge(emb_sb, 1)
                    for m in range(2):
                        for c in range(2):
                            at = D * which + HALF * m
                            projected(ps[0:HALF, 4 * which + 2 * m + c, 0:CH], w[:, :, at:at + HALF],
                                      x[:, :, CH * c:CH * (c + 1)]).then_inc(qk_ps, 1)
                for i in range(TILES):
                    if i % 2 == 0:
                        pe.wait_ge(q_sb, 4 * a + i // 2 + 1)
                    ins = projected(ps[0:TT, i // 2, D * (i % 2):D * (i % 2 + 1)], x[:, :, TT * i:TT * (i + 1)],
                                    w[:, :, 2 * D:3 * D])
                    if i % 2:
                        ins.then_inc(v_ps, 1)
                if a == 1:
                    routing_logits(0)
                for b in range(NB):
                    if b % 2 == 0:
                        j = b // 2
                        pe.wait_ge(k_sb, 4 * a + min(j, 3) + 1)
                        pe.wait_ge(v_sb, 3 * a + (b + 1) // 3 // 2 + 1)
                        if j >= 4:
                            pe.wait_ge(vx_sb, 8 * a + j - 3)
                    s = TT * (b % 3)
                    ins = mm(ps[0:TT, 4 + b // 2 % 4, D * (b % 2):D * (b % 2 + 1)],
                             const("spread", TT)[:, s:s + TT], vtok[:, b // 3, :])
                    if b % 2:
                        ins.then_inc(vrep_ps, 1)

                if a == 1:
                    routing_logits(1)

                def scores(p):
                    n = PAIRS_OF_IMAGES * a + p
                    if p == 0:
                        pe.wait_ge(q_sb, 4 * a + 4)
                        pe.wait_ge(kx_sb, a + 1)
                        pe.wait_ge(v_sb, 3 * a + 3)
                    if p >= 2:
                        pe.wait_ge(score_used, n - 1)
                    for y in range(2):
                        b = 2 * p + y
                        for m in range(2):
                            ins = mm(ps[64 * y:64 * y + 64, p % 2, 222 * m:222 * (m + 1)], qt[:, m, NT * b:NT * b + 64],
                                     kx[:, m, :, NT * b:NT * (b + 1)])
                    ins.then_inc(score_ps, 1)

                def turn(p):
                    n = PAIRS_OF_IMAGES * a + p
                    pe.wait_ge(prob_sb, n + 1)
                    if n >= 2:
                        pe.wait_ge(probT_sb, n - 1)
                    if a == 1 and p == 0:
                        pe.wait_ge(e_sb, 2)
                    for g in range(GROUPS):
                        ins = nc.tensor.transpose(ps[0:TT, 2 + p % 2, P * g:P * (g + 1)],
                                                  probs[:, n % 2, TT * g:TT * (g + 1)], ident)
                    ins.then_inc(probT_ps, 1)

                def contexts(p):
                    n = PAIRS_OF_IMAGES * a + p
                    pe.wait_ge(probT_sb, n + 1)
                    if p == 0:
                        pe.wait_ge(vx_sb, 8 * a + 8)
                    for y in range(2):
                        b = 2 * p + y
                        for g in range(GROUPS):
                            ins = mm(ps[64 * (g % 2):64 * (g % 2) + 64, 4 + 2 * (g // 2) + b // 8,
                                        NT * (b % 8):NT * (b % 8 + 1)],
                                     vx[:, b, g, :], probsT[:, n % 2, P * g + 64 * y:P * g + 64 * y + NT])
                    ins.then_inc(ctx_ps, 1)

                for s in range(PAIRS_OF_IMAGES + 2):
                    if s < PAIRS_OF_IMAGES:
                        scores(s)
                    if 1 <= s <= PAIRS_OF_IMAGES:
                        turn(s - 1)
                    if s >= 2:
                        contexts(s - 2)
                for i in range(TILES):
                    if i == 0:
                        pe.wait_ge(score_used, PAIRS_OF_IMAGES * (a + 1))
                        pe.wait_ge(probT_sb, PAIRS_OF_IMAGES * (a + 1))
                        pe.wait_ge(ctx_sb, 4 * a + 4)
                    dst = ps[0:TT, i // 2, D * (i % 2):D * (i % 2 + 1)]
                    mm(dst, ctxT[:, 0, TT * i:TT * (i + 1)], attn_wo[a][:, 0, :], stop=False)
                    ins = mm(dst, ctxT[:, 1, TT * i:TT * (i + 1)], attn_wo[a][:, 1, :], start=False)
                    if i % 2:
                        ins.then_inc(att_ps, 1)

            def encoder():
                pe.wait_ge(in_diff, 64)
                x = xt[3]
                for c in range(2):
                    projected(ps[0:ENC1, c, 0:CH], diff_w[:, :, FC1:FC1 + ENC1], x[:, :, CH * c:CH * (c + 1)]).then_inc(enc1_ps, 1)
                pe.wait_ge(enc1_sb, 2)
                for i in range(TILES):
                    ins = mm(ps[0:TT, 2, ENC2 * i:ENC2 * (i + 1)], enc1[:, TT * i:TT * (i + 1)], enc_w2[:])
                ins.then_inc(enc2_ps, 1)
                for i in range(2, TILES):
                    ins = projected(ps[0:TT, i // 2 - 1, D * (i % 2):D * (i % 2 + 1)], x[:, :, TT * i:TT * (i + 1)],
                                    diff_w[:, :, KW:KW + D])
                    if i % 2:
                        ins.then_inc(k_ref_ps, 1)
                pe.wait_ge(code_rdy, 1)
                for i in range(2, TILES):
                    n = TT if i < TILES - 1 else LAST
                    ins = mm(ps[0:TT, 7, 0:ENC2], const("sametoken", n), code2[0:n, i, :], i == 2, i == TILES - 1)
                ins.then_inc(refsum_ps, 1)
                pe.wait_ge(k_ref_sb, 2)
                for h in range(2):
                    for i in range(4):
                        n = TT if i < 3 else LAST
                        k = ksb[0:n, i, HALF * h:HALF * (h + 1)]
                        ins = mm(ps[0:HALF, 3, HALF * h:HALF * (h + 1)], k, k, i == 0, i == 3)
                ins.then_inc(gram_ps, 1)

            def diffuser_step(s):
                for i in range(2):
                    if s == 0:
                        pe.wait_ge(gated, 1)
                    else:
                        pe.wait_ge(ln_out, 4 * TILES + 2 * (s - 1) + i + 1)
                    for m in range(2):
                        ins = nc.tensor.transpose(ps[0:HALF, 4, XT_ * m + TT * i:XT_ * m + TT * (i + 1)],
                                                  n1[:, i, HALF * m:HALF * (m + 1)], ident[0:TT, 0:TT])
                ins.then_inc(xd_ps, 1)
                pe.wait_ge(xd_sb, s + 1)
                for i in range(2):
                    projected(ps[0:TT, i, 0:D], xd[:, :, TT * i:TT * (i + 1)],
                              diff_w[:, :, QV:QV + D]).then_inc(qtok_ps, 1)
                if s == 0:
                    pe.wait_ge(alike_rdy, 1)
                    pe.wait_ge(gram_sb, 1)
                for i in range(2):
                    projected(ps[0:TT, (3, 7)[i], 0:D], xd[:, :, TT * i:TT * (i + 1)],
                              diff_w[:, :, QV + D:QV + 2 * D]).then_inc(qv_ps, 1)
                for m in range(2):
                    ins = projected(ps[0:HALF, 2, XT_ * m:XT_ * (m + 1)],
                                    diff_w[:, :, QV + HALF * m:QV + HALF * (m + 1)], xd[:])
                ins.then_inc(qd_ps, 1)
                pe.wait_ge(qtok_sb, 2 * s + 2)
                for i in range(2):
                    pe.wait_ge(vmask_sb, 2 * s + i + 1)
                    for h in range(2):
                        ins = mm(ps[0:HALF, 4 + 2 * h + i, 0:3 * HALF], qtok[:, i, HALF * h:HALF * (h + 1)],
                                 vmask[:, i, :, HALF * h:HALF * (h + 1)])
                    ins.then_inc(m_ps, 1)
                for h in range(2):
                    for i in range(2):
                        pe.wait_ge(m_sb, 4 * s + 4)
                        mm(ps[0:HALF, (0, 1, 3, 4)[2 * h + i], 0:3 * HALF], gram[:, h, :],
                           mblock[:, h, 3 * i:3 * i + 3, :]).then_inc(gm_ps, 1)
                pe.wait_ge(qd_sb, s + 1)
                pe.wait_ge(gm_sb, 4 * s + 4)
                for b in range(XM):
                    for h in range(HEADS):
                        ins = mm(ps[0:DH, b, NT * h:NT * (h + 1)], gmask[:, h // 6, b, DH * (h % 6):DH * (h % 6 + 1)],
                                 qd[:, h // 6, NT * b:NT * (b + 1)])
                    if b % 3 == 2:
                        ins.then_inc(o_ps, 1)
                for i in range(2):
                    pe.wait_ge((o_sb_act, o_sb_dve)[i], s + 1)
                    for k in range(3):
                        ins = mm(ps[0:TT, 6, D * i:D * (i + 1)], od[:, k, TT * i:TT * (i + 1)], proj_w[:, k, :], k == 0, k == 2)
                ins.then_inc(proj_ps, 1)

            def route():
                pe.wait_ge(xt_rdy, 12)
                pe.wait_ge(moe_buf, 1)
                for c in range(2):
                    projected(ps[:, c, 0:CH], diff_w[:, :, ROUTE:ROUTE + P], xt[4][:, :, CH * c:CH * (c + 1)]).then_inc(key_ps, 1)
                pe.wait_ge(key_sb, 2)
                pe.wait_ge(emb_sb, 2)
                for i in range(TILES):
                    ins = mm(ps[0:TT, 2 + i // 2, 2 * NN * (i % 2):2 * NN * (i % 2 + 1)], keyT[:, TT * i:TT * (i + 1)], emb_block[:])
                    if i % 2:
                        ins.then_inc(logit_ps, 1)
                rows_of = [TT if i < TILES - 1 else LAST for i in range(TILES)]
                pe.wait_ge(chosen_rdy, 1)
                for r in range(2):
                    for i, n in enumerate(rows_of):
                        ins = mm(ps[:, 5, r:r + 1], chosen[0:n, 2 * i + r, :], ones_bf[0:n, 0:1], i == 0, i == TILES - 1)
                ins.then_inc(count_ps, 1)
                pe.wait_ge(count_rdy, 1)
                for i, n in enumerate(rows_of):
                    dst = ps[0:TT, 2 + i // 2, 2 * NN * (i % 2):2 * NN * (i % 2 + 1)]
                    for e in range(i):
                        mm(dst, ones_bf[0:TT, :], chosen[:, 2 * e:2 * e + 2, :], e == 0, False)
                    mm(dst, upto_bf[0:n, :], chosen[0:n, 2 * i:2 * i + 2, :], i == 0, False)
                    for r in range(2):
                        ins = mm(dst[:, NN * r:NN * (r + 1)], count_wide[:, r, :], const("before"), False, r == 1)
                    if i % 2:
                        ins.then_inc(place_ps, 1)
                mm(ps[:, 6, 0:4], const("before"), counts[:])
                for r in range(2):
                    ins = mm(ps[0:1, 7, NN * r:NN * (r + 1)], counts[:, r:r + 1], const("before"))
                ins.then_inc(first_ps, 1)
                pe.wait_ge(table_in, 1)
                mm(ps[0:1, 7, 2 * NN:2 * NN + 4 * EXTRA], ones[:, 0:1], table_f[:]).then_inc(table_ps, 1)

            def turn_pairs(st):
                for t in range(PTILES):
                    n = P if t < PTILES - 1 else PLAST
                    per, bank = (2, t // 2) if st == 0 else (4, t // 4)
                    if t % 6 == 0:
                        pe.wait_ge(rows_in[t // 6], 16 * st + 16)
                    if t % per == 0 and bank >= 4:
                        pe.wait_ge(turned_sb, (0, 10)[st] + bank - 3)
                    for m in range(2 - st):
                        at = 2 * P * (t % 2) + P * m if st == 0 else P * (t % 4)
                        w = HALF if st == 0 else R
                        ins = nc.tensor.transpose(ps[0:w, bank % 4, at:at + n], rows[0:n, t, w * m:w * (m + 1)], ident[0:n, 0:n])
                    if t % per == per - 1 or t == PTILES - 1:
                        ins.then_inc(turned_ps, 1)

            offs = [pe.alloc_register(f"pe_first{j}") for j in range(8)]

            def neurons(st, src, ring, extra):
                pe.wait_ge(table_rdy, 1)
                pe.wait_ge(turned_sb, (10, 15)[st])

                def one(w, at, bank):
                    if st == 0:
                        mm(ps[:, bank, 0:SLOT], w[:, 0:R], src[:, 0, bass.ds(at, SLOT)], stop=False)
                        ins = mm(ps[:, bank, 0:SLOT], w[:, R:2 * R], src[:, 1, bass.ds(at, SLOT)], start=False)
                    else:
                        for m in range(2):
                            ins = mm(ps[0:HALF, bank, SLOT * m:SLOT * (m + 1)], w[:, HALF * m:HALF * (m + 1)],
                                     src[:, bass.ds(at, SLOT)])
                    ins.then_inc(product[st], 1)

                def further(i, wait):
                    pe.load(offs[0:4], table[0:1, st, bass.ds(NN + 4 * i, 4)])
                    for j in range(4):
                        at = pe.snap(offs[j], min_val=0, max_val=TRASH)
                        if wait:
                            pe.wait_ge(taken[st], 4 * i + j - 3)
                        pe.wait_ge(extra_in[st][j], 16 * i + 16)
                        one(extra[:, j, :], at, 4 + j)

                further(0, False)
                with pe.Fori(1, EXTRA // 4) as i:
                    further(i, True)
                with pe.Fori(0, NN // 32) as i:
                    for g in range(4):
                        pe.load(offs, table[0:1, st, bass.ds(32 * i + 8 * g, 8)])
                        pe.wait_ge(ring_in[st][g], 16 * i + 16)
                        for j in range(8):
                            at = pe.snap(offs[j], min_val=0, max_val=PAIRS)
                            pe.wait_ge(taken[st], 32 * i + 8 * g + j + (EXTRA - 7))
                            one(ring[:, g, j, :], at, j)

            def back(st, src):
                pe.wait_ge(taken[st], EXTRA + NN)
                for n, (a, b) in enumerate((HID_BANKS, OUT_BANKS)[st]):
                    if n >= 4:
                        pe.wait_ge(backed_sb, (0, 5)[st] + n - 3)
                    for t in range(a, b):
                        for m in range(1 + st):
                            w = R if st == 0 else HALF
                            at = R * (t - a) if st == 0 else D * (t - a) + HALF * m
                            cols = src[:, P * t:P * (t + 1)] if st == 0 else src[:, m, P * t:P * (t + 1)]
                            ins = nc.tensor.transpose(ps[:, n % 4, at:at + w], cols, ident[0:w, 0:w])
                    ins.then_inc(backed_ps, 1)

            tokens()
            pe.wait_ge(in_const, 16)
            pe.wait_ge(emb_rdy, 1)
            nc.tensor.transpose(ps[:, 7, 0:P], emb2[:].rearrange("p r e -> p (r e)"), ident).then_inc(embT_ps, 1)
            turn_h0()
            pe.wait_ge(ready, 1)
            attention(0)
            turn_to_features(0, n1, 4, TILES)
            pe.wait_ge(xt_rdy, 3)
            attention(1)
            mix()
            turn_to_features(1, n1, 0, 2 * TILES)
            feed_forward()
            turn_to_features(2, h2, 4, 3 * TILES)
            pe.wait_ge(xt_rdy, 9)
            encoder()
            for s in range(3):
                diffuser_step(s)
            turn_to_features(3, h1, 0, 4 * TILES + 6)
            route()
            turn_pairs(0)
            neurons(0, xg, feature_ring, extra_f)
            back(0, hg)
            turn_pairs(1)
            neurons(1, hg, restore_ring, extra_r)
            back(1, yg)

        @block.scalar
        def _(act):
            def attention(a):
                for j in range(4):
                    act.wait_ge(qk_ps, 8 * a + j + 1)
                    m, c = j // 2, j % 2
                    nc.scalar.mul(qt[:, m, CH * c:CH * (c + 1)], ps[0:HALF, j, 0:CH], DH ** -0.5).then_inc(q_sb, 1)
                for j in range(3):
                    act.wait_ge(v_ps, 3 * a + j + 1)
                    nc.scalar.copy(vtok[:, 2 * j:2 * j + 2, :],
                                   ps[0:TT, j, 0:2 * D].rearrange("p (i d) -> p i d", i=2)).then_inc(v_sb, 1)
                if a == 1:
                    routing_logits(0)
                    routing_logits(1)
                for s in range(PAIRS_OF_IMAGES + 1):
                    if s < PAIRS_OF_IMAGES:
                        n = PAIRS_OF_IMAGES * a + s
                        act.wait_ge(score_used, n + 1)
                        nc.scalar.activation(shifted[:, n % 2, :], shifted[:, n % 2, :], ACT.Exp).then_inc(exped, 1)
                    if s >= 1:
                        n = PAIRS_OF_IMAGES * a + s - 1
                        act.wait_ge(probT_ps, n + 1)
                        if n >= 2:
                            act.wait_ge(ctx_ps, n - 1)
                        nc.scalar.copy(probsT[:, n % 2, :], ps[0:TT, 2 + n % 2, :]).then_inc(probT_sb, 1)
                for c in range(2):
                    act.wait_ge(ctx_ps, PAIRS_OF_IMAGES * a + 4 * (c + 1))
                    for m in range(2):
                        for g in range(2):
                            ins = nc.scalar.copy(ctxT[64 * g:64 * g + GF, m, CH * c:CH * (c + 1)],
                                                 ps[64 * g:64 * g + GF, 4 + 2 * m + c, 0:CH])
                        ins.then_inc(ctx_sb, 1)

            def to_features(n, dst, bank, gain=None, bias=None):
                for j in range(3):
                    act.wait_ge(turn_ps, 3 * n + j + 1)
                    src = ps[0:HALF, bank + j, 0:4 * TT].rearrange("p (m t) -> p m t", m=2)
                    to = dst[0:HALF, :, 2 * TT * j:2 * TT * (j + 1)]
                    if gain is None:
                        ins = nc.scalar.copy(to, src)
                    else:
                        for m in range(2):
                            ins = nc.scalar.activation(to[:, m], src[:, m], ACT.Identity,
                                                       scale=vec[:, gain + m:gain + m + 1],
                                                       bias=vec[:, bias + m:bias + m + 1])
                    ins.then_inc(xt_rdy, 1)

            def routing_logits(c):
                act.wait_ge(z_ps, c + 1)
                nc.scalar.copy(zb[:, CH * c:CH * (c + 1)], ps[0:TT, 3, 0:CH]).then_inc(z_sb, 1)
                nc.scalar.activation(sig[:, CH * c:CH * (c + 1)], ps[0:HALF, 3, 0:CH], ACT.Exp,
                                     scale=-1.0).then_inc(e_sb, 1)

            for j in range(3):
                act.wait_ge(h0_ps, j + 1)
                nc.scalar.copy(h0[:, 2 * j:2 * j + 2, :],
                               ps[0:TT, 4 + j, 0:2 * D].rearrange("p (i d) -> p i d", i=2)).then_inc(h0_sb, 1)
            act.wait_ge(ready, 1)
            attention(0)
            to_features(0, xt[1], 4, G1, B1)
            attention(1)
            to_features(1, xt[2], 0, G2, B2)
            for k in range(6):
                for c in range(2):
                    act.wait_ge(hid_ps, 2 * k + c + 1)
                    nc.scalar.activation(hid[:, k, CH * c:CH * (c + 1)], ps[:, 3 + (2 * k + c) % 4, 0:CH], ACT.Gelu,
                                         bias=b1[:, k:k + 1]).then_inc(hid_sb, 1)
            to_features(2, xt[3], 4)
            act.wait_ge(in_diff, 64)
            act.wait_ge(buf_rdy, 1)
            for c in range(2):
                act.wait_ge(enc1_ps, c + 1)
                nc.scalar.activation(enc1[0:ENC1, CH * c:CH * (c + 1)], ps[0:ENC1, c, 0:CH], ACT.Gelu,
                                     bias=vec[0:ENC1, FC1B:FC1B + 1]).then_inc(enc1_sb, 1)
            for j in range(2):
                act.wait_ge(k_ref_ps, j + 1)
                nc.scalar.copy(ksb[:, 2 * j:2 * j + 2, :],
                               ps[0:TT, j, 0:2 * D].rearrange("p (i d) -> p i d", i=2)).then_inc(k_ref_sb, 1)
            act.wait_ge(alike_rdy, 1)
            nc.scalar.activation(alike[:], alike[:], ACT.Tanh, scale=25.0 / (2 * REFS)).then_inc(tanh_rdy, 1)
            for s in range(3):
                act.wait_ge(xd_ps, s + 1)
                src = ps[0:HALF, 4, 0:2 * XT_].rearrange("p (m t) -> p m t", m=2)
                if s == 0:
                    nc.scalar.copy(xd[0:HALF], src).then_inc(xd_sb, 1)
                else:
                    for m in range(2):
                        ins = nc.scalar.activation(xd[0:HALF, m], src[:, m], ACT.Identity,
                                                   scale=vec[:, LNG + m:LNG + m + 1], bias=vec[:, LNB + m:LNB + m + 1])
                    ins.then_inc(xd_sb, 1)
                for i in range(2):
                    act.wait_ge(qtok_ps, 2 * s + i + 1)
                    nc.scalar.copy(qtok[:, i, :], ps[0:TT, i, 0:D]).then_inc(qtok_sb, 1)
                act.wait_ge(qd_ps, s + 1)
                nc.scalar.copy(qd[:], ps[0:HALF, 2, 0:2 * XT_].rearrange("p (m t) -> p m t", m=2)).then_inc(qd_sb, 1)
                for j in range(4):
                    act.wait_ge(gm_ps, 4 * s + j + 1)
                    nc.scalar.copy(gmask[:, j // 2, 3 * (j % 2):3 * (j % 2) + 3, :],
                                   ps[0:HALF, (0, 1, 3, 4)[j], 0:3 * HALF].rearrange("p (b f) -> p b f", b=3)).then_inc(gm_sb, 1)
                act.wait_ge(o_ps, 2 * s + 1)
                for j in range(HEADS):
                    ins = nc.scalar.copy(*folded(0, j))
                ins.then_inc(o_sb_act, 1)
            to_features(3, xt[4], 0)
            for c in range(2):
                act.wait_ge(key_ps, c + 1)
                nc.scalar.copy(keyT[:, CH * c:CH * (c + 1)], ps[:, c, 0:CH]).then_inc(key_sb, 1)
            for j in range(3):
                act.wait_ge(logit_ps, j + 1)
                nc.scalar.copy(logit[:, 4 * j:4 * j + 4, 0:NN],
                               ps[0:TT, 2 + j, :].rearrange("p (q n) -> p q n", n=NN)).then_inc(logit_sb, 1)
            act.wait_ge(shift_rdy, 1)
            nc.scalar.activation(expo[:], expo[:], ACT.Exp).then_inc(expo_rdy, 1)

            def turn_pairs(st):
                if st == 0:
                    act.wait_ge(moe_buf, 2)
                for n in range((10, 5)[st]):
                    act.wait_ge(turned_ps, (0, 10)[st] + n + 1)
                    if st == 0:
                        w = 2 * P if n < 9 else PLAST
                        to = xg[:, :, 2 * P * n:2 * P * n + w]
                        src = ps[0:HALF, n % 4, 0:4 * P].rearrange("p (t m c) -> p m t c", t=2, m=2)
                        if n < 9:
                            to = to.rearrange("p m (t c) -> p m t c", t=2)
                        else:
                            src = src[:, :, 0, 0:w]
                    else:
                        w = min(4 * P, PAIRS - 4 * P * n)
                        to, src = hg[:, 4 * P * n:4 * P * n + w], ps[:, n % 4, 0:w]
                    nc.scalar.copy(to, src).then_inc(turned_sb, 1)

            offs = [act.alloc_register(f"act_first{j}") for j in range(8)]

            def neurons(st, dst):
                act.wait_ge(table_rdy, 1)

                def one(count, at, bank):
                    act.wait_ge(product[st], count + 1)
                    if st == 0:
                        ins = nc.scalar.copy(dst[:, bass.ds(at, SLOT)], ps[:, bank, 0:SLOT])
                    else:
                        ins = nc.scalar.copy(dst[:, :, bass.ds(at, SLOT)],
                                             ps[0:HALF, bank, 0:2 * SLOT].rearrange("p (m c) -> p m c", m=2))
                    ins.then_inc(taken[st], 1)
                    act.wait_ge(taken[st], count + 1)

                with act.Fori(0, EXTRA // 4) as i:
                    act.load(offs[0:4], table[0:1, st, bass.ds(NN + 4 * i, 4)])
                    for j in range(4):
                        one(4 * i + j, act.snap(offs[j], min_val=0, max_val=TRASH), 4 + j)
                with act.Fori(0, NN // 8) as i:
                    act.load(offs, table[0:1, st, bass.ds(8 * i, 8)])
                    for j in range(8):
                        one(8 * i + j + EXTRA, act.snap(offs[j], min_val=0, max_val=PAIRS), j)

            def back(st):
                for n, (a, b) in enumerate((HID_BANKS, OUT_BANKS)[st]):
                    act.wait_ge(backed_ps, (0, 5)[st] + n + 1)
                    w = (R, D)[st]
                    nc.scalar.copy(rows[:, a:b, 0:w], ps[:, n % 4, 0:(b - a) * w].rearrange("p (t f) -> p t f", f=w)).then_inc(
                        backed_sb, 1)

            turn_pairs(0)
            neurons(0, hg)
            back(0)
            turn_pairs(1)
            neurons(1, yg)
            back(1)

        @block.vector
        def _(dve):
            steps = [0]

            def link(ins):
                steps[0] += 1
                ins.then_inc(dve_chain, 1)
                dve.wait_ge(dve_chain, steps[0])

            def embed():
                dve.wait_ge(in_vec, 16)
                pos = vec[:, POS:POS + 2 * NT].rearrange("p (m t) -> p m t", m=2)
                for m in range(2):
                    nc.vector.tensor_scalar(posb[:, m, 1:NT], pos[:, m, 1:NT], vec[:, TOKB + m:TOKB + m + 1], None, ALU.add)
                    ins = nc.vector.tensor_scalar(posb[:, m, 0:1], pos[:, m, 0:1], vec[:, CLS + m:CLS + m + 1], None,
                                                  ALU.add)
                link(ins)
                dve.wait_ge(ready, 1)
                xv = xt[0][0:HALF, :, 0:T].rearrange("p m (b t) -> p m b t", b=NB)
                for m in range(2):
                    ins = nc.vector.tensor_copy(xv[:, m, :, 0:1], posb[:, m, 0:1].unsqueeze(1).to_broadcast([HALF, NB, 1]))
                ins.then_inc(tok_xt, 1)
                for m in range(2):
                    for c in range(2):
                        dve.wait_ge(tok_ps, 2 * m + c + 1)
                        nc.vector.tensor_tensor(
                            xv[:, m, 8 * c:8 * c + 8, 1:NT],
                            ps[0:HALF, 2 * m + c, 0:8 * (NT - 1)].rearrange("p (b t) -> p b t", b=8),
                            posb[:, m, 1:NT].unsqueeze(1).to_broadcast([HALF, 8, NT - 1]), ALU.add).then_inc(tok_xt, 1)

            def attention(a):
                for j in range(4):
                    dve.wait_ge(qk_ps, 8 * a + 5 + j)
                    m, c = j // 2, j % 2
                    nc.vector.tensor_copy(kt[:, m, CH * c:CH * (c + 1)], ps[0:HALF, 4 + j, 0:CH]).then_inc(k_sb, 1)
                dve.wait_ge(k_sb, 4 * a + 4)
                for h in range(6):
                    ins = nc.vector.tensor_scalar(kx[:, :, h, :], kt[:], const("headof", HALF)[:, h:h + 1], None, ALU.mult)
                ins.then_inc(kx_sb, 1)
                for j in range(NB // 2):
                    dve.wait_ge(vrep_ps, 8 * a + j + 1)
                    nc.vector.tensor_tensor(
                        vx[:, 2 * j:2 * j + 2, :, 0:GF].rearrange("p b g f -> p (b g) f"),
                        ps[0:TT, 4 + j % 4, 0:2 * D].rearrange("p (x f) -> p x f", f=GF),
                        const("vmask", TT).unsqueeze(1).to_broadcast([TT, 2 * GROUPS, GF]), ALU.mult).then_inc(vx_sb, 1)

                if a == 1:
                    sigmoid()

                def top(p):
                    n = PAIRS_OF_IMAGES * a + p
                    dve.wait_ge(score_ps, n + 1)
                    s = ps[:, p % 2, 0:HEADS * NT].rearrange("p (h k) -> p h k", h=HEADS)
                    if n >= 2:
                        dve.wait_ge(prob_sb, n - 1)
                    link(nc.vector.tensor_reduce(smax[:, n % 2, :], s, AX, ALU.max))
                    nc.vector.tensor_tensor(
                        shifted[:, n % 2, :].rearrange("p (h k) -> p h k", h=HEADS), s,
                        smax[:, n % 2, :].unsqueeze(2).to_broadcast([P, HEADS, NT]), ALU.subtract).then_inc(score_used, 1)

                def total(p):
                    n = PAIRS_OF_IMAGES * a + p
                    dve.wait_ge(exped, n + 1)
                    link(nc.vector.tensor_reduce(ssum[:, n % 2, :], shifted[:, n % 2, :].rearrange("p (h k) -> p h k", h=HEADS),
                                                 AX, ALU.add))
                    nc.vector.reciprocal(sinv[:, n % 2, :], ssum[:, n % 2, :]).then_inc(inv_rdy, 1)

                for s in range(PAIRS_OF_IMAGES + 1):
                    if a == 1 and s == 1:
                        pool_inputs()
                    if a == 1 and s == 3:
                        ranks()
                    if s < PAIRS_OF_IMAGES:
                        top(s)
                    if s >= 1:
                        total(s - 1)

            def sigmoid():
                dve.wait_ge(e_sb, 2)
                link(nc.vector.tensor_scalar(sig[:], sig[:], 1.0, None, ALU.add))
                nc.vector.reciprocal(sig[:], sig[:]).then_inc(sig_rdy, 1)

            def pool_inputs():
                link(nc.vector.tensor_reduce(sigsum[:], sig[:].rearrange("p (b t) -> p b t", b=NB), AX, ALU.add))
                link(nc.vector.tensor_scalar(sigsum[:], sigsum[:], 1e-6, None, ALU.add))
                nc.vector.reciprocal(sigsum[:], sigsum[:])
                dve.wait_ge(weighed_rdy, 1)
                link(nc.vector.tensor_reduce(pooled[:], weighed[:].rearrange("p m (b t) -> p m b t", b=NB), AX, ALU.add))
                nc.vector.tensor_tensor(pooled[:], pooled[:], sigsum[:].unsqueeze(1).to_broadcast([HALF, 2, NB]),
                                        ALU.mult).then_inc(pooled_rdy, 1)

            def ranks():
                for i in range(TILES):
                    ins = nc.vector.tensor_tensor_reduce(scratch[:, i, 0:TT], zb[:, TT * i:TT * (i + 1)], ident[0:TT, 0:TT], 1.0,
                                                   0.0, ALU.mult, ALU.add, zcol[:, i:i + 1])
                link(ins)
                for i in range(TILES):
                    if i == 4:
                        link(ins)
                    for n, (op, mask) in enumerate(((ALU.is_lt, "same"), (ALU.is_equal, "earlier"))):
                        ins = nc.vector.scalar_tensor_tensor(
                            out=scratch[:, (2 * i + n) % 8, 0:TT], in0=zb[:, TT * i:TT * (i + 1)], scalar=zcol[:, i:i + 1],
                            in1=const(mask, TT), op0=op, op1=ALU.mult, accum_out=below[:, n, i:i + 1])
                link(ins)
                link(nc.vector.tensor_tensor(takes[:, 0], below[:, 0], below[:, 1], ALU.add))
                link(nc.vector.tensor_scalar(takes[:, 0], takes[:, 0], ROUTED - 0.5, None, ALU.is_lt))
                link(nc.vector.tensor_scalar(takes[:, 1], takes[:, 0], -1.0, 1.0, ALU.mult, ALU.add))

            def merge():
                for i in range(TILES):
                    if i % 2 == 0:
                        dve.wait_ge(att_ps, 3 + i // 2 + 1)
                    ins = nc.vector.scalar_tensor_tensor(
                        out=hp[:, i, :], in0=ps[0:TT, i // 2, D * (i % 2):D * (i % 2 + 1)], scalar=takes[:, 0, i:i + 1],
                        in1=h1[:, i, :], op0=ALU.mult, op1=ALU.add)
                link(ins)
                for i in range(TILES):
                    if i % 2 == 0:
                        dve.wait_ge(mix_ps, i // 2 + 1)
                    nc.vector.scalar_tensor_tensor(
                        out=hp[:, i, :], in0=ps[0:TT, 3 + i // 2, D * (i % 2):D * (i % 2 + 1)], scalar=takes[:, 1, i:i + 1],
                        in1=hp[:, i, :], op0=ALU.mult, op1=ALU.add).then_inc(merged, 1)

            def add_tokens(ready_at, base, bank, to, res):
                for j in range(3):
                    dve.wait_ge(ready_at, base + j + 1)
                    ins = nc.vector.tensor_tensor(to[:, 2 * j:2 * j + 2, :],
                                                  ps[0:TT, bank + j, 0:2 * D].rearrange("p (i d) -> p i d", i=2),
                                                  res[:, 2 * j:2 * j + 2, :], ALU.add)
                link(ins)

            def layer_norm(n, dst, src=zln, tiles=TILES):
                src = src if src is not None else ps[0:TT, 6, 0:2 * D].rearrange("p (i d) -> p i d", i=2)
                for i in range(tiles):
                    ins = nc.vector.bn_stats(stats[:, i, :], src[:, i, :])
                link(ins)
                for i in range(tiles):
                    ins = nc.vector.bn_aggr(mv[:, i, :], stats[:, i, :])
                link(ins)
                nc.vector.tensor_scalar(rstd[:, 0:tiles], mv[:, 0:tiles, 1], EPS, None, ALU.add).then_inc(var_rdy, 1)
                dve.wait_ge(rstd_rdy, n + 1)
                for i in range(tiles):
                    nc.vector.tensor_scalar(dst[:, i, :], src[:, i, :], mv[:, i, 0:1], rstd[:, i:i + 1], ALU.subtract,
                                            ALU.mult).then_inc(ln_out, 1)

            def embedding_norms():
                dve.wait_ge(in_emb, 16)
                link(nc.vector.tensor_tensor(emb2[:], emb[:], emb[:], ALU.mult))
                nc.vector.tensor_reduce(emb_n[:], emb2[:], AX, ALU.add).then_inc(emb2_rdy, 1)
                dve.wait_ge(emb_root, 1)
                link(nc.vector.tensor_scalar(emb_n[:], emb_n[:], 1e-8, None, ALU.add))
                link(nc.vector.reciprocal(emb_n[:], emb_n[:]))
                nc.vector.tensor_tensor(emb2[:], emb[:], emb_n[:].unsqueeze(2).to_broadcast([P, 2, 64]),
                                        ALU.mult).then_inc(emb_rdy, 1)

            def choose():
                for j in range(3):
                    dve.wait_ge(logit_sb, j + 1)
                    for q in range(4 * j, 4 * j + 4):
                        ins = nc.vector.max(top8[:, q, :], logit[:, q, 0:NN])
                link(ins)
                nc.vector.tensor_tensor(expo[:], logit[:, :, 0:NN], top8[:, :, 0:1].to_broadcast([TT, 2 * TILES, NN]),
                                        ALU.subtract).then_inc(shift_rdy, 1)
                dve.wait_ge(shift_rdy, 1)
                link(nc.vector.memset(top8[:, :, TOPK:8], SENTINEL))
                for q in range(2 * TILES):
                    ins = nc.vector.match_replace(kept[:, q, :], top8[:, q, :], logit[:, q, :], -SENTINEL)
                link(ins)
                nc.vector.tensor_tensor(chosen, logit[:, :, 0:NN], kept[:, :, 0:NN], ALU.not_equal).then_inc(chosen_rdy, 1)

            def tables():
                dve.wait_ge(count_ps, 1)
                link(nc.vector.tensor_copy(counts[:, 0:2], ps[:, 5, 0:2]))
                link(nc.vector.tensor_tensor(over[:], counts[:, 0:2].unsqueeze(2).to_broadcast([P, 2, 10]),
                                             const("steps64").unsqueeze(1).to_broadcast([P, 2, 10]), ALU.is_gt))
                nc.vector.tensor_reduce(counts[:, 2:4], over[:], AX, ALU.add)
                nc.vector.tensor_copy(count_wide[:], counts[:, 0:2].unsqueeze(2).to_broadcast([P, 2, TT])).then_inc(count_rdy, 1)

            def further_slots():
                dve.wait_ge(first_ps, 1)
                link(nc.vector.tensor_copy(first[:], ps[:, 6, 0:4]))
                link(nc.vector.tensor_tensor(reach[:], first[:, 2:4], counts[:, 2:4], ALU.add))
                link(nc.vector.scalar_tensor_tensor(out=first[:, 0:2], in0=first[:, 2:4], scalar=-float(SLOT),
                                                    in1=first[:, 0:2], op0=ALU.mult, op1=ALU.add))
                for r in range(2):
                    nc.vector.tensor_scalar(owns[:, 0], const("slots"), first[:, 2 + r:3 + r], None, ALU.is_ge)
                    link(nc.vector.tensor_scalar(owns[:, 1], const("slots"), reach[:, r:r + 1], None, ALU.is_lt))
                    link(nc.vector.tensor_tensor(owns[:, 2], owns[:, 0], owns[:, 1], ALU.mult))
                    nc.vector.scalar_tensor_tensor(out=table_f[:, r, 0, :], in0=const("slots64"), scalar=first[:, r:r + 1],
                                                   in1=owns[:, 2], op0=ALU.add, op1=ALU.mult)
                    ins = nc.vector.tensor_scalar(table_f[:, r, 1, :], owns[:, 2], const("neuron"), None, ALU.mult)
                    if r == 0:
                        link(ins)
                ins.then_inc(table_in, 1)
                dve.wait_ge(table_ps, 1)
                for r in range(2):
                    nc.vector.tensor_copy(table[:, r, 0:NN], ps[0:1, 7, NN * r:NN * (r + 1)])
                    at = 2 * NN + 2 * EXTRA * r
                    nc.vector.tensor_scalar(table[:, r, NN:NN + EXTRA], ps[0:1, 7, at:at + EXTRA], float(TRASH), None, ALU.add)
                    ins = nc.vector.tensor_copy(table[:, r, NN + EXTRA:], ps[0:1, 7, at + EXTRA:at + 2 * EXTRA])
                ins.then_inc(table_rdy, 1)

            def slots(r):
                for i in range(TILES):
                    ins = nc.vector.max(slot8[:, 2 * i + r, :], place[:, 2 * i + r, :])
                link(ins)
                nc.vector.tensor_scalar(slot[:, r::2, :], slot8[:, r::2, 0:TOPK], -1.0, None, ALU.add).then_inc(slot_rdy, 1)

            def weights():
                dve.wait_ge(expo_rdy, 1)
                nc.vector.tensor_reduce(esum[:], expo[:], AX, ALU.add)
                n = 0
                for q in range(2 * TILES):
                    for k in range(TOPK):
                        ins = nc.vector.scalar_tensor_tensor(
                            out=scratch[:, n % 8, 0:NN], in0=place[:, q, :], scalar=slot8[:, q, k:k + 1],
                            in1=expo[:, q, :], op0=ALU.is_equal, op1=ALU.mult, accum_out=weight[:, q, k:k + 1])
                        n += 1
                        if n % 8 == 0:
                            link(ins)
                link(nc.vector.reciprocal(esum[:], esum[:]))
                link(nc.vector.tensor_tensor(weight[:], weight[:], esum[:].unsqueeze(2).to_broadcast([TT, 2 * TILES, TOPK]),
                                             ALU.mult))
                link(nc.vector.tensor_reduce(esum[:], weight[:], AX, ALU.add))
                link(nc.vector.tensor_scalar(esum[:], esum[:], 1e-8, None, ALU.add))
                link(nc.vector.reciprocal(esum[:], esum[:]))
                link(nc.vector.tensor_tensor(weight[:], weight[:], esum[:].unsqueeze(2).to_broadcast([TT, 2 * TILES, TOPK]),
                                             ALU.mult))

            def combine(st, got, dst, base):
                rows_of = [TT if i < TILES - 1 else LAST for i in range(TILES)]
                dve.wait_ge(gathered, 16 * TOPK * TILES * (st + 1))
                for k in range(TOPK):
                    for i, n in enumerate(rows_of):
                        w = weight[0:n, 2 * i + st, k:k + 1]
                        if k == 0 and base is None:
                            ins = nc.vector.tensor_scalar(dst[0:n, i, :], got[0:n, i, k, :], w, None, ALU.mult)
                        else:
                            ins = nc.vector.scalar_tensor_tensor(
                                out=dst[0:n, i, :], in0=got[0:n, i, k, :], scalar=w,
                                in1=base[0:n, i, :] if k == 0 else dst[0:n, i, :], op0=ALU.mult, op1=ALU.add)
                        if st == 0 and k == TOPK - 1:
                            ins.then_inc(combined, 1)
                    if not (st == 0 and k == TOPK - 1):
                        link(ins)

            dve.wait_ge(in_const, 16)
            embedding_norms()
            embed()
            dve.wait_ge(embT_ps, 1)
            nc.vector.tensor_copy(emb2[:].rearrange("p r e -> p (r e)"), ps[:, 7, 0:P]).then_inc(emb_sb, 1)
            attention(0)
            add_tokens(att_ps, 0, 0, zln, h0)
            layer_norm(0, h1)
            dve.wait_ge(ln_out, TILES)
            layer_norm(1, n1, h1)
            attention(1)
            merge()
            dve.wait_ge(merged, TILES)
            layer_norm(2, n1, hp)
            dve.wait_ge(hs_rdy, 1)
            add_tokens(ffn_ps, 0, 0, zln, hs)
            layer_norm(3, h2)
            dve.wait_ge(enc2_ps, 1)
            link(nc.vector.tensor_copy(code[:], ps[0:TT, 2, 0:TILES * ENC2].rearrange("p (i e) -> p i e", i=TILES)))
            link(nc.vector.tensor_tensor(code2[:], code[:], code[:], ALU.mult))
            link(nc.vector.tensor_reduce(norm2[:], code2[:], AX, ALU.add))
            nc.vector.tensor_scalar(norm2[:], norm2[:], 1e-16, None, ALU.max).then_inc(norm_rdy, 1)
            dve.wait_ge(inorm_rdy, 1)
            nc.vector.tensor_tensor(code2[:], code[:], norm2[:].unsqueeze(2).to_broadcast([TT, TILES, ENC2]),
                                    ALU.mult).then_inc(code_rdy, 1)
            dve.wait_ge(refsum_ps, 1)
            dve.wait_ge(code_rdy, 1)
            link(nc.vector.tensor_tensor(code[:, 0:2], code2[:, 0:2],
                                         ps[0:TT, 7, 0:ENC2].unsqueeze(1).to_broadcast([TT, 2, ENC2]), ALU.mult))
            nc.vector.tensor_reduce(alike[:], code[:, 0:2], AX, ALU.add).then_inc(alike_rdy, 1)
            dve.wait_ge(gram_ps, 1)
            nc.vector.scalar_tensor_tensor(
                out=gram[:], in0=ps[0:HALF, 3, 0:2 * HALF].rearrange("p (h f) -> p h f", h=2), scalar=1.0 / (DH * REFS),
                in1=const("headblock", HALF).unsqueeze(1).to_broadcast([HALF, 2, HALF]), op0=ALU.mult,
                op1=ALU.mult).then_inc(gram_sb, 1)
            dve.wait_ge(tanh_rdy, 1)
            nc.vector.tensor_scalar(gate[:, 0], alike[:], 0.5, 0.5, ALU.mult, ALU.add)
            link(nc.vector.tensor_scalar(gate[:, 1], alike[:], -0.5, 0.5, ALU.mult, ALU.add))
            dve.wait_ge(ln_out, 4 * TILES)
            for i in range(2):
                ins = nc.vector.tensor_scalar(n1[:, i, :], h2[:, i, :], gate[:, 0, i:i + 1], None, ALU.mult)
            ins.then_inc(gated, 1)
            for i in range(2):
                nc.vector.scalar_tensor_tensor(out=hs[:, i, :], in0=h2[:, i, :], scalar=gate[:, 1, i:i + 1],
                                               in1=h2[:, i, :], op0=ALU.mult, op1=ALU.add)
            nc.vector.tensor_scalar(zln[:, 2:TILES, :], h2[:, 2:TILES, :], 2.0, None, ALU.mult)
            for s in range(3):
                for i in range(2):
                    dve.wait_ge(qv_ps, 2 * s + i + 1)
                    nc.vector.tensor_tensor(
                        vmask[:, i], ps[0:TT, (3, 7)[i], 0:D].unsqueeze(1).to_broadcast([TT, 3, D]),
                        const("imageof", TT).unsqueeze(2).to_broadcast([TT, 3, D]), ALU.mult).then_inc(vmask_sb, 1)
                for i in range(2):
                    dve.wait_ge(m_ps, 2 * s + i + 1)
                    for h in range(2):
                        nc.vector.tensor_tensor(
                            mblock[:, h, 3 * i:3 * i + 3, :],
                            ps[0:HALF, 4 + 2 * h + i, 0:3 * HALF].rearrange("p (b f) -> p b f", b=3),
                            const("headblock", HALF).unsqueeze(1).to_broadcast([HALF, 3, HALF]), ALU.mult).then_inc(m_sb, 1)
                dve.wait_ge(o_ps, 2 * s + 2)
                for j in range(HEADS):
                    ins = nc.vector.tensor_copy(*folded(1, j))
                ins.then_inc(o_sb_dve, 1)
                dve.wait_ge(proj_ps, s + 1)
                layer_norm(4 + s, n1, None, 2)
            dve.wait_ge(ln_out, 4 * TILES + 6)
            link(nc.vector.tensor_tensor(n1[:, 0:2], n1[:, 0:2], diff_ln[:, 0:1, :].to_broadcast([TT, 2, D]), ALU.mult))
            link(nc.vector.tensor_tensor(n1[:, 0:2], n1[:, 0:2], diff_ln[:, 1:2, :].to_broadcast([TT, 2, D]), ALU.add))
            for i in range(2):
                ins = nc.vector.scalar_tensor_tensor(out=zln[:, i, :], in0=n1[:, i, :], scalar=gate[:, 0, i:i + 1],
                                                     in1=hs[:, i, :], op0=ALU.mult, op1=ALU.add)
            link(ins)
            layer_norm(7, h1)
            dve.wait_ge(moe_buf, 1)
            for r in range(2):
                ins = nc.vector.tensor_copy(emb_block[64 * r:64 * (r + 1), NN * r:NN * (r + 1)],
                                            emb2[64 * r:64 * (r + 1)].rearrange("p r e -> p (r e)"))
            ins.then_inc(emb_sb, 1)
            choose()
            tables()
            for j in range(3):
                dve.wait_ge(place_ps, j + 1)
                ins = nc.vector.tensor_tensor(place[:, 4 * j:4 * j + 4, :], ps[0:TT, 2 + j, :].rearrange("p (q n) -> p q n", n=NN),
                                              chosen[:, 4 * j:4 * j + 4, :], ALU.mult)
            link(ins)
            slots(0)
            further_slots()
            slots(1)
            weights()
            combine(0, got_h, mixed_h, None)
            combine(1, got_y, zln, h1)
            layer_norm(8, hs)


def kernel(**inputs):
    import numpy as np
    import concourse.bacc as bacc
    from concourse import mybir
    from concourse.bass_utils import run_bass_kernel_spmd

    a = {k: np.asarray(v) for k, v in inputs.items()}
    f32 = np.float32

    def halves(w, bias=None, width=None):
        out = np.zeros((HALF + 1, 2, w.shape[1]), f32)
        out[:HALF] = w.reshape(2, HALF, -1).transpose(1, 0, 2)
        if bias is not None:
            out[HALF, 0] = bias
        return out

    def context_rows(w, bias):
        out = np.zeros((P, 2, D), f32)
        for g in range(GROUPS):
            out[64 * (g % 2):64 * (g % 2) + GF, g // 2] = w[GF * g:GF * (g + 1)]
        out[GF, 0] = bias
        return out

    def columns(v):
        return v.reshape(2, HALF).T

    pos = a["L0_tok_pos_embedding"][0].T.reshape(2, HALF, NT).transpose(1, 0, 2).reshape(HALF, 2 * NT)
    fc1_b = np.zeros((HALF, 1), f32)
    fc1_b[:ENC1, 0] = a["L1_attn_fc1_b"]
    vectors = np.concatenate(
        [columns(a["L0_ffn_g1"]), columns(a["L0_ffn_b1"]), columns(a["L0_ffn_g2"]), columns(a["L0_ffn_b2"]),
         columns(a["L1_attn_ln_g"]), columns(a["L1_attn_ln_b"]), columns(a["L0_tok_proj_b"]),
         columns(a["L0_tok_cls_token"][0, 0]), pos, fc1_b], axis=1)
    proj = np.zeros((P, 3, D), f32)
    for j in range(HEADS):
        proj[32 * (j % 4):32 * (j % 4) + DH, j // 4] = a["L1_attn_proj_w"][DH * j:DH * (j + 1)]
    proj[DH, 0] = a["L1_attn_proj_b"]
    fc2 = np.zeros((65, ENC2), f32)
    fc2[:ENC1] = a["L1_attn_fc2_w"]
    fc2[64] = a["L1_attn_fc2_b"]
    patches = a["x"].reshape(NB, 3, 6, 16, 6, 16).transpose(1, 3, 5, 0, 2, 4).reshape(6, P, NB * (NT - 1))
    wr = a["L0_ffn_Wr"].reshape(D, 1)
    arrays = {
        "constants": constants(),
        "vectors": vectors,
        "patches": patches.transpose(1, 0, 2),
        "token_w": a["L0_tok_proj_w"].T.reshape(6, P, D).transpose(1, 0, 2),
        "attn1_w": np.concatenate([halves(a[f"L0_attn_W{c}"].T, a[f"L0_attn_b{c}"]) for c in "qkv"], axis=2),
        "attn1_wo": context_rows(a["L0_attn_Wo"].T, a["L0_attn_bo"]),
        "attn2_w": np.concatenate(
            [halves(a[f"L0_ffn_W{c}"], a[f"L0_ffn_b{c}"]) for c in "qkvm"]
            + [halves(np.repeat(wr, TT, axis=1), a["L0_ffn_br"])], axis=2),
        "attn2_wo": context_rows(a["L0_ffn_Wo"], a["L0_ffn_bo"]),
        "ffn_w1": halves(a["L0_ffn_W1"])[:HALF],
        "ffn_b1": a["L0_ffn_bf1"].reshape(6, P).T,
        "ffn_w2": a["L0_ffn_W2"].reshape(6, P, D).transpose(1, 0, 2),
        "ffn_b2": a["L0_ffn_bf2"].reshape(1, D),
        "diff_w": np.concatenate(
            [halves(a["L1_attn_qv_w"]), halves(a["L1_attn_k_w"]),
             halves(a["L1_attn_fc1_w"]), halves(a["L1_ffn_W_fk"], a["L1_ffn_b_fk"]),
             halves(a["L1_ffn_W_rk"], a["L1_ffn_b_rk"])], axis=2),
        "diff_ln": np.stack([np.broadcast_to(a["L1_attn_ln_g"], (TT, D)), np.broadcast_to(a["L1_attn_ln_b"], (TT, D))], 1),
        "enc_w2": fc2,
        "proj_w": proj,
        "emb": np.stack([a["L1_ffn_emb_fk"], a["L1_ffn_emb_rk"]], axis=1),
        "feature_w": a["L1_ffn_f_know"].reshape(NN, 2, HALF, R).transpose(2, 0, 1, 3).reshape(HALF, NN, 2 * R),
        "restore_w": a["L1_ffn_r_know"].transpose(1, 0, 2),
    }
    arrays = {k: np.ascontiguousarray(v) for k, v in arrays.items()}
    nc = bacc.Bacc("TRN2", target_bir_lowering=False, num_devices=1)
    handles = {k: nc.dram_tensor(f"in_{k}", v.shape, mybir.dt.float32, kind="ExternalInput").ap() for k, v in arrays.items()}
    out = nc.dram_tensor("tower", (NB, NT, D), mybir.dt.float32, kind="ExternalOutput").ap()
    vit_tower(nc, handles, out)
    r = run_bass_kernel_spmd(nc, [{f"in_{k}": v for k, v in arrays.items()}], core_ids=[0])
    return r.results[0]["tower"]
```

```python
from contextlib import ExitStack

import numpy as np

import concourse.bass as bass
from concourse import mybir

ALU = mybir.AluOpType
ACT = mybir.ActivationFunctionType
AX = mybir.AxisListType.X
F32 = mybir.dt.float32
BF16 = mybir.dt.bfloat16
I32 = mybir.dt.int32
U32 = mybir.dt.uint32

P = 128
NB, NT, D = 16, 37, 192
T = NB * NT
HALF = D // 2
HEADS, DH = 12, 16
GROUPS, GF = 4, 3 * DH
TT = 3 * NT
TILES = -(-NB // 3)
PAD = TILES * TT
LAST = T - (TILES - 1) * TT
CH = T // 2
F = 768
ENC1, ENC2 = 48, 24
XM = 6
XT_ = XM * NT
REFS = NB - XM
ROUTED = 6
EPS = 1e-5
NN, R, TOPK = 128, 128, 4
PAIRS = T * TOPK
SLOT = 64
EXTRA = (PAIRS - NN) // SLOT + 1
SLOTS = NN + EXTRA
PCOLS = PAIRS + SLOT
PTILES = -(-PAIRS // P)
PLAST = PAIRS - (PTILES - 1) * P
SENTINEL = 3e38
QUAD = 4
QUADS, FURTHER = NN // QUAD, EXTRA // QUAD
RING = 8

_WIDTHS = [("ident", P), ("same", TT), ("earlier", TT), ("upto", TT), ("spread", 3 * TT), ("vmask", GF), ("headof", 6),
           ("imageof", 3), ("headblock", HALF), ("before", P), ("sametoken", TT), ("steps64", 10), ("slots", EXTRA),
           ("slots64", EXTRA), ("neuron", 1), ("rows64", NN), ("delta", 1)]
CONST = {}
_at = 0
for _name, _w in _WIDTHS:
    CONST[_name] = (_at, _w)
    _at += _w
NCONST = _at


def constants():
    p, c = np.arange(P)[:, None], np.arange(3 * TT)[None]
    t, u = c[:, :TT], c[:, :P]
    e = np.arange(EXTRA)[None]
    parts = {
        "ident": p == u,
        "same": p // NT == t // NT,
        "earlier": (p // NT == t // NT) & (t < p),
        "upto": p <= t,
        "spread": np.concatenate([p == NT * b + t % NT for b in range(3)], axis=1),
        "vmask": p // NT == c[:, :GF] // DH,
        "headof": p // DH == c[:, :6],
        "imageof": p // NT == c[:, :3],
        "headblock": p // DH == c[:, :HALF] // DH,
        "before": p < u,
        "sametoken": p % NT == t % NT,
        "steps64": SLOT * (1 + np.arange(10))[None] + 0 * p,
        "slots": e + 0 * p,
        "slots64": SLOT * (e + 1) + 0 * p,
        "neuron": p,
        "rows64": SLOT * u + 0 * p,
        "delta": SLOT * (NN - 1) - SLOT * p,
    }
    return np.concatenate([np.asarray(parts[n], np.float32) for n, _ in _WIDTHS], axis=1)


G1, B1, G2, B2, LNG, LNB, TOKB, CLS, POS = 0, 2, 4, 6, 8, 10, 12, 14, 16
FC1B = POS + 2 * NT
NVEC = FC1B + 1
QV, KW, FC1, ROUTE = 0, 2 * D, 3 * D, 3 * D + ENC1
NDIFF = ROUTE + P
MIXW, RW = 3 * D, 4 * D
NATT2 = RW + TT


def vit_tower(nc, dram, out):
    with ExitStack() as ctx:
        def sb(name, shape, dt=F32):
            return ctx.enter_context(nc.sbuf_tensor(name, shape, dt))

        def sem(name):
            return ctx.enter_context(nc.semaphore(name))

        ps = ctx.enter_context(nc.psum_tensor("ps", [P, 8, 512], F32))

        def carve(base, shapes, start=0):
            views = []
            for rows, *dims in shapes:
                size = int(np.prod(dims))
                view = base[0:rows, start:start + size]
                names = "abc"[:len(dims)]
                if len(dims) > 1:
                    view = view.rearrange(f"p ({' '.join(names)}) -> p {' '.join(names)}", **dict(zip(names, dims)))
                views.append(view)
                start += size
            assert start <= base.shape[1], (start, base.shape)
            return views

        cst = sb("cst", [P, NCONST])
        vec = sb("vec", [HALF, NVEC])
        early = sb("early", [P, 4 * 8 * 2 * R])
        main = sb("main", [P, 29014])

        def const(name, rows=P):
            a, w = CONST[name]
            return cst[0:rows, a:a + w]

        ident = const("ident")

        patches, token_w = carve(early, [(P, 6, NB * (NT - 1)), (P, 6, D)])
        (hid,) = carve(early, [(P, 6, PAD)])

        xt = [sb(f"xt{n}", [HALF + 1, 2, PAD]) for n in range(3)]
        xt += xt[0:2]
        posb = sb("posb", [HALF, 2, NT])
        h1 = sb("h1", [TT, TILES, D])
        zln = sb("zln", [TT, TILES, D])
        n1 = sb("n1", [TT, TILES, D])
        h2 = sb("h2", [TT, TILES, D])
        hs = sb("hs", [TT, TILES, D])
        stats = sb("stats", [TT, TILES, 6])
        mv = sb("mv", [TT, TILES, 2])
        rstd = sb("rstd", [TT, TILES])
        power = sb("power", [TT, TILES])
        (w_a, w_b, wo_a, wo_b, w1, w2, qt, kt, kx, vtok, vx, shifted, probs, probsT, ctxT, h0, mixT, zb, sig) = carve(
            main, [(HALF + 1, 2, 3 * D), (HALF + 1, 2, NATT2), (P, 2, D), (P, 2, D), (HALF, 2, F), (P, 6, D),
                   (HALF, 2, T + 64 - NT), (HALF, 2, T), (HALF, 2, 6, T), (TT, TILES, D), (TT, NB, GROUPS, 64),
                   (P, 2, HEADS * NT), (P, 2, HEADS * NT), (TT, 2, 4 * P), (P, 2, PAD), (TT, TILES, D),
                   (HALF + 1, 2, PAD), (TT, PAD), (HALF, T)])
        attn_w, attn_wo = [w_a, w_b], [wo_a, wo_b]
        hp = h0
        weighed = kt
        smax = sb("smax", [P, 2, HEADS])
        ssum = sb("ssum", [P, 2, HEADS])
        sinv = sb("sinv", [P, 2, HEADS])
        sigsum = sb("sigsum", [HALF, NB])
        pooled = sb("pooled", [HALF, 2, NB])
        zcol = sb("zcol", [TT, TILES])
        below = sb("below", [TT, 2, TILES])
        takes = sb("takes", [TT, 2, TILES])
        scratch = zln[:].rearrange("p i d -> p (i d)")[:, 0:8 * P].rearrange("p (a b) -> p a b", b=P)
        b1 = sb("b1", [P, 6])
        b2 = sb("b2", [1, D])
        ones = sb("ones", [P, P])
        diff_w = sb("diff_w", [HALF + 1, 2, NDIFF])
        proj_w = sb("proj_w", [P, 3, D])
        diff_ln = sb("diff_ln", [TT, 2, D])
        enc_w2 = sb("enc_w2", [65, ENC2])
        (enc1, code, code2, ksb, gram, qtok, vmask, mblock, gmask, qd, xd, od, refsum) = carve(
            main, [(65, PAD), (TT, TILES, ENC2), (TT, TILES, ENC2), (TT, 4, D), (HALF, 2, HALF), (TT, 2, D),
                   (TT, 2, 3, D), (HALF, 2, XM, HALF), (HALF, 2, XM, HALF), (HALF, 2, XT_), (HALF + 1, 2, XT_),
                   (P, 3, XT_), (TT, ENC2)], start=14000)
        norm2 = sb("norm2", [TT, TILES])
        (ring,) = carve(early, [(P, RING, QUAD * 2 * R)])
        (xg, hg, staged, products, extra, rows, logit, kept, expo, keyT, emb_block, count_wide, delta_wide, base, sel_f32,
         place, place_out) = carve(
            main, [(HALF, 2, PCOLS), (P, PCOLS), (P, 4 * QUAD, 2 * SLOT), (P, 4, 2 * D), (P, 3, QUAD * 2 * R),
                   (P, PTILES, D), (TT, 2 * TILES, NN + 4), (TT, 2 * TILES, NN + 4), (TT, 2 * TILES, NN), (P, PAD),
                   (P, 2 * NN), (P, 2, TT), (P, 2, TT), (TT, 2, 2, NN), (TT, TILES * NN), (TT, 2 * TILES, NN),
                   (TT, 2 * TILES, NN)])
        (got_y,) = carve(main, [(TT, TILES, TOPK, D)])
        got_h = rows[0:TT].rearrange("p t f -> p (t f)")[:, 0:TILES * TOPK * R].rearrange(
            "p (i k r) -> p i k r", i=TILES, k=TOPK)
        chosen = sel_f32.bitcast(BF16).rearrange("p (q n) -> p q n", n=NN)
        mixed_h = hs[:, :, 0:R]
        emb = sb("emb", [P, 2, 64])
        emb2 = sb("emb2", [P, 2, 64])
        emb_n = sb("emb_n", [P, 2])
        half_p = sb("half_p", [P, 2])
        ones_bf = sb("ones_bf", [P, TT], BF16)
        upto_bf = sb("upto_bf", [TT, TT], BF16)
        top8 = sb("top8", [TT, 2 * TILES, 8])
        slot8 = sb("slot8", [TT, 2 * TILES, 8])
        row_in = sb("row_in", [TT, 2 * TILES, TOPK], U32)
        row_out = sb("row_out", [TT, 2 * TILES, TOPK], U32)
        weight = sb("weight", [TT, 2 * TILES, TOPK])
        esum = sb("esum", [TT, 2 * TILES])
        counts = sb("counts", [P, 4])
        over = sb("over", [P, 2, 10])
        first = sb("first", [P, 4])
        reach = sb("reach", [P, 2])
        delta = sb("delta", [P, 2])
        owns = sb("owns", [P, 3, EXTRA])
        table_f = sb("table_f", [P, 2, 2, EXTRA])
        table = sb("table", [1, 2, NN + 2 * EXTRA], I32)
        alike = sb("alike", [TT, 2])
        gate = sb("gate", [TT, 2, 2])

        xs = nc.dram_tensor("xs", (PAIRS, D), F32, kind="Internal").ap()
        hxs = nc.dram_tensor("hxs", (PAIRS, R), F32, kind="Internal").ap()
        hsd = nc.dram_tensor("hsd", (SLOTS * SLOT, R), F32, kind="Internal").ap()
        ysd = nc.dram_tensor("ysd", (SLOTS * SLOT, D), F32, kind="Internal").ap()
        in_const, in_vec, in_tok, in_w1, in_w2 = (sem(f"in_{n}") for n in ("const", "vec", "tok", "w1", "w2"))
        ready = sem("ready")
        dve_chain = sem("dve_chain")
        pool_chain = sem("pool_chain")
        tok_ps, tok_xt, h0_ps, h0_sb = sem("tok_ps"), sem("tok_xt"), sem("h0_ps"), sem("h0_sb")
        qk_ps, q_sb, k_sb, kx_sb = sem("qk_ps"), sem("q_sb"), sem("k_sb"), sem("kx_sb")
        v_ps, v_sb, vrep_ps, vx_sb = sem("v_ps"), sem("v_sb"), sem("vrep_ps"), sem("vx_sb")
        score_ps, score_used, exped, prob_sb = sem("score_ps"), sem("score_used"), sem("exped"), sem("prob_sb")
        probT_ps, probT_sb, ctx_ps, ctx_sb = sem("probT_ps"), sem("probT_sb"), sem("ctx_ps"), sem("ctx_sb")
        sum_rdy, inv_rdy = sem("sum_rdy"), sem("inv_rdy")
        att_ps = sem("att_ps")
        var_rdy, rstd_rdy = sem("var_rdy"), sem("rstd_rdy")
        ln_out = sem("ln_out")
        stored = sem("stored")
        in_ffn = sem("in_ffn")
        pads_rdy = sem("pads_rdy")
        turn_ps, xt_rdy = sem("turn_ps"), sem("xt_rdy")
        z_ps, z_sb, e_sb = sem("z_ps"), sem("z_sb"), sem("e_sb")
        sig_rdy, weighed_rdy, pooled_rdy, mixT_rdy = sem("sig_rdy"), sem("weighed_rdy"), sem("pooled_rdy"), sem("mixT_rdy")
        mix_ps, merged = sem("mix_ps"), sem("merged")
        in_diff, buf_rdy = sem("in_diff"), sem("buf_rdy")
        enc1_ps, enc1_sb, enc2_ps, norm_rdy, inorm_rdy = (sem(f"enc_{n}") for n in ("a", "b", "c", "d", "e"))
        code_rdy, refsum_ps, alike_rdy, tanh_rdy = sem("code_rdy"), sem("refsum_ps"), sem("alike_rdy"), sem("tanh_rdy")
        gated = sem("gated")
        k_ref_ps, k_ref_sb, gram_ps, gram_sb = sem("k_ref_ps"), sem("k_ref_sb"), sem("gram_ps"), sem("gram_sb")
        xd_ps, xd_sb, qv_ps, qd_ps, qtok_sb, qd_sb, vmask_sb = (sem(f"diff_{n}") for n in "abcdefg")
        qtok_ps = sem("qtok_ps")
        m_ps, m_sb, gm_ps, gm_sb, o_ps, o_sb_act, o_sb_dve, proj_ps = (sem(f"diff_{n}") for n in "hijklmno")
        in_emb, emb2_rdy, emb_root, emb_rdy, embT_ps, emb_sb = (sem(f"emb_{n}") for n in "abcdef")
        bf_rdy, moe_buf = sem("bf_rdy"), sem("moe_buf")
        key_ps, key_sb, logit_ps, logit_sb, chosen_rdy, count_ps, count_rdy, first_ps = (sem(f"route_{n}") for n in "abcdefgh")
        shift_rdy, expo_rdy, in_rdy, out_rdy, table_in, table_ps, table_rdy, weight_rdy = (
            sem(f"route_{n}") for n in "ijklmnop")
        base_ps, base_sb, delta_rdy, rank_ps, ranks_used = (
            sem(f"{n}") for n in ("base_ps", "base_sb", "delta_rdy", "rank_ps", "ranks_used"))
        rows_in = [sem(f"rows_in{j}") for j in range(4)]
        scattered, turned_ps, turned_sb, gathered = (sem(f"pairs_{n}") for n in "abcd")
        ring_in = [sem(f"ring_in{j}") for j in range(RING)]
        extra_in = [sem(f"extra_in{j}") for j in range(3)]
        stored_rows = [sem(f"stored_rows{j}") for j in range(4)]
        staged_rdy, product, taken = sem("staged_rdy"), sem("product"), sem("taken")
        ALL = QUADS + FURTHER
        STORES = [QUADS // 4 + (FURTHER // 3 if j < 3 else 0) for j in range(4)]
        combined = sem("combined")
        hid_ps, hid_sb, ffn_ps, hs_rdy = sem("hid_ps"), sem("hid_sb"), sem("ffn_ps"), sem("hs_rdy")
        block = ctx.enter_context(nc.Block())

        def folded(i, j):
            to = od[32 * (j % 4):32 * (j % 4) + DH, j // 4, TT * i:TT * (i + 1)].rearrange("p (b n) -> p b n", b=3)
            return to, ps[0:DH, 3 * i:3 * i + 3, j:HEADS * NT:HEADS]

        PAIRS_OF_IMAGES = NB // 2

        @block.sync
        def _(sp):
            sp.dma_start(token_w[:], dram["token_w"]).then_inc(in_tok, 16)
            sp.dma_start(patches[:], dram["patches"]).then_inc(in_tok, 16)
            sp.dma_start(cst[:], dram["constants"]).then_inc(in_const, 16)
            sp.dma_start(vec[:], dram["vectors"]).then_inc(in_vec, 16)
            sp.dma_start(attn_w[0][:], dram["attn1_w"]).then_inc(in_w1, 16)
            sp.dma_start(attn_wo[0][:], dram["attn1_wo"]).then_inc(in_w1, 16)
            sp.dma_start(attn_w[1][:], dram["attn2_w"]).then_inc(in_w2, 16)
            sp.dma_start(attn_wo[1][:], dram["attn2_wo"]).then_inc(in_w2, 16)
            sp.dma_start(emb[:], dram["emb"]).then_inc(in_emb, 16)
            for t, n in ((w1, "ffn_w1"), (b1, "ffn_b1"), (w2, "ffn_w2"), (b2, "ffn_b2")):
                sp.dma_start(t[:], dram[n]).then_inc(in_ffn, 16)
            for t, n in ((diff_w, "diff_w"), (proj_w, "proj_w"), (diff_ln, "diff_ln"), (enc_w2, "enc_w2")):
                sp.dma_start(t[:], dram[n]).then_inc(in_diff, 16)
            def weights_in(st, to, at):
                n = (HALF, P)[st]
                w, width = dram[("feature_w", "restore_w")[st]], (2 * R, D)[st]
                return sp.dma_start(to[0:n, 0:QUAD * width].rearrange("p (c f) -> p c f", c=QUAD), w[:, bass.ds(at, QUAD), :])

            def prefetch(st):
                for j in range(RING):
                    if st == 1:
                        sp.wait_ge(product, QUADS - RING + 1 + j)
                    weights_in(st, ring[:, j], QUAD * j).then_inc(ring_in[j], 16)

            sp.wait_ge(ffn_ps, 3)
            prefetch(0)

            def tiles_of(d, a, b):
                return d[P * a:P * b, :].rearrange("(t p) f -> p t f", p=P)

            def pairs_in(st, d, width):
                sp.wait_ge(scattered, 16 * TOPK * TILES * (st + 1))
                for j in range(3):
                    sp.dma_start(rows[:, 6 * j:6 * j + 6, 0:width], tiles_of(d, 6 * j, 6 * j + 6)).then_inc(rows_in[j], 16)
                sp.dma_start(rows[0:PLAST, PTILES - 1, 0:width], d[P * (PTILES - 1):PAIRS, :]).then_inc(rows_in[3], 16)

            regs = [sp.alloc_register(f"sp_neuron{j}") for j in range(QUAD)]

            def neurons(st):
                with sp.Fori(1, QUADS // RING) as i:
                    for j in range(RING):
                        sp.wait_ge(product, RING * i + (j - RING + 1 + ALL * st))
                        weights_in(st, ring[:, j], QUAD * RING * i + QUAD * j).then_inc(ring_in[j], 16)
                sp.wait_ge(table_rdy, 1)
                n, width = (HALF, P)[st], (2 * R, D)[st]
                w = dram[("feature_w", "restore_w")[st]]

                def further(i, wait):
                    for j in range(3):
                        sp.load(regs, table[0:1, st, bass.ds(NN + EXTRA + 3 * QUAD * i + QUAD * j, QUAD)])
                        if wait:
                            sp.wait_ge(product, 3 * i + (j + QUADS - 2 + ALL * st))
                        for c in range(QUAD):
                            neuron = sp.snap(regs[c], min_val=0, max_val=NN - 1)
                            sp.dma_start(extra[0:n, j, width * c:width * (c + 1)],
                                         w[:, bass.ds(neuron, 1), :].rearrange("p o f -> p (o f)")).then_inc(extra_in[j], 16)

                further(0, False)
                with sp.Fori(1, FURTHER // 3) as i:
                    further(i, True)

            pairs_in(0, xs, D)
            neurons(0)
            prefetch(1)
            pairs_in(1, hxs, R)
            sp.wait_ge(product, ALL)
            neurons(1)
            flat = out.rearrange("b n d -> (b n) d")
            for i in range(TILES):
                n = TT if i < TILES - 1 else LAST
                sp.wait_ge(ln_out, 4 * TILES + 6 + TILES + i + 1)
                sp.dma_start(flat[TT * i:TT * i + n, :], hs[0:n, i, :]).then_inc(stored, 16)
            sp.wait_ge(stored, 16 * TILES)

        @block.gpsimd
        def _(pool):
            steps = [0]

            def link(ins):
                steps[0] += 1
                ins.then_inc(pool_chain, 1)
                pool.wait_ge(pool_chain, steps[0])

            for x in xt[0:3]:
                nc.gpsimd.memset(x[:, :, T:PAD], 0.0)
            nc.gpsimd.memset(qt[:, :, T:], 0.0)
            nc.gpsimd.memset(vx[:], 0.0)
            nc.gpsimd.memset(ctxT[:], 1.0)
            nc.gpsimd.memset(zb[:, T:PAD], 0.0)
            nc.gpsimd.memset(mixT[:, :, T:PAD], 0.0)
            nc.gpsimd.memset(ones[:], 1.0)
            nc.gpsimd.memset(half_p[:], 0.5)
            link(nc.gpsimd.memset(power[:], -0.5))
            for x in (*xt[0:3], mixT):
                ins = nc.gpsimd.memset(x[HALF:HALF + 1, :, :], 1.0)
            ins.then_inc(ready, 1)

            def softmax_products(a):
                for p in range(PAIRS_OF_IMAGES):
                    n = a * PAIRS_OF_IMAGES + p
                    pool.wait_ge(inv_rdy, n + 1)
                    if n >= 2:
                        pool.wait_ge(probT_ps, n - 1)
                    e = shifted[:, n % 2, :].rearrange("p (h k) -> p h k", h=HEADS)
                    nc.gpsimd.tensor_tensor(
                        probs[:, n % 2, :].rearrange("p (h k) -> p h k", h=HEADS), e,
                        sinv[:, n % 2, :].unsqueeze(2).to_broadcast([P, HEADS, NT]), ALU.mult).then_inc(prob_sb, 1)

            def root(n, tiles=TILES):
                pool.wait_ge(var_rdy, n + 1)
                nc.gpsimd.tensor_tensor(rstd[:, 0:tiles], rstd[:, 0:tiles], power[:, 0:tiles],
                                        ALU.pow).then_inc(rstd_rdy, 1)

            pool.wait_ge(in_const, 16)
            pool.wait_ge(ready, 1)
            link(nc.gpsimd.tensor_copy(ones_bf[:], ones[:, 0:TT]))
            nc.gpsimd.tensor_copy(upto_bf[:], const("upto", TT)).then_inc(bf_rdy, 1)
            pool.wait_ge(emb2_rdy, 1)
            pool.wait_ge(bf_rdy, 1)
            nc.gpsimd.tensor_tensor(emb_n[:], emb_n[:], half_p[:], ALU.pow).then_inc(emb_root, 1)
            softmax_products(0)
            root(0)
            root(1)
            nc.gpsimd.memset(hid[:, :, T:PAD], 0.0).then_inc(pads_rdy, 1)
            pool.wait_ge(sig_rdy, 1)
            pool.wait_ge(xt_rdy, 3)
            nc.gpsimd.tensor_tensor(weighed[:], xt[1][0:HALF, :, 0:T], sig[:].unsqueeze(1).to_broadcast([HALF, 2, T]),
                                    ALU.mult).then_inc(weighed_rdy, 1)
            softmax_products(1)
            pool.wait_ge(pooled_rdy, 1)
            for m in range(2):
                ins = nc.gpsimd.tensor_tensor(
                    weighed[:, m, :].rearrange("p (b t) -> p b t", b=NB), sig[:].rearrange("p (b t) -> p b t", b=NB),
                    pooled[:, m, :].unsqueeze(2).to_broadcast([HALF, NB, NT]), ALU.mult)
            link(ins)
            nc.gpsimd.tensor_tensor(mixT[0:HALF, :, 0:T], weighed[:], xt[1][0:HALF, :, 0:T],
                                    ALU.add).then_inc(mixT_rdy, 1)
            root(2)
            pool.wait_ge(merged, TILES)
            nc.gpsimd.tensor_tensor(hs[:], h1[:], hp[:], ALU.add).then_inc(hs_rdy, 1)
            pool.wait_ge(hs_rdy, 1)
            pool.wait_ge(ffn_ps, 1)
            link(nc.gpsimd.memset(enc1[:], 1.0))
            link(nc.gpsimd.memset(xd[HALF:HALF + 1, :, :], 1.0))
            ins = nc.gpsimd.memset(od[:], 1.0)
            ins.then_inc(buf_rdy, 1)
            pool.wait_ge(buf_rdy, 1)
            root(3)
            pool.wait_ge(norm_rdy, 1)
            nc.gpsimd.tensor_tensor(norm2[:], norm2[:], power[:], ALU.pow).then_inc(inorm_rdy, 1)
            for s in range(3):
                root(4 + s, 2)
            pool.wait_ge(xd_sb, 3)
            nc.gpsimd.memset(emb_block[:], 0.0)
            link(nc.gpsimd.memset(keyT[:, T:PAD], 0.0))
            nc.gpsimd.memset(logit[:, :, NN:NN + 4], SENTINEL).then_inc(moe_buf, 1)
            root(7)
            rows_of = [TT if i < TILES - 1 else LAST for i in range(TILES)]

            def scatter(st, src, d):
                pool.wait_ge(in_rdy, st + 1)
                for i, n in enumerate(rows_of):
                    if st == 1:
                        pool.wait_ge(combined, i + 1)
                    for k in range(TOPK):
                        nc.gpsimd.indirect_dma_start(
                            out=d[:, :], out_offset=bass.IndirectOffsetOnAxis(ap=row_in[0:n, 2 * i + st, k:k + 1], axis=0),
                            in_=src[0:n, i, :], in_offset=None).then_inc(scattered, 16)

            def gather(st, dst, d):
                pool.wait_ge(out_rdy, 1)
                for j in range(4):
                    pool.wait_ge(stored_rows[j], 16 * STORES[j] * (st + 1))
                for i, n in enumerate(rows_of):
                    for k in range(TOPK):
                        nc.gpsimd.indirect_dma_start(
                            out=dst[0:n, i, k, :], out_offset=None, in_=d[:, :],
                            in_offset=bass.IndirectOffsetOnAxis(ap=row_out[0:n, 2 * i + st, k:k + 1], axis=0)).then_inc(gathered, 16)

            link(nc.gpsimd.memset(xg[:, :, PAIRS:PCOLS], 0.0))
            nc.gpsimd.memset(hg[:, PAIRS:PCOLS], 0.0).then_inc(moe_buf, 1)
            pool.wait_ge(ln_out, 4 * TILES + 6 + TILES)
            scatter(0, h1, xs)
            gather(0, got_h, hsd)
            scatter(1, mixed_h, hxs)
            gather(1, got_y, ysd)
            root(8)

        @block.tensor
        def _(pe):
            def mm(dst, lhs, rhs, start=True, stop=True):
                return nc.tensor.matmul(dst, lhs, rhs, start=start, stop=stop)

            def projected(dst, w, x):
                mm(dst, w[0:HALF + 1, 0], x[0:HALF + 1, 0], stop=False)
                return mm(dst, w[0:HALF, 1], x[0:HALF, 1], start=False)

            def tokens():
                pe.wait_ge(in_tok, 32)
                for m in range(2):
                    for c in range(2):
                        for k in range(6):
                            ins = mm(ps[0:HALF, 2 * m + c, 0:8 * (NT - 1)], token_w[:, k, HALF * m:HALF * (m + 1)],
                                     patches[:, k, 8 * (NT - 1) * c:8 * (NT - 1) * (c + 1)], k == 0, k == 5)
                        ins.then_inc(tok_ps, 1)

            def turn_h0():
                pe.wait_ge(tok_xt, 5)
                pe.wait_ge(in_const, 16)
                for i in range(TILES):
                    for m in range(2):
                        ins = nc.tensor.transpose(
                            ps[0:TT, 4 + i // 2, D * (i % 2) + HALF * m:D * (i % 2) + HALF * (m + 1)],
                            xt[0][0:HALF, m, TT * i:TT * (i + 1)], ident[0:HALF, 0:HALF])
                    if i % 2:
                        ins.then_inc(h0_ps, 1)

            def turn_to_features(n, src, bank, need):
                for i in range(TILES):
                    pe.wait_ge(ln_out, need + i + 1)
                    for m in range(2):
                        at = TT * (2 * m + i % 2)
                        ins = nc.tensor.transpose(ps[0:HALF, bank + i // 2, at:at + TT],
                                                  src[:, i, HALF * m:HALF * (m + 1)], ident[0:TT, 0:TT])
                    if i % 2:
                        ins.then_inc(turn_ps, 1)

            def routing_logits(c):
                if c == 0:
                    pe.wait_ge(q_sb, 8)
                else:
                    pe.wait_ge(e_sb, 1)
                projected(ps[0:TT, 3, 0:CH], attn_w[1][:, :, RW:RW + TT],
                          xt[1][:, :, CH * c:CH * (c + 1)]).then_inc(z_ps, 1)

            def mix():
                for i in range(TILES):
                    if i == 0:
                        pe.wait_ge(mixT_rdy, 1)
                    ins = projected(ps[0:TT, 3 + i // 2, D * (i % 2):D * (i % 2 + 1)], mixT[:, :, TT * i:TT * (i + 1)],
                                    attn_w[1][:, :, MIXW:MIXW + D])
                    if i % 2:
                        ins.then_inc(mix_ps, 1)

            def feed_forward():
                pe.wait_ge(in_ffn, 64)
                pe.wait_ge(xt_rdy, 6)
                for k in range(6):
                    for c in range(2):
                        q = 2 * k + c
                        if q >= 4:
                            pe.wait_ge(hid_sb, q - 3)
                        bank = 3 + q % 4
                        mm(ps[:, bank, 0:CH], w1[:, 0, P * k:P * (k + 1)], xt[2][0:HALF, 0, CH * c:CH * (c + 1)],
                           stop=False)
                        mm(ps[:, bank, 0:CH], w1[:, 1, P * k:P * (k + 1)], xt[2][0:HALF, 1, CH * c:CH * (c + 1)],
                           start=False).then_inc(hid_ps, 1)
                pe.wait_ge(hid_sb, 12)
                pe.wait_ge(pads_rdy, 1)
                for i in range(TILES):
                    dst = ps[0:TT, i // 2, D * (i % 2):D * (i % 2 + 1)]
                    mm(dst, ones[0:1, 0:TT], b2[:], stop=False)
                    for k in range(6):
                        ins = mm(dst, hid[:, k, TT * i:TT * (i + 1)], w2[:, k, :], False, k == 5)
                    if i % 2:
                        ins.then_inc(ffn_ps, 1)

            def attention(a):
                w, x = attn_w[a], xt[a]
                pe.wait_ge((in_w1, in_w2)[a], 32)
                for which in range(2):
                    if which == 1 and a == 0:
                        pe.wait_ge(h0_sb, 3)
                        pe.wait_ge(emb_sb, 1)
                    for m in range(2):
                        for c in range(2):
                            at = D * which + HALF * m
                            projected(ps[0:HALF, 4 * which + 2 * m + c, 0:CH], w[:, :, at:at + HALF],
                                      x[:, :, CH * c:CH * (c + 1)]).then_inc(qk_ps, 1)
                for i in range(TILES):
                    if i % 2 == 0:
                        pe.wait_ge(q_sb, 4 * a + i // 2 + 1)
                    ins = projected(ps[0:TT, i // 2, D * (i % 2):D * (i % 2 + 1)], x[:, :, TT * i:TT * (i + 1)],
                                    w[:, :, 2 * D:3 * D])
                    if i % 2:
                        ins.then_inc(v_ps, 1)
                if a == 1:
                    routing_logits(0)
                for b in range(NB):
                    if b % 2 == 0:
                        j = b // 2
                        pe.wait_ge(k_sb, 4 * a + min(j, 3) + 1)
                        pe.wait_ge(v_sb, 3 * a + (b + 1) // 3 // 2 + 1)
                        if j >= 4:
                            pe.wait_ge(vx_sb, 8 * a + j - 3)
                    s = TT * (b % 3)
                    ins = mm(ps[0:TT, 4 + b // 2 % 4, D * (b % 2):D * (b % 2 + 1)],
                             const("spread", TT)[:, s:s + TT], vtok[:, b // 3, :])
                    if b % 2:
                        ins.then_inc(vrep_ps, 1)

                if a == 1:
                    routing_logits(1)

                def scores(p):
                    n = PAIRS_OF_IMAGES * a + p
                    if p == 0:
                        pe.wait_ge(q_sb, 4 * a + 4)
                        pe.wait_ge(kx_sb, a + 1)
                        pe.wait_ge(v_sb, 3 * a + 3)
                    if p >= 2:
                        pe.wait_ge(score_used, n - 1)
                    for y in range(2):
                        b = 2 * p + y
                        for m in range(2):
                            ins = mm(ps[64 * y:64 * y + 64, p % 2, 222 * m:222 * (m + 1)], qt[:, m, NT * b:NT * b + 64],
                                     kx[:, m, :, NT * b:NT * (b + 1)])
                    ins.then_inc(score_ps, 1)

                def turn(p):
                    n = PAIRS_OF_IMAGES * a + p
                    pe.wait_ge(prob_sb, n + 1)
                    if n >= 2:
                        pe.wait_ge(probT_sb, n - 1)
                    if a == 1 and p == 0:
                        pe.wait_ge(e_sb, 2)
                    for g in range(GROUPS):
                        ins = nc.tensor.transpose(ps[0:TT, 2 + p % 2, P * g:P * (g + 1)],
                                                  probs[:, n % 2, TT * g:TT * (g + 1)], ident)
                    ins.then_inc(probT_ps, 1)

                def contexts(p):
                    n = PAIRS_OF_IMAGES * a + p
                    pe.wait_ge(probT_sb, n + 1)
                    if p == 0:
                        pe.wait_ge(vx_sb, 8 * a + 8)
                    for y in range(2):
                        b = 2 * p + y
                        for g in range(GROUPS):
                            ins = mm(ps[64 * (g % 2):64 * (g % 2) + 64, 4 + 2 * (g // 2) + b // 8,
                                        NT * (b % 8):NT * (b % 8 + 1)],
                                     vx[:, b, g, :], probsT[:, n % 2, P * g + 64 * y:P * g + 64 * y + NT])
                    ins.then_inc(ctx_ps, 1)

                for s in range(PAIRS_OF_IMAGES + 2):
                    if s < PAIRS_OF_IMAGES:
                        scores(s)
                    if 1 <= s <= PAIRS_OF_IMAGES:
                        turn(s - 1)
                    if s >= 2:
                        contexts(s - 2)
                for i in range(TILES):
                    if i == 0:
                        pe.wait_ge(score_used, PAIRS_OF_IMAGES * (a + 1))
                        pe.wait_ge(probT_sb, PAIRS_OF_IMAGES * (a + 1))
                        pe.wait_ge(ctx_sb, 4 * a + 4)
                    dst = ps[0:TT, i // 2, D * (i % 2):D * (i % 2 + 1)]
                    mm(dst, ctxT[:, 0, TT * i:TT * (i + 1)], attn_wo[a][:, 0, :], stop=False)
                    ins = mm(dst, ctxT[:, 1, TT * i:TT * (i + 1)], attn_wo[a][:, 1, :], start=False)
                    if i % 2:
                        ins.then_inc(att_ps, 1)

            def encoder():
                pe.wait_ge(in_diff, 64)
                x = xt[3]
                for c in range(2):
                    projected(ps[0:ENC1, c, 0:CH], diff_w[:, :, FC1:FC1 + ENC1], x[:, :, CH * c:CH * (c + 1)]).then_inc(enc1_ps, 1)
                pe.wait_ge(enc1_sb, 2)
                for i in range(TILES):
                    ins = mm(ps[0:TT, 2, ENC2 * i:ENC2 * (i + 1)], enc1[:, TT * i:TT * (i + 1)], enc_w2[:])
                ins.then_inc(enc2_ps, 1)
                for i in range(2, TILES):
                    ins = projected(ps[0:TT, i // 2 - 1, D * (i % 2):D * (i % 2 + 1)], x[:, :, TT * i:TT * (i + 1)],
                                    diff_w[:, :, KW:KW + D])
                    if i % 2:
                        ins.then_inc(k_ref_ps, 1)
                pe.wait_ge(code_rdy, 1)
                for i in range(2, TILES):
                    n = TT if i < TILES - 1 else LAST
                    ins = mm(ps[0:TT, 7, 0:ENC2], const("sametoken", n), code2[0:n, i, :], i == 2, i == TILES - 1)
                ins.then_inc(refsum_ps, 1)
                pe.wait_ge(k_ref_sb, 2)
                for h in range(2):
                    for i in range(4):
                        n = TT if i < 3 else LAST
                        k = ksb[0:n, i, HALF * h:HALF * (h + 1)]
                        ins = mm(ps[0:HALF, 3, HALF * h:HALF * (h + 1)], k, k, i == 0, i == 3)
                ins.then_inc(gram_ps, 1)

            def diffuser_step(s):
                for i in range(2):
                    if s == 0:
                        pe.wait_ge(gated, 1)
                    else:
                        pe.wait_ge(ln_out, 4 * TILES + 2 * (s - 1) + i + 1)
                    for m in range(2):
                        ins = nc.tensor.transpose(ps[0:HALF, 4, XT_ * m + TT * i:XT_ * m + TT * (i + 1)],
                                                  n1[:, i, HALF * m:HALF * (m + 1)], ident[0:TT, 0:TT])
                ins.then_inc(xd_ps, 1)
                pe.wait_ge(xd_sb, s + 1)
                for i in range(2):
                    projected(ps[0:TT, i, 0:D], xd[:, :, TT * i:TT * (i + 1)],
                              diff_w[:, :, QV:QV + D]).then_inc(qtok_ps, 1)
                if s == 0:
                    pe.wait_ge(alike_rdy, 1)
                    pe.wait_ge(gram_sb, 1)
                for i in range(2):
                    projected(ps[0:TT, (3, 7)[i], 0:D], xd[:, :, TT * i:TT * (i + 1)],
                              diff_w[:, :, QV + D:QV + 2 * D]).then_inc(qv_ps, 1)
                for m in range(2):
                    ins = projected(ps[0:HALF, 2, XT_ * m:XT_ * (m + 1)],
                                    diff_w[:, :, QV + HALF * m:QV + HALF * (m + 1)], xd[:])
                ins.then_inc(qd_ps, 1)
                pe.wait_ge(qtok_sb, 2 * s + 2)
                for i in range(2):
                    pe.wait_ge(vmask_sb, 2 * s + i + 1)
                    for h in range(2):
                        ins = mm(ps[0:HALF, 4 + 2 * h + i, 0:3 * HALF], qtok[:, i, HALF * h:HALF * (h + 1)],
                                 vmask[:, i, :, HALF * h:HALF * (h + 1)])
                    ins.then_inc(m_ps, 1)
                for h in range(2):
                    for i in range(2):
                        pe.wait_ge(m_sb, 4 * s + 4)
                        mm(ps[0:HALF, (0, 1, 3, 4)[2 * h + i], 0:3 * HALF], gram[:, h, :],
                           mblock[:, h, 3 * i:3 * i + 3, :]).then_inc(gm_ps, 1)
                pe.wait_ge(qd_sb, s + 1)
                pe.wait_ge(gm_sb, 4 * s + 4)
                for b in range(XM):
                    for h in range(HEADS):
                        ins = mm(ps[0:DH, b, NT * h:NT * (h + 1)], gmask[:, h // 6, b, DH * (h % 6):DH * (h % 6 + 1)],
                                 qd[:, h // 6, NT * b:NT * (b + 1)])
                    if b % 3 == 2:
                        ins.then_inc(o_ps, 1)
                for i in range(2):
                    pe.wait_ge((o_sb_act, o_sb_dve)[i], s + 1)
                    for k in range(3):
                        ins = mm(ps[0:TT, 6, D * i:D * (i + 1)], od[:, k, TT * i:TT * (i + 1)], proj_w[:, k, :], k == 0, k == 2)
                ins.then_inc(proj_ps, 1)

            def route():
                pe.wait_ge(xt_rdy, 12)
                pe.wait_ge(moe_buf, 1)
                for c in range(2):
                    projected(ps[:, c, 0:CH], diff_w[:, :, ROUTE:ROUTE + P], xt[4][:, :, CH * c:CH * (c + 1)]).then_inc(key_ps, 1)
                pe.wait_ge(key_sb, 2)
                pe.wait_ge(emb_sb, 2)
                for i in range(TILES):
                    ins = mm(ps[0:TT, 2 + i // 2, 2 * NN * (i % 2):2 * NN * (i % 2 + 1)], keyT[:, TT * i:TT * (i + 1)], emb_block[:])
                    if i % 2:
                        ins.then_inc(logit_ps, 1)
                rows_of = [TT if i < TILES - 1 else LAST for i in range(TILES)]
                pe.wait_ge(chosen_rdy, 1)
                for r in range(2):
                    for i, n in enumerate(rows_of):
                        ins = mm(ps[:, 5, r:r + 1], chosen[0:n, 2 * i + r, :], ones_bf[0:n, 0:1], i == 0, i == TILES - 1)
                ins.then_inc(count_ps, 1)
                for i, n in enumerate(rows_of):
                    dst = ps[0:TT, 2 + i // 2, 2 * NN * (i % 2):2 * NN * (i % 2 + 1)]
                    for e in range(i):
                        mm(dst, ones_bf[0:TT, :], chosen[:, 2 * e:2 * e + 2, :], e == 0, False)
                    ins = mm(dst, upto_bf[0:n, :], chosen[0:n, 2 * i:2 * i + 2, :], i == 0)
                    if i % 2:
                        ins.then_inc(rank_ps, 1)
                pe.wait_ge(count_rdy, 1)
                for r in range(2):
                    ins = mm(ps[0:TT, 0, NN * r:NN * (r + 1)], count_wide[:, r, :], const("before"))
                ins.then_inc(base_ps, 1)
                mm(ps[:, 6, 0:4], const("before"), counts[:])
                for r in range(2):
                    ins = mm(ps[0:1, 7, NN * r:NN * (r + 1)], counts[:, r:r + 1], const("before"))
                ins.then_inc(first_ps, 1)
                pe.wait_ge(delta_rdy, 1)
                for r in range(2):
                    ins = mm(ps[0:TT, 1, NN * r:NN * (r + 1)], delta_wide[:, r, :], ident)
                ins.then_inc(base_ps, 1)
                pe.wait_ge(table_in, 1)
                mm(ps[0:1, 7, 2 * NN:2 * NN + 4 * EXTRA], ones[:, 0:1], table_f[:]).then_inc(table_ps, 1)

            def turn_pairs(st):
                if st == 0:
                    pe.wait_ge(base_sb, 2)
                    pe.wait_ge(ranks_used, 1)
                for t in range(PTILES):
                    n = P if t < PTILES - 1 else PLAST
                    per, bank = (2, t // 2) if st == 0 else (4, t // 4)
                    if t % 6 == 0:
                        pe.wait_ge(rows_in[t // 6], 16 * st + 16)
                    if t % per == 0 and bank >= 4:
                        pe.wait_ge(turned_sb, (0, 10)[st] + bank - 3)
                    for m in range(2 - st):
                        at = 2 * P * (t % 2) + P * m if st == 0 else P * (t % 4)
                        w = HALF if st == 0 else R
                        ins = nc.tensor.transpose(ps[0:w, bank % 4, at:at + n], rows[0:n, t, w * m:w * (m + 1)], ident[0:n, 0:n])
                    if t % per == per - 1 or t == PTILES - 1:
                        ins.then_inc(turned_ps, 1)

            def neurons(st):
                pe.wait_ge(turned_sb, (10, 15)[st])
                width = (2 * R, D)[st]

                def quad(w, bank, buf):
                    for c in range(QUAD):
                        dst = ps[64 * (c % 2):64 * (c % 2) + SLOT, bank, (R, D)[st] * (c // 2):(R, D)[st] * (c // 2 + 1)]
                        x = staged[:, QUAD * buf + c, :]
                        if st == 0:
                            mm(dst, x[0:HALF, 0:SLOT], w[0:HALF, width * c:width * c + R], stop=False)
                            ins = mm(dst, x[0:HALF, SLOT:2 * SLOT], w[0:HALF, width * c + R:width * (c + 1)], start=False)
                        else:
                            ins = mm(dst, x[:, 0:SLOT], w[:, width * c:width * (c + 1)])
                    ins.then_inc(product, 1)

                def ring_quads(i, first):
                    for j in range(RING):
                        pe.wait_ge(staged_rdy, RING * i + (j + 1 + ALL * st))
                        pe.wait_ge(ring_in[j], 16 * i + (16 + 16 * QUADS // RING * st))
                        if not first:
                            pe.wait_ge(taken, RING * i + (j - RING + 1 + ALL * st))
                        quad(ring[:, j], j, j % 4)

                ring_quads(0, True)
                with pe.Fori(1, QUADS // RING) as i:
                    ring_quads(i, False)
                with pe.Fori(0, FURTHER // 3) as i:
                    for j in range(3):
                        pe.wait_ge(staged_rdy, 3 * i + (j + QUADS + 1 + ALL * st))
                        pe.wait_ge(extra_in[j], 16 * QUAD * i + 16 * QUAD * (1 + FURTHER // 3 * st))
                        pe.wait_ge(taken, 3 * i + (j + QUADS - 2 + ALL * st))
                        quad(extra[:, j], j, j)

            tokens()
            pe.wait_ge(in_const, 16)
            pe.wait_ge(emb_rdy, 1)
            nc.tensor.transpose(ps[:, 7, 0:P], emb2[:].rearrange("p r e -> p (r e)"), ident).then_inc(embT_ps, 1)
            turn_h0()
            pe.wait_ge(ready, 1)
            attention(0)
            turn_to_features(0, n1, 4, TILES)
            pe.wait_ge(xt_rdy, 3)
            attention(1)
            mix()
            turn_to_features(1, n1, 0, 2 * TILES)
            feed_forward()
            turn_to_features(2, h2, 4, 3 * TILES)
            pe.wait_ge(xt_rdy, 9)
            encoder()
            for s in range(3):
                diffuser_step(s)
            turn_to_features(3, h1, 0, 4 * TILES + 6)
            route()
            turn_pairs(0)
            neurons(0)
            pe.wait_ge(taken, ALL)
            turn_pairs(1)
            neurons(1)

        @block.scalar
        def _(act):
            def attention(a):
                for j in range(4):
                    act.wait_ge(qk_ps, 8 * a + j + 1)
                    m, c = j // 2, j % 2
                    nc.scalar.mul(qt[:, m, CH * c:CH * (c + 1)], ps[0:HALF, j, 0:CH], DH ** -0.5).then_inc(q_sb, 1)
                for j in range(3):
                    act.wait_ge(v_ps, 3 * a + j + 1)
                    nc.scalar.copy(vtok[:, 2 * j:2 * j + 2, :],
                                   ps[0:TT, j, 0:2 * D].rearrange("p (i d) -> p i d", i=2)).then_inc(v_sb, 1)
                if a == 1:
                    routing_logits(0)
                    routing_logits(1)
                for s in range(PAIRS_OF_IMAGES + 1):
                    if s < PAIRS_OF_IMAGES:
                        n = PAIRS_OF_IMAGES * a + s
                        act.wait_ge(score_used, n + 1)
                        nc.scalar.activation(shifted[:, n % 2, :], shifted[:, n % 2, :], ACT.Exp).then_inc(exped, 1)
                    if s >= 1:
                        n = PAIRS_OF_IMAGES * a + s - 1
                        act.wait_ge(probT_ps, n + 1)
                        if n >= 2:
                            act.wait_ge(ctx_ps, n - 1)
                        nc.scalar.copy(probsT[:, n % 2, :], ps[0:TT, 2 + n % 2, :]).then_inc(probT_sb, 1)
                for c in range(2):
                    act.wait_ge(ctx_ps, PAIRS_OF_IMAGES * a + 4 * (c + 1))
                    for m in range(2):
                        for g in range(2):
                            ins = nc.scalar.copy(ctxT[64 * g:64 * g + GF, m, CH * c:CH * (c + 1)],
                                                 ps[64 * g:64 * g + GF, 4 + 2 * m + c, 0:CH])
                        ins.then_inc(ctx_sb, 1)

            def to_features(n, dst, bank, gain=None, bias=None):
                for j in range(3):
                    act.wait_ge(turn_ps, 3 * n + j + 1)
                    src = ps[0:HALF, bank + j, 0:4 * TT].rearrange("p (m t) -> p m t", m=2)
                    to = dst[0:HALF, :, 2 * TT * j:2 * TT * (j + 1)]
                    if gain is None:
                        ins = nc.scalar.copy(to, src)
                    else:
                        for m in range(2):
                            ins = nc.scalar.activation(to[:, m], src[:, m], ACT.Identity,
                                                       scale=vec[:, gain + m:gain + m + 1],
                                                       bias=vec[:, bias + m:bias + m + 1])
                    ins.then_inc(xt_rdy, 1)

            def routing_logits(c):
                act.wait_ge(z_ps, c + 1)
                nc.scalar.copy(zb[:, CH * c:CH * (c + 1)], ps[0:TT, 3, 0:CH]).then_inc(z_sb, 1)
                nc.scalar.activation(sig[:, CH * c:CH * (c + 1)], ps[0:HALF, 3, 0:CH], ACT.Exp,
                                     scale=-1.0).then_inc(e_sb, 1)

            for j in range(3):
                act.wait_ge(h0_ps, j + 1)
                nc.scalar.copy(h0[:, 2 * j:2 * j + 2, :],
                               ps[0:TT, 4 + j, 0:2 * D].rearrange("p (i d) -> p i d", i=2)).then_inc(h0_sb, 1)
            act.wait_ge(ready, 1)
            attention(0)
            to_features(0, xt[1], 4, G1, B1)
            attention(1)
            to_features(1, xt[2], 0, G2, B2)
            for k in range(6):
                for c in range(2):
                    act.wait_ge(hid_ps, 2 * k + c + 1)
                    nc.scalar.activation(hid[:, k, CH * c:CH * (c + 1)], ps[:, 3 + (2 * k + c) % 4, 0:CH], ACT.Gelu,
                                         bias=b1[:, k:k + 1]).then_inc(hid_sb, 1)
            to_features(2, xt[3], 4)
            act.wait_ge(in_diff, 64)
            act.wait_ge(buf_rdy, 1)
            for c in range(2):
                act.wait_ge(enc1_ps, c + 1)
                nc.scalar.activation(enc1[0:ENC1, CH * c:CH * (c + 1)], ps[0:ENC1, c, 0:CH], ACT.Gelu,
                                     bias=vec[0:ENC1, FC1B:FC1B + 1]).then_inc(enc1_sb, 1)
            for j in range(2):
                act.wait_ge(k_ref_ps, j + 1)
                nc.scalar.copy(ksb[:, 2 * j:2 * j + 2, :],
                               ps[0:TT, j, 0:2 * D].rearrange("p (i d) -> p i d", i=2)).then_inc(k_ref_sb, 1)
            act.wait_ge(alike_rdy, 1)
            nc.scalar.activation(alike[:], alike[:], ACT.Tanh, scale=25.0 / (2 * REFS)).then_inc(tanh_rdy, 1)
            for s in range(3):
                act.wait_ge(xd_ps, s + 1)
                src = ps[0:HALF, 4, 0:2 * XT_].rearrange("p (m t) -> p m t", m=2)
                if s == 0:
                    nc.scalar.copy(xd[0:HALF], src).then_inc(xd_sb, 1)
                else:
                    for m in range(2):
                        ins = nc.scalar.activation(xd[0:HALF, m], src[:, m], ACT.Identity,
                                                   scale=vec[:, LNG + m:LNG + m + 1], bias=vec[:, LNB + m:LNB + m + 1])
                    ins.then_inc(xd_sb, 1)
                for i in range(2):
                    act.wait_ge(qtok_ps, 2 * s + i + 1)
                    nc.scalar.copy(qtok[:, i, :], ps[0:TT, i, 0:D]).then_inc(qtok_sb, 1)
                act.wait_ge(qd_ps, s + 1)
                nc.scalar.copy(qd[:], ps[0:HALF, 2, 0:2 * XT_].rearrange("p (m t) -> p m t", m=2)).then_inc(qd_sb, 1)
                for j in range(4):
                    act.wait_ge(gm_ps, 4 * s + j + 1)
                    nc.scalar.copy(gmask[:, j // 2, 3 * (j % 2):3 * (j % 2) + 3, :],
                                   ps[0:HALF, (0, 1, 3, 4)[j], 0:3 * HALF].rearrange("p (b f) -> p b f", b=3)).then_inc(gm_sb, 1)
                act.wait_ge(o_ps, 2 * s + 1)
                for j in range(HEADS):
                    ins = nc.scalar.copy(*folded(0, j))
                ins.then_inc(o_sb_act, 1)
            to_features(3, xt[4], 0)
            for c in range(2):
                act.wait_ge(key_ps, c + 1)
                nc.scalar.copy(keyT[:, CH * c:CH * (c + 1)], ps[:, c, 0:CH]).then_inc(key_sb, 1)
            for j in range(3):
                act.wait_ge(logit_ps, j + 1)
                nc.scalar.copy(logit[:, 4 * j:4 * j + 4, 0:NN],
                               ps[0:TT, 2 + j, :].rearrange("p (q n) -> p q n", n=NN)).then_inc(logit_sb, 1)
            act.wait_ge(shift_rdy, 1)
            nc.scalar.activation(expo[:], expo[:], ACT.Exp).then_inc(expo_rdy, 1)
            for n in range(2):
                act.wait_ge(base_ps, n + 1)
                nc.scalar.copy(base[:, n].rearrange("p r n -> p (r n)"), ps[0:TT, n, 0:2 * NN]).then_inc(base_sb, 1)

            def turn_pairs(st):
                if st == 0:
                    act.wait_ge(moe_buf, 2)
                for n in range((10, 5)[st]):
                    act.wait_ge(turned_ps, (0, 10)[st] + n + 1)
                    if st == 0:
                        w = 2 * P if n < 9 else PLAST
                        to = xg[:, :, 2 * P * n:2 * P * n + w]
                        src = ps[0:HALF, n % 4, 0:4 * P].rearrange("p (t m c) -> p m t c", t=2, m=2)
                        if n < 9:
                            to = to.rearrange("p m (t c) -> p m t c", t=2)
                        else:
                            src = src[:, :, 0, 0:w]
                    else:
                        w = min(4 * P, PAIRS - 4 * P * n)
                        to, src = hg[:, 4 * P * n:4 * P * n + w], ps[:, n % 4, 0:w]
                    nc.scalar.copy(to, src).then_inc(turned_sb, 1)

            def neurons(st, d):
                w = (R, D)[st]

                def quad(count, bank, buf, at):
                    act.wait_ge(product, count + (1 + ALL * st))
                    nc.scalar.copy(products[:, buf, 0:2 * w], ps[:, bank, 0:2 * w]).then_inc(taken, 1)
                    act.wait_ge(taken, count + (1 + ALL * st))
                    nc.scalar.dma_start(d[bass.ds(at, QUAD * SLOT), :].rearrange("(q p) f -> p q f", p=P),
                                        products[:, buf, 0:2 * w].rearrange("p (q f) -> p q f", q=2)).then_inc(stored_rows[buf], 16)

                def ring_quads(i, first):
                    for j in range(RING):
                        if j >= 4 or not first:
                            act.wait_ge(stored_rows[j % 4], 32 * i + 16 * (j // 4 + STORES[j % 4] * st))
                        quad(RING * i + j, j, j % 4, QUAD * SLOT * RING * i + QUAD * SLOT * j)

                ring_quads(0, True)
                with act.Fori(1, QUADS // RING) as i:
                    ring_quads(i, False)
                with act.Fori(0, FURTHER // 3) as i:
                    for j in range(3):
                        act.wait_ge(stored_rows[j], 16 * i + 16 * (QUADS // 4 + STORES[j] * st))
                        quad(3 * i + (j + QUADS), j, j, QUAD * SLOT * 3 * i + QUAD * SLOT * (QUADS + j))

            turn_pairs(0)
            neurons(0, hsd)
            turn_pairs(1)
            neurons(1, ysd)

        @block.vector
        def _(dve):
            steps = [0]

            def link(ins):
                steps[0] += 1
                ins.then_inc(dve_chain, 1)
                dve.wait_ge(dve_chain, steps[0])

            def embed():
                dve.wait_ge(in_vec, 16)
                pos = vec[:, POS:POS + 2 * NT].rearrange("p (m t) -> p m t", m=2)
                for m in range(2):
                    nc.vector.tensor_scalar(posb[:, m, 1:NT], pos[:, m, 1:NT], vec[:, TOKB + m:TOKB + m + 1], None, ALU.add)
                    ins = nc.vector.tensor_scalar(posb[:, m, 0:1], pos[:, m, 0:1], vec[:, CLS + m:CLS + m + 1], None,
                                                  ALU.add)
                link(ins)
                dve.wait_ge(ready, 1)
                xv = xt[0][0:HALF, :, 0:T].rearrange("p m (b t) -> p m b t", b=NB)
                for m in range(2):
                    ins = nc.vector.tensor_copy(xv[:, m, :, 0:1], posb[:, m, 0:1].unsqueeze(1).to_broadcast([HALF, NB, 1]))
                ins.then_inc(tok_xt, 1)
                for m in range(2):
                    for c in range(2):
                        dve.wait_ge(tok_ps, 2 * m + c + 1)
                        nc.vector.tensor_tensor(
                            xv[:, m, 8 * c:8 * c + 8, 1:NT],
                            ps[0:HALF, 2 * m + c, 0:8 * (NT - 1)].rearrange("p (b t) -> p b t", b=8),
                            posb[:, m, 1:NT].unsqueeze(1).to_broadcast([HALF, 8, NT - 1]), ALU.add).then_inc(tok_xt, 1)

            def attention(a):
                for j in range(4):
                    dve.wait_ge(qk_ps, 8 * a + 5 + j)
                    m, c = j // 2, j % 2
                    nc.vector.tensor_copy(kt[:, m, CH * c:CH * (c + 1)], ps[0:HALF, 4 + j, 0:CH]).then_inc(k_sb, 1)
                dve.wait_ge(k_sb, 4 * a + 4)
                for h in range(6):
                    ins = nc.vector.tensor_scalar(kx[:, :, h, :], kt[:], const("headof", HALF)[:, h:h + 1], None, ALU.mult)
                ins.then_inc(kx_sb, 1)
                for j in range(NB // 2):
                    dve.wait_ge(vrep_ps, 8 * a + j + 1)
                    nc.vector.tensor_tensor(
                        vx[:, 2 * j:2 * j + 2, :, 0:GF].rearrange("p b g f -> p (b g) f"),
                        ps[0:TT, 4 + j % 4, 0:2 * D].rearrange("p (x f) -> p x f", f=GF),
                        const("vmask", TT).unsqueeze(1).to_broadcast([TT, 2 * GROUPS, GF]), ALU.mult).then_inc(vx_sb, 1)

                if a == 1:
                    sigmoid()

                def top(p):
                    n = PAIRS_OF_IMAGES * a + p
                    dve.wait_ge(score_ps, n + 1)
                    s = ps[:, p % 2, 0:HEADS * NT].rearrange("p (h k) -> p h k", h=HEADS)
                    if n >= 2:
                        dve.wait_ge(prob_sb, n - 1)
                    link(nc.vector.tensor_reduce(smax[:, n % 2, :], s, AX, ALU.max))
                    nc.vector.tensor_tensor(
                        shifted[:, n % 2, :].rearrange("p (h k) -> p h k", h=HEADS), s,
                        smax[:, n % 2, :].unsqueeze(2).to_broadcast([P, HEADS, NT]), ALU.subtract).then_inc(score_used, 1)

                def total(p):
                    n = PAIRS_OF_IMAGES * a + p
                    dve.wait_ge(exped, n + 1)
                    link(nc.vector.tensor_reduce(ssum[:, n % 2, :], shifted[:, n % 2, :].rearrange("p (h k) -> p h k", h=HEADS),
                                                 AX, ALU.add))
                    nc.vector.reciprocal(sinv[:, n % 2, :], ssum[:, n % 2, :]).then_inc(inv_rdy, 1)

                for s in range(PAIRS_OF_IMAGES + 1):
                    if a == 1 and s == 1:
                        pool_inputs()
                    if a == 1 and s == 3:
                        ranks()
                    if s < PAIRS_OF_IMAGES:
                        top(s)
                    if s >= 1:
                        total(s - 1)

            def sigmoid():
                dve.wait_ge(e_sb, 2)
                link(nc.vector.tensor_scalar(sig[:], sig[:], 1.0, None, ALU.add))
                nc.vector.reciprocal(sig[:], sig[:]).then_inc(sig_rdy, 1)

            def pool_inputs():
                link(nc.vector.tensor_reduce(sigsum[:], sig[:].rearrange("p (b t) -> p b t", b=NB), AX, ALU.add))
                link(nc.vector.tensor_scalar(sigsum[:], sigsum[:], 1e-6, None, ALU.add))
                nc.vector.reciprocal(sigsum[:], sigsum[:])
                dve.wait_ge(weighed_rdy, 1)
                link(nc.vector.tensor_reduce(pooled[:], weighed[:].rearrange("p m (b t) -> p m b t", b=NB), AX, ALU.add))
                nc.vector.tensor_tensor(pooled[:], pooled[:], sigsum[:].unsqueeze(1).to_broadcast([HALF, 2, NB]),
                                        ALU.mult).then_inc(pooled_rdy, 1)

            def ranks():
                for i in range(TILES):
                    ins = nc.vector.tensor_tensor_reduce(scratch[:, i, 0:TT], zb[:, TT * i:TT * (i + 1)], ident[0:TT, 0:TT], 1.0,
                                                   0.0, ALU.mult, ALU.add, zcol[:, i:i + 1])
                link(ins)
                for i in range(TILES):
                    if i == 4:
                        link(ins)
                    for n, (op, mask) in enumerate(((ALU.is_lt, "same"), (ALU.is_equal, "earlier"))):
                        ins = nc.vector.scalar_tensor_tensor(
                            out=scratch[:, (2 * i + n) % 8, 0:TT], in0=zb[:, TT * i:TT * (i + 1)], scalar=zcol[:, i:i + 1],
                            in1=const(mask, TT), op0=op, op1=ALU.mult, accum_out=below[:, n, i:i + 1])
                link(ins)
                link(nc.vector.tensor_tensor(takes[:, 0], below[:, 0], below[:, 1], ALU.add))
                link(nc.vector.tensor_scalar(takes[:, 0], takes[:, 0], ROUTED - 0.5, None, ALU.is_lt))
                link(nc.vector.tensor_scalar(takes[:, 1], takes[:, 0], -1.0, 1.0, ALU.mult, ALU.add))

            def merge():
                for i in range(TILES):
                    if i % 2 == 0:
                        dve.wait_ge(att_ps, 3 + i // 2 + 1)
                    ins = nc.vector.scalar_tensor_tensor(
                        out=hp[:, i, :], in0=ps[0:TT, i // 2, D * (i % 2):D * (i % 2 + 1)], scalar=takes[:, 0, i:i + 1],
                        in1=h1[:, i, :], op0=ALU.mult, op1=ALU.add)
                link(ins)
                for i in range(TILES):
                    if i % 2 == 0:
                        dve.wait_ge(mix_ps, i // 2 + 1)
                    nc.vector.scalar_tensor_tensor(
                        out=hp[:, i, :], in0=ps[0:TT, 3 + i // 2, D * (i % 2):D * (i % 2 + 1)], scalar=takes[:, 1, i:i + 1],
                        in1=hp[:, i, :], op0=ALU.mult, op1=ALU.add).then_inc(merged, 1)

            def add_tokens(ready_at, base, bank, to, res):
                for j in range(3):
                    dve.wait_ge(ready_at, base + j + 1)
                    ins = nc.vector.tensor_tensor(to[:, 2 * j:2 * j + 2, :],
                                                  ps[0:TT, bank + j, 0:2 * D].rearrange("p (i d) -> p i d", i=2),
                                                  res[:, 2 * j:2 * j + 2, :], ALU.add)
                link(ins)

            def layer_norm(n, dst, src=zln, tiles=TILES):
                src = src if src is not None else ps[0:TT, 6, 0:2 * D].rearrange("p (i d) -> p i d", i=2)
                for i in range(tiles):
                    ins = nc.vector.bn_stats(stats[:, i, :], src[:, i, :])
                link(ins)
                for i in range(tiles):
                    ins = nc.vector.bn_aggr(mv[:, i, :], stats[:, i, :])
                link(ins)
                nc.vector.tensor_scalar(rstd[:, 0:tiles], mv[:, 0:tiles, 1], EPS, None, ALU.add).then_inc(var_rdy, 1)
                dve.wait_ge(rstd_rdy, n + 1)
                for i in range(tiles):
                    nc.vector.tensor_scalar(dst[:, i, :], src[:, i, :], mv[:, i, 0:1], rstd[:, i:i + 1], ALU.subtract,
                                            ALU.mult).then_inc(ln_out, 1)

            def embedding_norms():
                dve.wait_ge(in_emb, 16)
                link(nc.vector.tensor_tensor(emb2[:], emb[:], emb[:], ALU.mult))
                nc.vector.tensor_reduce(emb_n[:], emb2[:], AX, ALU.add).then_inc(emb2_rdy, 1)
                dve.wait_ge(emb_root, 1)
                link(nc.vector.tensor_scalar(emb_n[:], emb_n[:], 1e-8, None, ALU.add))
                link(nc.vector.reciprocal(emb_n[:], emb_n[:]))
                nc.vector.tensor_tensor(emb2[:], emb[:], emb_n[:].unsqueeze(2).to_broadcast([P, 2, 64]),
                                        ALU.mult).then_inc(emb_rdy, 1)

            def choose():
                for j in range(3):
                    dve.wait_ge(logit_sb, j + 1)
                    for q in range(4 * j, 4 * j + 4):
                        ins = nc.vector.max(top8[:, q, :], logit[:, q, 0:NN])
                link(ins)
                nc.vector.tensor_tensor(expo[:], logit[:, :, 0:NN], top8[:, :, 0:1].to_broadcast([TT, 2 * TILES, NN]),
                                        ALU.subtract).then_inc(shift_rdy, 1)
                dve.wait_ge(shift_rdy, 1)
                link(nc.vector.memset(top8[:, :, TOPK:8], SENTINEL))
                for q in range(2 * TILES):
                    ins = nc.vector.match_replace(kept[:, q, :], top8[:, q, :], logit[:, q, :], -SENTINEL)
                link(ins)
                nc.vector.tensor_tensor(chosen, logit[:, :, 0:NN], kept[:, :, 0:NN], ALU.not_equal).then_inc(chosen_rdy, 1)

            def tables():
                dve.wait_ge(count_ps, 1)
                link(nc.vector.tensor_copy(counts[:, 0:2], ps[:, 5, 0:2]))
                link(nc.vector.tensor_tensor(over[:], counts[:, 0:2].unsqueeze(2).to_broadcast([P, 2, 10]),
                                             const("steps64").unsqueeze(1).to_broadcast([P, 2, 10]), ALU.is_gt))
                nc.vector.tensor_reduce(counts[:, 2:4], over[:], AX, ALU.add)
                nc.vector.tensor_copy(count_wide[:], counts[:, 0:2].unsqueeze(2).to_broadcast([P, 2, TT])).then_inc(count_rdy, 1)

            def further_slots():
                dve.wait_ge(first_ps, 1)
                link(nc.vector.tensor_copy(first[:], ps[:, 6, 0:4]))
                link(nc.vector.tensor_tensor(reach[:], first[:, 2:4], counts[:, 2:4], ALU.add))
                link(nc.vector.tensor_scalar(delta[:], first[:, 2:4], float(SLOT), const("delta"), ALU.mult, ALU.add))
                nc.vector.tensor_copy(delta_wide[:], delta[:].unsqueeze(2).to_broadcast([P, 2, TT])).then_inc(delta_rdy, 1)
                link(nc.vector.scalar_tensor_tensor(out=first[:, 0:2], in0=first[:, 2:4], scalar=-float(SLOT),
                                                    in1=first[:, 0:2], op0=ALU.mult, op1=ALU.add))
                for r in range(2):
                    nc.vector.tensor_scalar(owns[:, 0], const("slots"), first[:, 2 + r:3 + r], None, ALU.is_ge)
                    link(nc.vector.tensor_scalar(owns[:, 1], const("slots"), reach[:, r:r + 1], None, ALU.is_lt))
                    link(nc.vector.tensor_tensor(owns[:, 2], owns[:, 0], owns[:, 1], ALU.mult))
                    nc.vector.scalar_tensor_tensor(out=table_f[:, r, 0, :], in0=const("slots64"), scalar=first[:, r:r + 1],
                                                   in1=owns[:, 2], op0=ALU.add, op1=ALU.mult)
                    ins = nc.vector.tensor_scalar(table_f[:, r, 1, :], owns[:, 2], const("neuron"), None, ALU.mult)
                    if r == 0:
                        link(ins)
                ins.then_inc(table_in, 1)
                dve.wait_ge(table_ps, 1)
                for r in range(2):
                    nc.vector.tensor_copy(table[:, r, 0:NN], ps[0:1, 7, NN * r:NN * (r + 1)])
                    at = 2 * NN + 2 * EXTRA * r
                    nc.vector.tensor_copy(table[:, r, NN:NN + EXTRA], ps[0:1, 7, at:at + EXTRA])
                    ins = nc.vector.tensor_copy(table[:, r, NN + EXTRA:], ps[0:1, 7, at + EXTRA:at + 2 * EXTRA])
                ins.then_inc(table_rdy, 1)

            def ranks_of(j, r):
                return ps[0:TT, 2 + j, :].rearrange("p (i r n) -> p i r n", i=2, r=2)[:, :, r, :]

            def rows_in_order(r):
                if r == 0:
                    dve.wait_ge(base_sb, 1)
                    dve.wait_ge(rank_ps, 3)
                for j in range(3):
                    ins = nc.vector.tensor_tensor(place[:, 4 * j + r:4 * j + 4:2, :], ranks_of(j, r),
                                                  base[:, 0, r:r + 1, :].to_broadcast([TT, 2, NN]), ALU.add)
                link(ins)
                link(nc.vector.tensor_tensor(place[:, r::2, :], place[:, r::2, :], chosen[:, r::2, :], ALU.mult))
                for i in range(TILES):
                    ins = nc.vector.max(slot8[:, 2 * i + r, :], place[:, 2 * i + r, :])
                link(ins)
                nc.vector.tensor_scalar(row_in[:, r::2, :], slot8[:, r::2, 0:TOPK], -1.0, None, ALU.add).then_inc(in_rdy, 1)

            def rows_of_products():
                dve.wait_ge(base_sb, 2)
                for r in range(2):
                    for j in range(3):
                        ins = nc.vector.scalar_tensor_tensor(
                            out=place_out[:, 4 * j + r:4 * j + 4:2, :], in0=ranks_of(j, r), scalar=SLOT + 0.5,
                            in1=base[:, 1, r:r + 1, :].to_broadcast([TT, 2, NN]), op0=ALU.is_gt, op1=ALU.mult)
                link(ins)
                for r in range(2):
                    for j in range(3):
                        ins = nc.vector.tensor_tensor(place_out[:, 4 * j + r:4 * j + 4:2, :], ranks_of(j, r),
                                                      place_out[:, 4 * j + r:4 * j + 4:2, :], ALU.add)
                ins.then_inc(ranks_used, 1)
                dve.wait_ge(ranks_used, 1)
                link(nc.vector.tensor_tensor(place_out[:], place_out[:],
                                             const("rows64", TT).unsqueeze(1).to_broadcast([TT, 2 * TILES, NN]), ALU.add))
                link(nc.vector.tensor_tensor(place_out[:], place_out[:], chosen, ALU.mult))
                for q in range(2 * TILES):
                    ins = nc.vector.max(slot8[:, q, :], place_out[:, q, :])
                link(ins)
                nc.vector.tensor_scalar(row_out[:], slot8[:, :, 0:TOPK], -1.0, None, ALU.add).then_inc(out_rdy, 1)

            def weights():
                dve.wait_ge(expo_rdy, 1)
                nc.vector.tensor_reduce(esum[:], expo[:], AX, ALU.add)
                n = 0
                for q in range(2 * TILES):
                    for k in range(TOPK):
                        ins = nc.vector.scalar_tensor_tensor(
                            out=scratch[:, n % 8, 0:NN], in0=place_out[:, q, :], scalar=slot8[:, q, k:k + 1],
                            in1=expo[:, q, :], op0=ALU.is_equal, op1=ALU.mult, accum_out=weight[:, q, k:k + 1])
                        n += 1
                        if n % 8 == 0:
                            link(ins)
                link(nc.vector.reciprocal(esum[:], esum[:]))
                link(nc.vector.tensor_tensor(weight[:], weight[:], esum[:].unsqueeze(2).to_broadcast([TT, 2 * TILES, TOPK]),
                                             ALU.mult))
                link(nc.vector.tensor_reduce(esum[:], weight[:], AX, ALU.add))
                link(nc.vector.tensor_scalar(esum[:], esum[:], 1e-8, None, ALU.add))
                link(nc.vector.reciprocal(esum[:], esum[:]))
                link(nc.vector.tensor_tensor(weight[:], weight[:], esum[:].unsqueeze(2).to_broadcast([TT, 2 * TILES, TOPK]),
                                             ALU.mult))

            offs = [dve.alloc_register(f"dve_first{j}") for j in range(8)]

            def neurons(st):
                dve.wait_ge(turned_sb, (10, 15)[st])
                dve.wait_ge(moe_buf, 2)

                def quad(o, buf):
                    for c in range(QUAD):
                        at = dve.snap(o[c], min_val=0, max_val=PAIRS)
                        x = staged[:, QUAD * buf + c, :]
                        if st == 0:
                            ins = nc.vector.tensor_copy(x[0:HALF].rearrange("p (m s) -> p m s", m=2), xg[:, :, bass.ds(at, SLOT)])
                        else:
                            ins = nc.vector.tensor_copy(x[:, 0:SLOT], hg[:, bass.ds(at, SLOT)])
                    ins.then_inc(staged_rdy, 1)

                def ring_quads(i, first):
                    for j in range(RING):
                        if j % 2 == 0:
                            dve.load(offs, table[0:1, st, bass.ds(QUAD * RING * i + QUAD * j, 2 * QUAD)])
                        if j >= 4 or not first:
                            dve.wait_ge(product, RING * i + (j - 3 + ALL * st))
                        quad(offs[4 * (j % 2):4 * (j % 2) + 4], j % 4)

                ring_quads(0, True)
                with dve.Fori(1, QUADS // RING) as i:
                    ring_quads(i, False)
                with dve.Fori(0, FURTHER // 3) as i:
                    for j in range(3):
                        dve.load(offs[0:4], table[0:1, st, bass.ds(NN + 3 * QUAD * i + QUAD * j, QUAD)])
                        dve.wait_ge(product, 3 * i + (j + QUADS - 2 + ALL * st))
                        quad(offs[0:4], j)

            def combine(st, got, dst, base):
                rows_of = [TT if i < TILES - 1 else LAST for i in range(TILES)]
                dve.wait_ge(gathered, 16 * TOPK * TILES * (st + 1))
                for k in range(TOPK):
                    for i, n in enumerate(rows_of):
                        w = weight[0:n, 2 * i + st, k:k + 1]
                        if k == 0 and base is None:
                            ins = nc.vector.tensor_scalar(dst[0:n, i, :], got[0:n, i, k, :], w, None, ALU.mult)
                        else:
                            ins = nc.vector.scalar_tensor_tensor(
                                out=dst[0:n, i, :], in0=got[0:n, i, k, :], scalar=w,
                                in1=base[0:n, i, :] if k == 0 else dst[0:n, i, :], op0=ALU.mult, op1=ALU.add)
                        if st == 0 and k == TOPK - 1:
                            ins.then_inc(combined, 1)
                    if not (st == 0 and k == TOPK - 1):
                        link(ins)

            dve.wait_ge(in_const, 16)
            embedding_norms()
            embed()
            dve.wait_ge(embT_ps, 1)
            nc.vector.tensor_copy(emb2[:].rearrange("p r e -> p (r e)"), ps[:, 7, 0:P]).then_inc(emb_sb, 1)
            attention(0)
            add_tokens(att_ps, 0, 0, zln, h0)
            layer_norm(0, h1)
            dve.wait_ge(ln_out, TILES)
            layer_norm(1, n1, h1)
            attention(1)
            merge()
            dve.wait_ge(merged, TILES)
            layer_norm(2, n1, hp)
            dve.wait_ge(hs_rdy, 1)
            add_tokens(ffn_ps, 0, 0, zln, hs)
            layer_norm(3, h2)
            dve.wait_ge(enc2_ps, 1)
            link(nc.vector.tensor_copy(code[:], ps[0:TT, 2, 0:TILES * ENC2].rearrange("p (i e) -> p i e", i=TILES)))
            link(nc.vector.tensor_tensor(code2[:], code[:], code[:], ALU.mult))
            link(nc.vector.tensor_reduce(norm2[:], code2[:], AX, ALU.add))
            nc.vector.tensor_scalar(norm2[:], norm2[:], 1e-16, None, ALU.max).then_inc(norm_rdy, 1)
            dve.wait_ge(inorm_rdy, 1)
            nc.vector.tensor_tensor(code2[:], code[:], norm2[:].unsqueeze(2).to_broadcast([TT, TILES, ENC2]),
                                    ALU.mult).then_inc(code_rdy, 1)
            dve.wait_ge(refsum_ps, 1)
            dve.wait_ge(code_rdy, 1)
            link(nc.vector.tensor_tensor(code[:, 0:2], code2[:, 0:2],
                                         ps[0:TT, 7, 0:ENC2].unsqueeze(1).to_broadcast([TT, 2, ENC2]), ALU.mult))
            nc.vector.tensor_reduce(alike[:], code[:, 0:2], AX, ALU.add).then_inc(alike_rdy, 1)
            dve.wait_ge(gram_ps, 1)
            nc.vector.scalar_tensor_tensor(
                out=gram[:], in0=ps[0:HALF, 3, 0:2 * HALF].rearrange("p (h f) -> p h f", h=2), scalar=1.0 / (DH * REFS),
                in1=const("headblock", HALF).unsqueeze(1).to_broadcast([HALF, 2, HALF]), op0=ALU.mult,
                op1=ALU.mult).then_inc(gram_sb, 1)
            dve.wait_ge(tanh_rdy, 1)
            nc.vector.tensor_scalar(gate[:, 0], alike[:], 0.5, 0.5, ALU.mult, ALU.add)
            link(nc.vector.tensor_scalar(gate[:, 1], alike[:], -0.5, 0.5, ALU.mult, ALU.add))
            dve.wait_ge(ln_out, 4 * TILES)
            for i in range(2):
                ins = nc.vector.tensor_scalar(n1[:, i, :], h2[:, i, :], gate[:, 0, i:i + 1], None, ALU.mult)
            ins.then_inc(gated, 1)
            for i in range(2):
                nc.vector.scalar_tensor_tensor(out=hs[:, i, :], in0=h2[:, i, :], scalar=gate[:, 1, i:i + 1],
                                               in1=h2[:, i, :], op0=ALU.mult, op1=ALU.add)
            nc.vector.tensor_scalar(zln[:, 2:TILES, :], h2[:, 2:TILES, :], 2.0, None, ALU.mult)
            for s in range(3):
                for i in range(2):
                    dve.wait_ge(qv_ps, 2 * s + i + 1)
                    nc.vector.tensor_tensor(
                        vmask[:, i], ps[0:TT, (3, 7)[i], 0:D].unsqueeze(1).to_broadcast([TT, 3, D]),
                        const("imageof", TT).unsqueeze(2).to_broadcast([TT, 3, D]), ALU.mult).then_inc(vmask_sb, 1)
                for i in range(2):
                    dve.wait_ge(m_ps, 2 * s + i + 1)
                    for h in range(2):
                        nc.vector.tensor_tensor(
                            mblock[:, h, 3 * i:3 * i + 3, :],
                            ps[0:HALF, 4 + 2 * h + i, 0:3 * HALF].rearrange("p (b f) -> p b f", b=3),
                            const("headblock", HALF).unsqueeze(1).to_broadcast([HALF, 3, HALF]), ALU.mult).then_inc(m_sb, 1)
                dve.wait_ge(o_ps, 2 * s + 2)
                for j in range(HEADS):
                    ins = nc.vector.tensor_copy(*folded(1, j))
                ins.then_inc(o_sb_dve, 1)
                dve.wait_ge(proj_ps, s + 1)
                layer_norm(4 + s, n1, None, 2)
            dve.wait_ge(ln_out, 4 * TILES + 6)
            link(nc.vector.tensor_tensor(n1[:, 0:2], n1[:, 0:2], diff_ln[:, 0:1, :].to_broadcast([TT, 2, D]), ALU.mult))
            link(nc.vector.tensor_tensor(n1[:, 0:2], n1[:, 0:2], diff_ln[:, 1:2, :].to_broadcast([TT, 2, D]), ALU.add))
            for i in range(2):
                ins = nc.vector.scalar_tensor_tensor(out=zln[:, i, :], in0=n1[:, i, :], scalar=gate[:, 0, i:i + 1],
                                                     in1=hs[:, i, :], op0=ALU.mult, op1=ALU.add)
            link(ins)
            layer_norm(7, h1)
            dve.wait_ge(moe_buf, 1)
            for r in range(2):
                ins = nc.vector.tensor_copy(emb_block[64 * r:64 * (r + 1), NN * r:NN * (r + 1)],
                                            emb2[64 * r:64 * (r + 1)].rearrange("p r e -> p (r e)"))
            ins.then_inc(emb_sb, 1)
            choose()
            tables()
            rows_in_order(0)
            further_slots()
            rows_in_order(1)
            rows_of_products()
            weights()
            neurons(0)
            combine(0, got_h, mixed_h, None)
            neurons(1)
            combine(1, got_y, zln, h1)
            layer_norm(8, hs)


def kernel(**inputs):
    import numpy as np
    import concourse.bacc as bacc
    from concourse import mybir
    from concourse.bass_utils import run_bass_kernel_spmd

    a = {k: np.asarray(v) for k, v in inputs.items()}
    f32 = np.float32

    def halves(w, bias=None, width=None):
        out = np.zeros((HALF + 1, 2, w.shape[1]), f32)
        out[:HALF] = w.reshape(2, HALF, -1).transpose(1, 0, 2)
        if bias is not None:
            out[HALF, 0] = bias
        return out

    def context_rows(w, bias):
        out = np.zeros((P, 2, D), f32)
        for g in range(GROUPS):
            out[64 * (g % 2):64 * (g % 2) + GF, g // 2] = w[GF * g:GF * (g + 1)]
        out[GF, 0] = bias
        return out

    def columns(v):
        return v.reshape(2, HALF).T

    pos = a["L0_tok_pos_embedding"][0].T.reshape(2, HALF, NT).transpose(1, 0, 2).reshape(HALF, 2 * NT)
    fc1_b = np.zeros((HALF, 1), f32)
    fc1_b[:ENC1, 0] = a["L1_attn_fc1_b"]
    vectors = np.concatenate(
        [columns(a["L0_ffn_g1"]), columns(a["L0_ffn_b1"]), columns(a["L0_ffn_g2"]), columns(a["L0_ffn_b2"]),
         columns(a["L1_attn_ln_g"]), columns(a["L1_attn_ln_b"]), columns(a["L0_tok_proj_b"]),
         columns(a["L0_tok_cls_token"][0, 0]), pos, fc1_b], axis=1)
    proj = np.zeros((P, 3, D), f32)
    for j in range(HEADS):
        proj[32 * (j % 4):32 * (j % 4) + DH, j // 4] = a["L1_attn_proj_w"][DH * j:DH * (j + 1)]
    proj[DH, 0] = a["L1_attn_proj_b"]
    fc2 = np.zeros((65, ENC2), f32)
    fc2[:ENC1] = a["L1_attn_fc2_w"]
    fc2[64] = a["L1_attn_fc2_b"]
    patches = a["x"].reshape(NB, 3, 6, 16, 6, 16).transpose(1, 3, 5, 0, 2, 4).reshape(6, P, NB * (NT - 1))
    wr = a["L0_ffn_Wr"].reshape(D, 1)
    arrays = {
        "constants": constants(),
        "vectors": vectors,
        "patches": patches.transpose(1, 0, 2),
        "token_w": a["L0_tok_proj_w"].T.reshape(6, P, D).transpose(1, 0, 2),
        "attn1_w": np.concatenate([halves(a[f"L0_attn_W{c}"].T, a[f"L0_attn_b{c}"]) for c in "qkv"], axis=2),
        "attn1_wo": context_rows(a["L0_attn_Wo"].T, a["L0_attn_bo"]),
        "attn2_w": np.concatenate(
            [halves(a[f"L0_ffn_W{c}"], a[f"L0_ffn_b{c}"]) for c in "qkvm"]
            + [halves(np.repeat(wr, TT, axis=1), a["L0_ffn_br"])], axis=2),
        "attn2_wo": context_rows(a["L0_ffn_Wo"], a["L0_ffn_bo"]),
        "ffn_w1": halves(a["L0_ffn_W1"])[:HALF],
        "ffn_b1": a["L0_ffn_bf1"].reshape(6, P).T,
        "ffn_w2": a["L0_ffn_W2"].reshape(6, P, D).transpose(1, 0, 2),
        "ffn_b2": a["L0_ffn_bf2"].reshape(1, D),
        "diff_w": np.concatenate(
            [halves(a["L1_attn_qv_w"]), halves(a["L1_attn_k_w"]),
             halves(a["L1_attn_fc1_w"]), halves(a["L1_ffn_W_fk"], a["L1_ffn_b_fk"]),
             halves(a["L1_ffn_W_rk"], a["L1_ffn_b_rk"])], axis=2),
        "diff_ln": np.stack([np.broadcast_to(a["L1_attn_ln_g"], (TT, D)), np.broadcast_to(a["L1_attn_ln_b"], (TT, D))], 1),
        "enc_w2": fc2,
        "proj_w": proj,
        "emb": np.stack([a["L1_ffn_emb_fk"], a["L1_ffn_emb_rk"]], axis=1),
        "feature_w": a["L1_ffn_f_know"].reshape(NN, 2, HALF, R).transpose(2, 0, 1, 3).reshape(HALF, NN, 2 * R),
        "restore_w": a["L1_ffn_r_know"].transpose(1, 0, 2),
    }
    arrays = {k: np.ascontiguousarray(v) for k, v in arrays.items()}
    nc = bacc.Bacc("TRN2", target_bir_lowering=False, num_devices=1)
    handles = {k: nc.dram_tensor(f"in_{k}", v.shape, mybir.dt.float32, kind="ExternalInput").ap() for k, v in arrays.items()}
    out = nc.dram_tensor("tower", (NB, NT, D), mybir.dt.float32, kind="ExternalOutput").ap()
    vit_tower(nc, handles, out)
    r = run_bass_kernel_spmd(nc, [{f"in_{k}": v for k, v in arrays.items()}], core_ids=[0])
    return r.results[0]["tower"]
```

```python
from contextlib import ExitStack

import numpy as np

import concourse.bass as bass
from concourse import mybir

ALU = mybir.AluOpType
ACT = mybir.ActivationFunctionType
AX = mybir.AxisListType.X
F32 = mybir.dt.float32
BF16 = mybir.dt.bfloat16
I32 = mybir.dt.int32
U32 = mybir.dt.uint32

P = 128
NB, NT, D = 16, 37, 192
T = NB * NT
HALF = D // 2
HEADS, DH = 12, 16
GROUPS, GF = 4, 3 * DH
TT = 3 * NT
TILES = -(-NB // 3)
PAD = TILES * TT
LAST = T - (TILES - 1) * TT
CH = T // 2
F = 768
ENC1, ENC2 = 48, 24
XM = 6
XT_ = XM * NT
REFS = NB - XM
ROUTED = 6
EPS = 1e-5
NN, R, TOPK = 128, 128, 4
PAIRS = T * TOPK
SLOT = 64
EXTRA = (PAIRS - NN) // SLOT + 1
SLOTS = NN + EXTRA
PCOLS = PAIRS + SLOT
WIDE = -(-T // P)
WIDE_ROWS = [min(P, T - P * i) for i in range(WIDE)]
PTILES = -(-PAIRS // P)
PLAST = PAIRS - (PTILES - 1) * P
SENTINEL = 3e38
QUAD = 4
QUADS, FURTHER = NN // QUAD, EXTRA // QUAD
AHEAD = 17
TURN = [0, "a", 1, 2, "b", 3, "c", 4]
OWN = 5
TURNS = (QUADS - AHEAD) // OWN
BANKS = 4

_WIDTHS = [("ident", P), ("same", TT), ("earlier", TT), ("upto", TT), ("spread", 3 * TT), ("vmask", GF), ("headof", 6),
           ("imageof", 3), ("headblock", HALF), ("before", P), ("sametoken", TT), ("steps64", 10), ("slots", EXTRA),
           ("slots64", EXTRA), ("neuron", 1), ("rows64", NN), ("delta", 1)]
CONST = {}
_at = 0
for _name, _w in _WIDTHS:
    CONST[_name] = (_at, _w)
    _at += _w
NCONST = _at


def constants():
    p, c = np.arange(P)[:, None], np.arange(3 * TT)[None]
    t, u = c[:, :TT], c[:, :P]
    e = np.arange(EXTRA)[None]
    parts = {
        "ident": p == u,
        "same": p // NT == t // NT,
        "earlier": (p // NT == t // NT) & (t < p),
        "upto": p <= t,
        "spread": np.concatenate([p == NT * b + t % NT for b in range(3)], axis=1),
        "vmask": p // NT == c[:, :GF] // DH,
        "headof": p // DH == c[:, :6],
        "imageof": p // NT == c[:, :3],
        "headblock": p // DH == c[:, :HALF] // DH,
        "before": p < u,
        "sametoken": p % NT == t % NT,
        "steps64": SLOT * (1 + np.arange(10))[None] + 0 * p,
        "slots": e + 0 * p,
        "slots64": SLOT * (e + 1) + 0 * p,
        "neuron": p,
        "rows64": SLOT * u + 0 * p,
        "delta": SLOT * (NN - 1) - SLOT * p,
    }
    return np.concatenate([np.asarray(parts[n], np.float32) for n, _ in _WIDTHS], axis=1)


G1, B1, G2, B2, LNG, LNB, TOKB, CLS, POS = 0, 2, 4, 6, 8, 10, 12, 14, 16
FC1B = POS + 2 * NT
NVEC = FC1B + 1
QV, KW, FC1, ROUTE = 0, 2 * D, 3 * D, 3 * D + ENC1
NDIFF = ROUTE + P
MIXW, RW = 3 * D, 4 * D
NATT2 = RW + TT


def vit_tower(nc, dram, out):
    with ExitStack() as ctx:
        def sb(name, shape, dt=F32):
            return ctx.enter_context(nc.sbuf_tensor(name, shape, dt))

        def sem(name):
            return ctx.enter_context(nc.semaphore(name))

        ps = ctx.enter_context(nc.psum_tensor("ps", [P, 8, 512], F32))

        def carve(base, shapes, start=0):
            views = []
            for rows, *dims in shapes:
                size = int(np.prod(dims))
                view = base[0:rows, start:start + size]
                names = "abc"[:len(dims)]
                if len(dims) > 1:
                    view = view.rearrange(f"p ({' '.join(names)}) -> p {' '.join(names)}", **dict(zip(names, dims)))
                views.append(view)
                start += size
            assert start <= base.shape[1], (start, base.shape)
            return views

        cst = sb("cst", [P, NCONST])
        vec = sb("vec", [HALF, NVEC])
        early = sb("early", [P, 4 * 8 * 2 * R])
        main = sb("main", [P, 24700])

        def const(name, rows=P):
            a, w = CONST[name]
            return cst[0:rows, a:a + w]

        ident = const("ident")

        patches, token_w = carve(early, [(P, 6, NB * (NT - 1)), (P, 6, D)])
        (hid,) = carve(early, [(P, 6, PAD)])

        xt = [sb(f"xt{n}", [HALF + 1, 2, PAD]) for n in range(3)]
        xt += xt[0:2]
        posb = sb("posb", [HALF, 2, NT])
        h1 = sb("h1", [TT, TILES, D])
        zln = sb("zln", [TT, TILES, D])
        n1 = sb("n1", [TT, TILES, D])
        h2 = sb("h2", [TT, TILES, D])
        hs = sb("hs", [TT, TILES, D])
        stats = sb("stats", [P, TILES, 6])
        mv = sb("mv", [P, TILES, 2])
        rstd = sb("rstd", [P, TILES])
        power = sb("power", [P, TILES])
        (w_a, w_b, wo_a, wo_b, w1, w2, qt, kt, kx, vtok, vx, probsT, ctxT, h0) = carve(
            main, [(HALF + 1, 2, 3 * D), (HALF + 1, 2, NATT2), (P, 2, D), (P, 2, D), (HALF, 2, F), (P, 6, D),
                   (HALF, 2, T + 64 - NT), (HALF, 2, T), (HALF, 2, 6, T), (TT, TILES, D), (TT, NB, GROUPS, GF),
                   (TT, 2, 4 * P), (P, 2, PAD), (TT, TILES, D)])
        attn_w, attn_wo = [w_a, w_b], [wo_a, wo_b]
        hp = h0
        weighed = kt
        late = sb("late", [P, 3 * QUAD * 2 * R])
        (mixT, zb, sig) = carve(late, [(HALF + 1, 2, PAD), (TT, PAD), (HALF, T)])
        shifted, probs = carve(early, [(P, 3, HEADS * NT), (P, 3, HEADS * NT)], start=6 * (NB * (NT - 1) + D))
        smax = sb("smax", [P, 3, HEADS])
        ssum = sb("ssum", [P, 3, HEADS])
        sinv = sb("sinv", [P, 3, HEADS])
        sigsum = sb("sigsum", [HALF, NB])
        pooled = sb("pooled", [HALF, 2, NB])
        zcol = sb("zcol", [TT, TILES])
        below = sb("below", [TT, 2, TILES])
        takes = sb("takes", [TT, 2, TILES])
        scratch = zln[:].rearrange("p i d -> p (i d)")[:, 0:8 * P].rearrange("p (a b) -> p a b", b=P)
        b1 = sb("b1", [P, 6])
        b2 = sb("b2", [1, D])
        ones = sb("ones", [P, P])
        diff_w = sb("diff_w", [HALF + 1, 2, NDIFF])
        proj_w = sb("proj_w", [P, 3, D])
        diff_ln = sb("diff_ln", [TT, 2, D])
        enc_w2 = sb("enc_w2", [65, ENC2])
        (enc1, code, code2, ksb, gram, qtok, vmask, mblock, gmask, qd, xd, od) = carve(
            main, [(65, PAD), (TT, TILES, ENC2), (TT, TILES, ENC2), (TT, 4, D), (HALF, 2, HALF), (TT, 2, D),
                   (TT, 2, 3, D), (HALF, 2, XM, HALF), (HALF, 2, XM, HALF), (HALF, 2, XT_), (HALF + 1, 2, XT_),
                   (P, 3, XT_)], start=14000)
        norm2 = sb("norm2", [TT, TILES])
        (xg, hg, staged, products, extra, rows, logit, kept, expo, base, sel_f32) = carve(
            main, [(HALF, 2, PCOLS), (P, PCOLS), (P, BANKS * QUAD, 2 * SLOT), (P, BANKS, 2 * D), (P, 3, QUAD * 2 * R),
                   (P, PTILES, D), (TT, 2 * TILES, NN + 4), (TT, 2 * TILES, NN + 4), (TT, 2 * TILES, NN),
                   (TT, 2, 2, NN), (TT, TILES * NN)])

        def spans(buffer, width, n):
            return [buffer[:, width * j:width * (j + 1)] for j in range(n)]

        def flat_of(buffer):
            return buffer[:].rearrange("p a b -> p (a b)")

        rings = [spans(early, QUAD * 2 * R, 8) + spans(late, QUAD * 2 * R, 3) + spans(hg, QUAD * 2 * R, 2)
                 + [flat_of(x) for x in (xt[2], xt[0], h2, hs)],
                 spans(early, QUAD * D, 10) + spans(late, QUAD * D, 4) + spans(main, QUAD * D, 3)]
        before_rows = 2 * PCOLS + PCOLS + BANKS * QUAD * 2 * SLOT + BANKS * 2 * D + 3 * QUAD * 2 * R
        (keyT, emb_block, count_wide, delta_wide) = carve(
            main, [(P, PAD), (P, 2 * NN), (P, 2, TT), (P, 2, TT)], start=before_rows)
        (place,) = carve(main, [(TT, 2 * TILES, NN)], start=3 * PCOLS)
        place_out = kept[:, :, 0:NN]
        (got_y,) = carve(main, [(P, WIDE, TOPK, D)])
        got_h = rows[:].rearrange("p t f -> p (t f)")[:, 0:WIDE * TOPK * R].rearrange(
            "p (i k r) -> p i k r", i=WIDE, k=TOPK)
        mixed_h = extra[:, 0, 0:WIDE * R].rearrange("p (i r) -> p i r", r=R)
        (h1_wide,) = carve(main, [(P, WIDE, D)], start=before_rows + PTILES * D)
        (z_wide, out_wide) = carve(main, [(P, WIDE, D), (P, WIDE, D)],
                                   start=before_rows + PTILES * D + 2 * TILES * (NN + 4))
        chosen = sel_f32.bitcast(BF16).rearrange("p (q n) -> p q n", n=NN)
        emb = sb("emb", [P, 2, 64])
        emb2 = sb("emb2", [P, 2, 64])
        emb_n = sb("emb_n", [P, 2])
        half_p = sb("half_p", [P, 2])
        ones_bf = sb("ones_bf", [P, TT], BF16)
        upto_bf = sb("upto_bf", [TT, TT], BF16)
        top8 = sb("top8", [TT, 2 * TILES, 8])
        slot8 = sb("slot8", [TT, 2 * TILES, 8])
        row_in = sb("row_in", [TT, 2 * TILES, TOPK], U32)
        row_out = sb("row_out", [TT, 2 * TILES, TOPK], U32)
        weight = sb("weight", [TT, 2 * TILES, TOPK])
        esum = sb("esum", [TT, 2 * TILES])
        rows_wide = sb("rows_wide", [P, WIDE, 3 * TOPK], U32)
        weight_wide = sb("weight_wide", [P, WIDE, 2 * TOPK])
        counts = sb("counts", [P, 4])
        over = sb("over", [P, 2, 10])
        first = sb("first", [P, 4])
        reach = sb("reach", [P, 2])
        delta = sb("delta", [P, 2])
        owns = sb("owns", [P, 3, EXTRA])
        table_f = sb("table_f", [P, 2, 2, EXTRA])
        table = sb("table", [1, 2, NN + 2 * EXTRA], I32)
        alike = sb("alike", [TT, 2])
        gate = sb("gate", [TT, 2, 2])

        xs = nc.dram_tensor("xs", (PAIRS, D), F32, kind="Internal").ap()
        rows_d = nc.dram_tensor("rows_d", (T, 3 * TOPK), U32, kind="Internal").ap()
        weight_d = nc.dram_tensor("weight_d", (T, 2 * TOPK), F32, kind="Internal").ap()
        h1_d = nc.dram_tensor("h1_d", (T, D), F32, kind="Internal").ap()
        hxs = nc.dram_tensor("hxs", (PAIRS, R), F32, kind="Internal").ap()
        hsd = nc.dram_tensor("hsd", (SLOTS * SLOT, R), F32, kind="Internal").ap()
        ysd = nc.dram_tensor("ysd", (SLOTS * SLOT, D), F32, kind="Internal").ap()

        def sems(names):
            return [sem(n) for n in names.split()]

        dve_chain, pool_chain = sems("dve_chain pool_chain")
        ready, pads_rdy, buf_rdy, moe_buf = sems("ready pads_rdy buf_rdy moe_buf")
        in_const, in_vec, in_w1, in_w2, in_ffn, in_diff, in_emb = sems("in_const in_vec in_w1 in_w2 in_ffn in_diff in_emb")
        in_tok = [sem(f"in_tok{j}") for j in range(3)]
        tok_ps, tok_xt, h0_ps, h0_sb = sems("tok_ps tok_xt h0_ps h0_sb")
        qk_ps, q_sb, k_sb, kx_sb, v_ps, v_sb, vrep_ps, vx_sb = sems("qk_ps q_sb k_sb kx_sb v_ps v_sb vrep_ps vx_sb")
        score_ps, score_used, exped, inv_rdy, prob_sb = sems("score_ps score_used exped inv_rdy prob_sb")
        probT_ps, probT_sb, ctx_ps, ctx_sb, att_ps = sems("probT_ps probT_sb ctx_ps ctx_sb att_ps")
        var_rdy, rstd_rdy, ln_out, turn_ps, xt_rdy = sems("var_rdy rstd_rdy ln_out turn_ps xt_rdy")
        refs_out = sem("refs_out")
        z_ps, e_sb, sig_rdy, weighed_rdy, pooled_rdy = sems("z_ps e_sb sig_rdy weighed_rdy pooled_rdy")
        mixT_rdy, mix_ps, merged = sems("mixT_rdy mix_ps merged")
        hid_ps, hid_sb, ffn_ps, hs_rdy = sems("hid_ps hid_sb ffn_ps hs_rdy")
        enc1_ps, enc1_sb, enc2_ps, norm_rdy, inorm_rdy = sems("enc1_ps enc1_sb enc2_ps norm_rdy inorm_rdy")
        code_rdy, refsum_ps, alike_rdy, tanh_rdy, gated = sems("code_rdy refsum_ps alike_rdy tanh_rdy gated")
        k_ref_ps, k_ref_sb, gram_ps, gram_sb = sems("k_ref_ps k_ref_sb gram_ps gram_sb")
        xd_ps, xd_sb, qtok_ps, qtok_sb, qv_ps, vmask_sb, qd_ps, qd_sb = sems(
            "xd_ps xd_sb qtok_ps qtok_sb qv_ps vmask_sb qd_ps qd_sb")
        m_ps, m_sb, gm_ps, gm_sb, o_ps, o_sb, proj_ps = sems("m_ps m_sb gm_ps gm_sb o_ps o_sb proj_ps")
        emb2_rdy, emb_root, emb_rdy, embT_ps, emb_sb, bf_rdy = sems("emb2_rdy emb_root emb_rdy embT_ps emb_sb bf_rdy")
        key_ps, key_sb, logit_ps, logit_sb, chosen_rdy = sems("key_ps key_sb logit_ps logit_sb chosen_rdy")
        count_ps, count_rdy, over_rdy, rank_ps, ranks_used = sems("count_ps count_rdy over_rdy rank_ps ranks_used")
        base_ps, base_sb, delta_rdy, first_ps = sems("base_ps base_sb delta_rdy first_ps")
        table_in, table_ps, table_rdy, in_rdy, out_rdy = sems("table_in table_ps table_rdy in_rdy out_rdy")
        shift_rdy, expo_rdy, weight_rdy, zero_rdy = sems("shift_rdy expo_rdy weight_rdy zero_rdy")
        scattered, turned_ps, turned_sb, combined, stored = sems("scattered turned_ps turned_sb combined stored")
        rows_in = [sem(f"rows_in{j}") for j in range(4)]
        gathered = [sem(f"gathered{i}") for i in range(WIDE)]
        tokens_out, tokens_in, weights_out, in_weights = sems("tokens_out tokens_in weights_out in_weights")
        ring_in = [sem(f"ring_in{j}") for j in range(OWN + (AHEAD - OWN) // 3)]
        extra_in = [sem(f"extra_in{j}") for j in range(3)]
        stored_rows = [sem(f"stored_rows{j}") for j in range(BANKS)]
        staged_rdy, product, taken = sems("staged_rdy product taken")
        ALL = QUADS + FURTHER
        STORES = [len(range(j, ALL, BANKS)) for j in range(BANKS)]

        def loaded(j):
            return (ring_in[j], 1 + TURNS) if j < OWN else (ring_in[OWN + (j - OWN) // 3], 3)

        def turns(i, p):
            return len(TURN) * i + (p + AHEAD - len(TURN))

        def which(i, q):
            return OWN * i + (AHEAD - OWN + q) if q in range(OWN) else 3 * i + (QUADS - 3 + "abc".index(q))

        def bank_of(p):
            return (AHEAD + p) % BANKS

        assert len(TURN) % BANKS == 0 and TURNS == FURTHER // 3

        block = ctx.enter_context(nc.Block())

        def folded(i, j):
            to = od[32 * (j % 4):32 * (j % 4) + DH, j // 4, TT * i:TT * (i + 1)].rearrange("p (b n) -> p b n", b=3)
            return to, ps[0:DH, 4 * i:4 * i + 3, j:HEADS * NT:HEADS]

        PAIRS_OF_IMAGES = NB // 2

        def to_dram(queue, d, src, done):
            full = TT * (TILES - 1)
            queue.dma_start(d[0:full].rearrange("(i p) c -> p i c", p=TT), src[:, 0:TILES - 1]).then_inc(done, 16)
            queue.dma_start(d[full:T], src[0:LAST, TILES - 1]).then_inc(done, 16)

        def from_dram(queue, dst, d, done):
            full = P * (WIDE - 1)
            queue.dma_start(dst[:, 0:WIDE - 1], d[0:full].rearrange("(i p) c -> p i c", p=P)).then_inc(done, 16)
            queue.dma_start(dst[0:WIDE_ROWS[-1], WIDE - 1], d[full:T]).then_inc(done, 16)

        @block.sync
        def _(sp):
            for j in range(3):
                sp.dma_start(token_w[:, 2 * j:2 * j + 2], dram["token_w"][:, 2 * j:2 * j + 2]).then_inc(in_tok[j], 16)
                sp.dma_start(patches[:, 2 * j:2 * j + 2], dram["patches"][:, 2 * j:2 * j + 2]).then_inc(in_tok[j], 16)
            sp.dma_start(cst[:], dram["constants"]).then_inc(in_const, 16)
            sp.dma_start(vec[:], dram["vectors"]).then_inc(in_vec, 16)
            sp.dma_start(attn_w[0][:], dram["attn1_w"]).then_inc(in_w1, 16)
            sp.dma_start(attn_wo[0][:], dram["attn1_wo"]).then_inc(in_w1, 16)
            sp.dma_start(attn_w[1][:], dram["attn2_w"]).then_inc(in_w2, 16)
            sp.dma_start(attn_wo[1][:], dram["attn2_wo"]).then_inc(in_w2, 16)
            sp.dma_start(emb[:], dram["emb"]).then_inc(in_emb, 16)
            for t, n in ((w1, "ffn_w1"), (b1, "ffn_b1"), (w2, "ffn_w2"), (b2, "ffn_b2")):
                sp.dma_start(t[:], dram[n]).then_inc(in_ffn, 16)
            for t, n in ((diff_w, "diff_w"), (proj_w, "proj_w"), (diff_ln, "diff_ln"), (enc_w2, "enc_w2")):
                sp.dma_start(t[:], dram[n]).then_inc(in_diff, 16)

            def weights_in(st, to, at):
                n = (HALF, P)[st]
                w, width = dram[("feature_w", "restore_w")[st]], (2 * R, D)[st]
                return sp.dma_start(to[0:n, 0:QUAD * width].rearrange("p (c f) -> p c f", c=QUAD), w[:, bass.ds(at, QUAD), :])

            def prefetch(st):
                for j in range(AHEAD):
                    if st == 1 and j == 0:
                        sp.wait_ge(product, ALL)
                    if st == 0 and j == AHEAD - 3:
                        sp.wait_ge(k_ref_ps, 2)
                    if st == 0 and j == AHEAD - 2:
                        sp.wait_ge(ln_out, 4 * TILES + 6 + 1)
                    weights_in(st, rings[st][j], QUAD * j).then_inc(loaded(j)[0], 16)

            sp.wait_ge(ffn_ps, 3)
            prefetch(0)

            def tiles_of(d, a, b):
                return d[P * a:P * b, :].rearrange("(t p) f -> p t f", p=P)

            def pairs_in(st, d, width):
                sp.wait_ge(scattered, 16 * TOPK * (TILES + WIDE * st))
                for j in range(3):
                    sp.dma_start(rows[:, 6 * j:6 * j + 6, 0:width], tiles_of(d, 6 * j, 6 * j + 6)).then_inc(rows_in[j], 16)
                sp.dma_start(rows[0:PLAST, PTILES - 1, 0:width], d[P * (PTILES - 1):PAIRS, :]).then_inc(rows_in[3], 16)

            regs = [sp.alloc_register(f"sp_neuron{j}") for j in range(QUAD)]

            def neurons(st):
                n, width = (HALF, P)[st], (2 * R, D)[st]
                w = dram[("feature_w", "restore_w")[st]]

                def turn(i):
                    for p, q in enumerate(TURN):
                        before = turns(i - 1, p)
                        if q in range(OWN):
                            sp.wait_ge(product, (q if isinstance(i, int) else before) + (1 + ALL * st))
                            weights_in(st, rings[st][q], which(i, q) * QUAD).then_inc(ring_in[q], 16)
                            continue
                        e = "abc".index(q)
                        sp.load(regs, table[0:1, st, bass.ds(which(i, q) * QUAD + EXTRA, QUAD)])
                        if not isinstance(i, int):
                            sp.wait_ge(product, before + (1 + ALL * st))
                        for c in range(QUAD):
                            neuron = sp.snap(regs[c], min_val=0, max_val=NN - 1)
                            sp.dma_start(extra[0:n, e, width * c:width * (c + 1)],
                                         w[:, bass.ds(neuron, 1), :].rearrange("p o f -> p (o f)")).then_inc(extra_in[e], 16)

                sp.wait_ge(table_rdy, 1)
                turn(1)
                with sp.Fori(2, TURNS + 1) as i:
                    turn(i)

            sp.wait_ge(base_ps, 3)
            pairs_in(0, xs, D)
            neurons(0)
            for j in range(BANKS):
                sp.wait_ge(stored_rows[j], 16 * STORES[j])
            prefetch(1)
            sp.wait_ge(weight_rdy, 2)
            to_dram(sp, weight_d[:, TOPK:], weight[:, 1::2, :], weights_out)
            sp.wait_ge(weights_out, 2 * 16)
            from_dram(sp, weight_wide[:, :, TOPK:], weight_d[:, TOPK:], in_weights)
            pairs_in(1, hxs, R)
            neurons(1)
            flat = out.rearrange("b n d -> (b n) d")
            for i, n in enumerate(WIDE_ROWS):
                sp.wait_ge(ln_out, 4 * TILES + 6 + 2 + i + 1)
                sp.dma_start(flat[P * i:P * i + n, :], out_wide[0:n, i, :]).then_inc(stored, 16)
            sp.wait_ge(stored, 16 * WIDE)

        @block.gpsimd
        def _(pool):
            steps = [0]

            def link(ins):
                steps[0] += 1
                ins.then_inc(pool_chain, 1)
                pool.wait_ge(pool_chain, steps[0])

            for x in xt[0:3]:
                nc.gpsimd.memset(x[:, :, T:PAD], 0.0)
            nc.gpsimd.memset(qt[:, :, T:], 0.0)
            nc.gpsimd.memset(ctxT[:], 1.0)
            nc.gpsimd.memset(zb[:, T:PAD], 0.0)
            nc.gpsimd.memset(mixT[:, :, T:PAD], 0.0)
            nc.gpsimd.memset(ones[:], 1.0)
            nc.gpsimd.memset(half_p[:], 0.5)
            link(nc.gpsimd.memset(power[:], -0.5))
            for x in (*xt[0:3], mixT):
                ins = nc.gpsimd.memset(x[HALF:HALF + 1, :, :], 1.0)
            ins.then_inc(ready, 1)

            def softmax_products(a):
                for p in range(PAIRS_OF_IMAGES):
                    n = a * PAIRS_OF_IMAGES + p
                    if a == 1 and p == 3:
                        weigh()
                    pool.wait_ge(inv_rdy, n + 1)
                    if n >= 3:
                        pool.wait_ge(probT_ps, n - 2)
                    e = shifted[:, n % 3, :].rearrange("p (h k) -> p h k", h=HEADS)
                    nc.gpsimd.tensor_tensor(
                        probs[:, n % 3, :].rearrange("p (h k) -> p h k", h=HEADS), e,
                        sinv[:, n % 3, :].unsqueeze(2).to_broadcast([P, HEADS, NT]), ALU.mult).then_inc(prob_sb, 1)

            def weigh():
                pool.wait_ge(sig_rdy, 1)
                pool.wait_ge(xt_rdy, 3)
                nc.gpsimd.tensor_tensor(weighed[:], xt[1][0:HALF, :, 0:T], sig[:].unsqueeze(1).to_broadcast([HALF, 2, T]),
                                        ALU.mult).then_inc(weighed_rdy, 1)

            def mixed_inputs():
                pool.wait_ge(pooled_rdy, 1)
                for m in range(2):
                    ins = nc.gpsimd.tensor_tensor(
                        weighed[:, m, :].rearrange("p (b t) -> p b t", b=NB), sig[:].rearrange("p (b t) -> p b t", b=NB),
                        pooled[:, m, :].unsqueeze(2).to_broadcast([HALF, NB, NT]), ALU.mult)
                link(ins)
                nc.gpsimd.tensor_tensor(mixT[0:HALF, :, 0:T], weighed[:], xt[1][0:HALF, :, 0:T],
                                        ALU.add).then_inc(mixT_rdy, 1)

            def root(n, tiles=TILES, rows=TT):
                pool.wait_ge(var_rdy, n + 1)
                nc.gpsimd.tensor_tensor(rstd[0:rows, 0:tiles], rstd[0:rows, 0:tiles], power[0:rows, 0:tiles],
                                        ALU.pow).then_inc(rstd_rdy, 1)

            pool.wait_ge(in_const, 16)
            pool.wait_ge(ready, 1)
            link(nc.gpsimd.tensor_copy(ones_bf[:], ones[:, 0:TT]))
            nc.gpsimd.tensor_copy(upto_bf[:], const("upto", TT)).then_inc(bf_rdy, 1)
            pool.wait_ge(emb2_rdy, 1)
            pool.wait_ge(bf_rdy, 1)
            nc.gpsimd.tensor_tensor(emb_n[:], emb_n[:], half_p[:], ALU.pow).then_inc(emb_root, 1)
            softmax_products(0)
            root(0)
            root(1)
            nc.gpsimd.memset(hid[:, :, T:PAD], 0.0).then_inc(pads_rdy, 1)
            softmax_products(1)
            mixed_inputs()
            root(2)
            pool.wait_ge(merged, TILES)
            nc.gpsimd.tensor_tensor(hs[:], h1[:], hp[:], ALU.add).then_inc(hs_rdy, 1)
            pool.wait_ge(hs_rdy, 1)
            pool.wait_ge(ffn_ps, 1)
            link(nc.gpsimd.memset(enc1[:], 1.0))
            link(nc.gpsimd.memset(xd[HALF:HALF + 1, :, :], 1.0))
            ins = nc.gpsimd.memset(od[:], 1.0)
            ins.then_inc(buf_rdy, 1)
            pool.wait_ge(buf_rdy, 1)
            root(3)
            pool.wait_ge(norm_rdy, 1)
            nc.gpsimd.tensor_tensor(norm2[:], norm2[:], power[0:TT], ALU.pow).then_inc(inorm_rdy, 1)
            for n in range(7):
                pool.wait_ge(var_rdy, 4 + n + 1)
                a, b = (2, TILES) if n == 0 else ((n - 1) % 2, (n - 1) % 2 + 1)
                nc.gpsimd.tensor_tensor(rstd[0:TT, a:b], rstd[0:TT, a:b], power[0:TT, a:b], ALU.pow).then_inc(rstd_rdy, 1)
            pool.wait_ge(xd_sb, 6)
            nc.gpsimd.memset(emb_block[:], 0.0)
            link(nc.gpsimd.memset(keyT[:, T:PAD], 0.0))
            nc.gpsimd.memset(logit[:, :, NN:NN + 4], SENTINEL).then_inc(moe_buf, 1)
            root(11, 2)
            rows_of = [TT if i < TILES - 1 else LAST for i in range(TILES)]

            def scatter(d, src, tiles, row_of, need):
                for i, n in enumerate(tiles):
                    if need is not None:
                        pool.wait_ge(need, i + 1)
                    for k in range(TOPK):
                        nc.gpsimd.indirect_dma_start(
                            out=d[:, :], out_offset=bass.IndirectOffsetOnAxis(ap=row_of(i, k)[0:n], axis=0),
                            in_=src[0:n, i, :], in_offset=None).then_inc(scattered, 16)

            def gather(st, dst, d):
                for j in range(BANKS):
                    pool.wait_ge(stored_rows[j], 16 * STORES[j] * (st + 1))
                for i, n in enumerate(WIDE_ROWS):
                    for k in range(TOPK):
                        at = rows_wide[0:n, i, TOPK * st + k:TOPK * st + k + 1]
                        nc.gpsimd.indirect_dma_start(out=dst[0:n, i, k, :], out_offset=None, in_=d[:, :],
                                                     in_offset=bass.IndirectOffsetOnAxis(ap=at, axis=0)).then_inc(gathered[i], 16)

            link(nc.gpsimd.memset(xg[:, :, PAIRS:PCOLS], 0.0))
            nc.gpsimd.memset(hg[:, PAIRS:PCOLS], 0.0).then_inc(moe_buf, 1)
            pool.wait_ge(ln_out, 4 * TILES + 6 + 2)
            pool.wait_ge(refs_out, TILES - 2)
            pool.wait_ge(in_rdy, 1)
            scatter(xs, h1, rows_of, lambda i, k: row_in[:, 2 * i, k:k + 1], None)
            pool.wait_ge(in_rdy, 2)
            pool.wait_ge(out_rdy, 1)
            pool.wait_ge(weight_rdy, 1)
            to_dram(nc.gpsimd, rows_d[:, 0:2 * TOPK], row_out[:].rearrange("p (i r) k -> p i (r k)", r=2), tokens_out)
            to_dram(nc.gpsimd, rows_d[:, 2 * TOPK:], row_in[:, 1::2, :], tokens_out)
            to_dram(nc.gpsimd, weight_d[:, 0:TOPK], weight[:, 0::2, :], tokens_out)
            to_dram(nc.gpsimd, h1_d, h1, tokens_out)
            pool.wait_ge(tokens_out, 8 * 16)
            from_dram(nc.gpsimd, rows_wide, rows_d, tokens_in)
            from_dram(nc.gpsimd, weight_wide[:, :, 0:TOPK], weight_d[:, 0:TOPK], tokens_in)
            from_dram(nc.gpsimd, h1_wide, h1_d, tokens_in)
            pool.wait_ge(tokens_in, 6 * 16)
            gather(0, got_h, hsd)
            scatter(hxs, mixed_h, WIDE_ROWS, lambda i, k: rows_wide[:, i, 2 * TOPK + k:2 * TOPK + k + 1], combined)
            gather(1, got_y, ysd)
            root(12, WIDE, P)

        @block.tensor
        def _(pe):
            def mm(dst, lhs, rhs, start=True, stop=True):
                return nc.tensor.matmul(dst, lhs, rhs, start=start, stop=stop)

            def projected(dst, w, x):
                mm(dst, w[0:HALF + 1, 0], x[0:HALF + 1, 0], stop=False)
                return mm(dst, w[0:HALF, 1], x[0:HALF, 1], start=False)

            def keep_warm(n, bank):
                for _ in range(n):
                    mm(ps[:, bank, 0:256], ident, cst[:, 0:256])

            def tokens():
                for k in range(6):
                    if k % 2 == 0:
                        pe.wait_ge(in_tok[k // 2], 32)
                    for m in range(2):
                        for c in range(2):
                            ins = mm(ps[0:HALF, 2 * m + c, 0:8 * (NT - 1)], token_w[:, k, HALF * m:HALF * (m + 1)],
                                     patches[:, k, 8 * (NT - 1) * c:8 * (NT - 1) * (c + 1)], k == 0, k == 5)
                            if k == 5:
                                ins.then_inc(tok_ps, 1)

            def turn_h0():
                pe.wait_ge(tok_xt, 5)
                pe.wait_ge(in_const, 16)
                for i in range(TILES):
                    for m in range(2):
                        ins = nc.tensor.transpose(
                            ps[0:TT, 4 + i // 2, D * (i % 2) + HALF * m:D * (i % 2) + HALF * (m + 1)],
                            xt[0][0:HALF, m, TT * i:TT * (i + 1)], ident[0:HALF, 0:HALF])
                    if i % 2:
                        ins.then_inc(h0_ps, 1)

            def turn_to_features(n, src, bank, need):
                for i in range(TILES) if n < 3 else (2, 3, 4, 5, 0, 1):
                    if n == 3 and i >= 2:
                        pe.wait_ge(refs_out, i - 1)
                    else:
                        if n == 3 and i == 0:
                            keep_warm(11, 5)
                        pe.wait_ge(ln_out, need + i + 1)
                    for m in range(2):
                        at = TT * (2 * m + i % 2)
                        ins = nc.tensor.transpose(ps[0:HALF, bank + i // 2, at:at + TT],
                                                  src[:, i, HALF * m:HALF * (m + 1)], ident[0:TT, 0:TT])
                    if i % 2:
                        ins.then_inc(turn_ps, 1)

            def routing_logits(c):
                if c == 0:
                    pe.wait_ge(q_sb, 8)
                else:
                    pe.wait_ge(e_sb, 1)
                projected(ps[0:TT, 3, 0:CH], attn_w[1][:, :, RW:RW + TT],
                          xt[1][:, :, CH * c:CH * (c + 1)]).then_inc(z_ps, 1)

            def mix():
                for i in range(TILES):
                    if i == 0:
                        pe.wait_ge(mixT_rdy, 1)
                    ins = projected(ps[0:TT, 3 + i // 2, D * (i % 2):D * (i % 2 + 1)], mixT[:, :, TT * i:TT * (i + 1)],
                                    attn_w[1][:, :, MIXW:MIXW + D])
                    if i % 2:
                        ins.then_inc(mix_ps, 1)

            def feed_forward():
                pe.wait_ge(in_ffn, 64)
                pe.wait_ge(xt_rdy, 6)
                for k in range(6):
                    for c in range(2):
                        q = 2 * k + c
                        if q >= 4:
                            pe.wait_ge(hid_sb, q - 3)
                        bank = 3 + q % 4
                        mm(ps[:, bank, 0:CH], w1[:, 0, P * k:P * (k + 1)], xt[2][0:HALF, 0, CH * c:CH * (c + 1)],
                           stop=False)
                        mm(ps[:, bank, 0:CH], w1[:, 1, P * k:P * (k + 1)], xt[2][0:HALF, 1, CH * c:CH * (c + 1)],
                           start=False).then_inc(hid_ps, 1)
                pe.wait_ge(hid_sb, 12)
                pe.wait_ge(pads_rdy, 1)
                for i in range(TILES):
                    dst = ps[0:TT, i // 2, D * (i % 2):D * (i % 2 + 1)]
                    mm(dst, ones[0:1, 0:TT], b2[:], stop=False)
                    for k in range(6):
                        ins = mm(dst, hid[:, k, TT * i:TT * (i + 1)], w2[:, k, :], False, k == 5)
                    if i % 2:
                        ins.then_inc(ffn_ps, 1)

            def attention(a):
                w, x = attn_w[a], xt[a]
                pe.wait_ge((in_w1, in_w2)[a], 32)
                for which in range(2):
                    if which == 1 and a == 0:
                        pe.wait_ge(h0_sb, 3)
                        pe.wait_ge(emb_sb, 1)
                    for m in range(2):
                        for c in range(2):
                            at = D * which + HALF * m
                            projected(ps[0:HALF, 4 * which + 2 * m + c, 0:CH], w[:, :, at:at + HALF],
                                      x[:, :, CH * c:CH * (c + 1)]).then_inc(qk_ps, 1)
                for i in range(TILES):
                    if i % 2 == 0:
                        pe.wait_ge(q_sb, 4 * a + i // 2 + 1)
                    ins = projected(ps[0:TT, i // 2, D * (i % 2):D * (i % 2 + 1)], x[:, :, TT * i:TT * (i + 1)],
                                    w[:, :, 2 * D:3 * D])
                    if i % 2:
                        ins.then_inc(v_ps, 1)
                if a == 1:
                    routing_logits(0)
                for b in range(NB):
                    if b % 2 == 0:
                        j = b // 2
                        pe.wait_ge(k_sb, 4 * a + min(j, 3) + 1)
                        pe.wait_ge(v_sb, 3 * a + (b + 1) // 3 // 2 + 1)
                        if j >= 4:
                            pe.wait_ge(vx_sb, 8 * a + j - 3)
                    s = TT * (b % 3)
                    ins = mm(ps[0:TT, 4 + b // 2 % 4, D * (b % 2):D * (b % 2 + 1)],
                             const("spread", TT)[:, s:s + TT], vtok[:, b // 3, :])
                    if b % 2:
                        ins.then_inc(vrep_ps, 1)

                if a == 1:
                    routing_logits(1)

                def scores(p):
                    n = PAIRS_OF_IMAGES * a + p
                    if p == 0:
                        pe.wait_ge(q_sb, 4 * a + 4)
                        pe.wait_ge(kx_sb, a + 1)
                        pe.wait_ge(v_sb, 3 * a + 3)
                    if p >= 2:
                        pe.wait_ge(score_used, n - 1)
                    for y in range(2):
                        b = 2 * p + y
                        for m in range(2):
                            ins = mm(ps[64 * y:64 * y + 64, p % 2, 222 * m:222 * (m + 1)], qt[:, m, NT * b:NT * b + 64],
                                     kx[:, m, :, NT * b:NT * (b + 1)])
                    ins.then_inc(score_ps, 1)

                def turn(p):
                    n = PAIRS_OF_IMAGES * a + p
                    pe.wait_ge(prob_sb, n + 1)
                    if n >= 2:
                        pe.wait_ge(probT_sb, n - 1)
                    if a == 1 and p == 0:
                        pe.wait_ge(e_sb, 2)
                    for g in range(GROUPS):
                        ins = nc.tensor.transpose(ps[0:TT, 2 + p % 2, P * g:P * (g + 1)],
                                                  probs[:, n % 3, TT * g:TT * (g + 1)], ident)
                    ins.then_inc(probT_ps, 1)

                def contexts(p):
                    n = PAIRS_OF_IMAGES * a + p
                    pe.wait_ge(probT_sb, n + 1)
                    if p == 0:
                        pe.wait_ge(vx_sb, 8 * a + 8)
                    for y in range(2):
                        b = 2 * p + y
                        for g in range(GROUPS):
                            ins = mm(ps[64 * (g % 2):64 * (g % 2) + GF, 4 + 2 * (g // 2) + b // 8,
                                        NT * (b % 8):NT * (b % 8 + 1)],
                                     vx[:, b, g, :], probsT[:, n % 2, P * g + 64 * y:P * g + 64 * y + NT])
                    ins.then_inc(ctx_ps, 1)

                for s in range(PAIRS_OF_IMAGES + 3):
                    if s < PAIRS_OF_IMAGES:
                        scores(s)
                    if s == PAIRS_OF_IMAGES:
                        pe.wait_ge(score_used, PAIRS_OF_IMAGES * (a + 1) - 1)
                        keep_warm(2, 0)
                    if 2 <= s < PAIRS_OF_IMAGES + 2:
                        turn(s - 2)
                    if s >= 3:
                        contexts(s - 3)
                for i in range(TILES):
                    if i == 0:
                        pe.wait_ge(score_used, PAIRS_OF_IMAGES * (a + 1))
                        pe.wait_ge(probT_sb, PAIRS_OF_IMAGES * (a + 1))
                        keep_warm(4, 3)
                        pe.wait_ge(ctx_sb, 4 * a + 4)
                    dst = ps[0:TT, i // 2, D * (i % 2):D * (i % 2 + 1)]
                    mm(dst, ctxT[:, 0, TT * i:TT * (i + 1)], attn_wo[a][:, 0, :], stop=False)
                    ins = mm(dst, ctxT[:, 1, TT * i:TT * (i + 1)], attn_wo[a][:, 1, :], start=False)
                    if i % 2:
                        ins.then_inc(att_ps, 1)

            def encoder():
                pe.wait_ge(in_diff, 64)
                x = xt[3]
                for c in range(2):
                    projected(ps[0:ENC1, c, 0:CH], diff_w[:, :, FC1:FC1 + ENC1], x[:, :, CH * c:CH * (c + 1)]).then_inc(enc1_ps, 1)
                pe.wait_ge(enc1_sb, 2)
                for i in range(TILES):
                    ins = mm(ps[0:TT, 2, ENC2 * i:ENC2 * (i + 1)], enc1[:, TT * i:TT * (i + 1)], enc_w2[:])
                ins.then_inc(enc2_ps, 1)
                for i in range(2, TILES):
                    ins = projected(ps[0:TT, i // 2 - 1, D * (i % 2):D * (i % 2 + 1)], x[:, :, TT * i:TT * (i + 1)],
                                    diff_w[:, :, KW:KW + D])
                    if i % 2:
                        ins.then_inc(k_ref_ps, 1)
                pe.wait_ge(code_rdy, 1)
                for i in range(2, TILES):
                    n = TT if i < TILES - 1 else LAST
                    ins = mm(ps[0:TT, 7, 0:ENC2], const("sametoken", n), code2[0:n, i, :], i == 2, i == TILES - 1)
                ins.then_inc(refsum_ps, 1)
                pe.wait_ge(k_ref_sb, 2)
                for h in range(2):
                    for i in range(4):
                        n = TT if i < 3 else LAST
                        k = ksb[0:n, i, HALF * h:HALF * (h + 1)]
                        ins = mm(ps[0:HALF, 3, HALF * h:HALF * (h + 1)], k, k, i == 0, i == 3)
                ins.then_inc(gram_ps, 1)

            def diffuser_step(s):
                for i in range(2):
                    n, b0 = 2 * s + i, 4 * i
                    if s == 0:
                        pe.wait_ge(gated, 1)
                    else:
                        pe.wait_ge(o_sb, n - 1)
                        keep_warm(5 - 3 * i, b0 + 1)
                        pe.wait_ge(ln_out, 4 * TILES + n - 1)
                    for m in range(2):
                        ins = nc.tensor.transpose(ps[0:HALF, b0, TT * m:TT * (m + 1)],
                                                  n1[:, i, HALF * m:HALF * (m + 1)], ident[0:TT, 0:TT])
                    ins.then_inc(xd_ps, 1)
                for i in range(2):
                    n, b0 = 2 * s + i, 4 * i
                    x = xd[:, :, TT * i:TT * (i + 1)]
                    if s == 0 and i == 0:
                        pe.wait_ge(gram_sb, 1)
                    if i == 0:
                        keep_warm(1, b0 + 1)
                    pe.wait_ge(xd_sb, n + 1)
                    projected(ps[0:TT, b0 + 1, 0:D], x, diff_w[:, :, QV:QV + D]).then_inc(qtok_ps, 1)
                    projected(ps[0:TT, b0 + 2, 0:D], x, diff_w[:, :, QV + D:QV + 2 * D]).then_inc(qv_ps, 1)
                    for m in range(2):
                        ins = projected(ps[0:HALF, b0 + 3, TT * m:TT * (m + 1)],
                                        diff_w[:, :, QV + HALF * m:QV + HALF * (m + 1)], x)
                    ins.then_inc(qd_ps, 1)
                for i in range(2):
                    n, b0 = 2 * s + i, 4 * i
                    pe.wait_ge(qtok_sb, n + 1)
                    pe.wait_ge(vmask_sb, n + 1)
                    for h in range(2):
                        mm(ps[0:HALF, b0 + h, 0:3 * HALF], qtok[:, i, HALF * h:HALF * (h + 1)],
                           vmask[:, i, :, HALF * h:HALF * (h + 1)]).then_inc(m_ps, 1)
                for i in range(2):
                    n, b0 = 2 * s + i, 4 * i
                    pe.wait_ge(qd_sb, n + 1)
                    for h in range(2):
                        pe.wait_ge(m_sb, 2 * n + h + 1)
                        mm(ps[0:HALF, b0 + 2 + h, 0:3 * HALF], gram[:, h, :],
                           mblock[:, h, 3 * i:3 * i + 3, :]).then_inc(gm_ps, 1)
                for i in range(2):
                    n, b0 = 2 * s + i, 4 * i
                    pe.wait_ge(gm_sb, 2 * n + 2)
                    for b in range(3):
                        for h in range(HEADS):
                            ins = mm(ps[0:DH, b0 + b, NT * h:NT * (h + 1)],
                                     gmask[:, h // 6, 3 * i + b, DH * (h % 6):DH * (h % 6 + 1)],
                                     qd[:, h // 6, NT * (3 * i + b):NT * (3 * i + b + 1)])
                    ins.then_inc(o_ps, 1)
                for i in range(2):
                    n, b0 = 2 * s + i, 4 * i
                    if i == 1:
                        keep_warm(1, 3 + b0)
                    pe.wait_ge(o_sb, n + 1)
                    for k in range(3):
                        ins = mm(ps[0:TT, b0 + 3, 0:D], od[:, k, TT * i:TT * (i + 1)], proj_w[:, k, :], k == 0, k == 2)
                    ins.then_inc(proj_ps, 1)

            def route():
                pe.wait_ge(xt_rdy, 12)
                pe.wait_ge(moe_buf, 1)
                for c in range(2):
                    projected(ps[:, c, 0:CH], diff_w[:, :, ROUTE:ROUTE + P], xt[4][:, :, CH * c:CH * (c + 1)]).then_inc(key_ps, 1)
                pe.wait_ge(key_sb, 2)
                pe.wait_ge(emb_sb, 2)
                for i in range(TILES):
                    ins = mm(ps[0:TT, 2 + i // 2, 2 * NN * (i % 2):2 * NN * (i % 2 + 1)], keyT[:, TT * i:TT * (i + 1)], emb_block[:])
                    if i % 2:
                        ins.then_inc(logit_ps, 1)
                rows_of = [TT if i < TILES - 1 else LAST for i in range(TILES)]
                keep_warm(8, 7)
                for r in range(2):
                    pe.wait_ge(chosen_rdy, r + 1)
                    for i, n in enumerate(rows_of):
                        ins = mm(ps[:, 5, r:r + 1], chosen[0:n, 2 * i + r, :], ones_bf[0:n, 0:1], i == 0, i == TILES - 1)
                    ins.then_inc(count_ps, 1)
                    for i, n in enumerate(rows_of):
                        at = 2 * NN * (i % 2) + NN * r
                        dst = ps[0:TT, 2 + i // 2, at:at + NN]
                        for e in range(i):
                            mm(dst, ones_bf[0:TT, :], chosen[:, 2 * e + r, :], e == 0, False)
                        ins = mm(dst, upto_bf[0:n, :], chosen[0:n, 2 * i + r, :], i == 0)
                        if i % 2:
                            ins.then_inc(rank_ps, 1)
                    pe.wait_ge(count_rdy, r + 1)
                    if r == 1:
                        pe.wait_ge(base_sb, 1)
                    mm(ps[0:TT, 0, NN * r:NN * (r + 1)], count_wide[:, r, :], const("before")).then_inc(base_ps, 1)
                pe.wait_ge(over_rdy, 2)
                mm(ps[:, 6, 0:4], const("before"), counts[:])
                for r in range(2):
                    ins = mm(ps[0:1, 7, NN * r:NN * (r + 1)], counts[:, r:r + 1], const("before"))
                ins.then_inc(first_ps, 1)
                pe.wait_ge(delta_rdy, 1)
                for r in range(2):
                    ins = mm(ps[0:TT, 1, NN * r:NN * (r + 1)], delta_wide[:, r, :], ident)
                ins.then_inc(base_ps, 1)
                pe.wait_ge(table_in, 1)
                mm(ps[0:1, 7, 2 * NN:2 * NN + 4 * EXTRA], ones[:, 0:1], table_f[:]).then_inc(table_ps, 1)

            def turn_pairs(st):
                if st == 0:
                    pe.wait_ge(out_rdy, 1)
                    keep_warm(7, 7)
                    pe.wait_ge(base_sb, 3)
                    pe.wait_ge(ranks_used, 1)
                for t in range(PTILES):
                    n = P if t < PTILES - 1 else PLAST
                    per, bank = (2, t // 2) if st == 0 else (4, t // 4)
                    if t % 6 == 0:
                        pe.wait_ge(rows_in[t // 6], 16 * st + 16)
                    if t % per == 0 and bank >= 4:
                        pe.wait_ge(turned_sb, (0, 10)[st] + bank - 3)
                    for m in range(2 - st):
                        at = 2 * P * (t % 2) + P * m if st == 0 else P * (t % 4)
                        w = HALF if st == 0 else R
                        ins = nc.tensor.transpose(ps[0:w, bank % 4, at:at + n], rows[0:n, t, w * m:w * (m + 1)], ident[0:n, 0:n])
                    if t % per == per - 1 or t == PTILES - 1:
                        ins.then_inc(turned_ps, 1)

            def neurons(st):
                pe.wait_ge(turned_sb, (10, 15)[st])
                width = (2 * R, D)[st]

                def quad(w, bank):
                    for c in range(QUAD):
                        dst = ps[64 * (c % 2):64 * (c % 2) + SLOT, bank, (R, D)[st] * (c // 2):(R, D)[st] * (c // 2 + 1)]
                        x = staged[:, QUAD * bank + c, :]
                        if st == 0:
                            mm(dst, x[0:HALF, 0:SLOT], w[0:HALF, width * c:width * c + R], stop=False)
                            ins = mm(dst, x[0:HALF, SLOT:2 * SLOT], w[0:HALF, width * c + R:width * (c + 1)], start=False)
                        else:
                            ins = mm(dst, x[:, 0:SLOT], w[:, width * c:width * (c + 1)])
                    ins.then_inc(product, 1)

                for j in range(AHEAD):
                    pe.wait_ge(staged_rdy, j + 1 + ALL * st)
                    if j >= BANKS:
                        pe.wait_ge(taken, j - BANKS + 1 + ALL * st)
                    done, loads = loaded(j)
                    pe.wait_ge(done, 16 * (1 if j < OWN else 3) + 16 * loads * st)
                    quad(rings[st][j], j % BANKS)
                with pe.Fori(1, TURNS + 1) as i:
                    for p, q in enumerate(TURN):
                        pe.wait_ge(staged_rdy, turns(i, p) + (1 + ALL * st))
                        pe.wait_ge(taken, turns(i, p) + (1 - BANKS + ALL * st))
                        if q in range(OWN):
                            pe.wait_ge(ring_in[q], 16 * i + (16 + 16 * (1 + TURNS) * st))
                            quad(rings[st][q], bank_of(p))
                        else:
                            e = "abc".index(q)
                            pe.wait_ge(extra_in[e], 16 * QUAD * i + 16 * QUAD * TURNS * st)
                            quad(extra[:, e], bank_of(p))

            tokens()
            pe.wait_ge(in_const, 16)
            pe.wait_ge(emb_rdy, 1)
            nc.tensor.transpose(ps[:, 7, 0:P], emb2[:].rearrange("p r e -> p (r e)"), ident).then_inc(embT_ps, 1)
            turn_h0()
            pe.wait_ge(ready, 1)
            attention(0)
            keep_warm(21, 7)
            turn_to_features(0, n1, 4, TILES)
            keep_warm(3, 7)
            pe.wait_ge(xt_rdy, 3)
            attention(1)
            mix()
            keep_warm(11, 7)
            turn_to_features(1, n1, 0, 2 * TILES)
            keep_warm(3, 7)
            feed_forward()
            keep_warm(10, 7)
            turn_to_features(2, h2, 4, 3 * TILES)
            keep_warm(2, 7)
            pe.wait_ge(xt_rdy, 9)
            encoder()
            for s in range(3):
                diffuser_step(s)
            turn_to_features(3, h1, 0, 4 * TILES + 6)
            keep_warm(2, 7)
            route()
            turn_pairs(0)
            pe.wait_ge(table_rdy, 1)
            keep_warm(6, 7)
            neurons(0)
            pe.wait_ge(taken, ALL)
            turn_pairs(1)
            keep_warm(6, 7)
            neurons(1)

        @block.scalar
        def _(act):
            def attention(a):
                for j in range(4):
                    act.wait_ge(qk_ps, 8 * a + j + 1)
                    m, c = j // 2, j % 2
                    nc.scalar.mul(qt[:, m, CH * c:CH * (c + 1)], ps[0:HALF, j, 0:CH], DH ** -0.5).then_inc(q_sb, 1)
                for j in range(3):
                    act.wait_ge(v_ps, 3 * a + j + 1)
                    nc.scalar.copy(vtok[:, 2 * j:2 * j + 2, :],
                                   ps[0:TT, j, 0:2 * D].rearrange("p (i d) -> p i d", i=2)).then_inc(v_sb, 1)
                if a == 1:
                    routing_logits(0)
                    routing_logits(1)
                for s in range(PAIRS_OF_IMAGES + 2):
                    if s < PAIRS_OF_IMAGES:
                        n = PAIRS_OF_IMAGES * a + s
                        act.wait_ge(score_used, n + 1)
                        nc.scalar.activation(shifted[:, n % 3, :], shifted[:, n % 3, :], ACT.Exp).then_inc(exped, 1)
                    if s >= 2:
                        n = PAIRS_OF_IMAGES * a + s - 2
                        act.wait_ge(probT_ps, n + 1)
                        if n >= 2:
                            act.wait_ge(ctx_ps, n - 1)
                        nc.scalar.copy(probsT[:, n % 2, :], ps[0:TT, 2 + n % 2, :]).then_inc(probT_sb, 1)
                for c in range(2):
                    act.wait_ge(ctx_ps, PAIRS_OF_IMAGES * a + 4 * (c + 1))
                    for m in range(2):
                        for g in range(2):
                            ins = nc.scalar.copy(ctxT[64 * g:64 * g + GF, m, CH * c:CH * (c + 1)],
                                                 ps[64 * g:64 * g + GF, 4 + 2 * m + c, 0:CH])
                        ins.then_inc(ctx_sb, 1)

            def to_features(n, dst, bank, gain=None, bias=None):
                for count, j in enumerate((0, 1, 2) if n < 3 else (1, 2, 0)):
                    act.wait_ge(turn_ps, 3 * n + count + 1)
                    src = ps[0:HALF, bank + j, 0:4 * TT].rearrange("p (m t) -> p m t", m=2)
                    to = dst[0:HALF, :, 2 * TT * j:2 * TT * (j + 1)]
                    if gain is None:
                        ins = nc.scalar.copy(to, src)
                    else:
                        for m in range(2):
                            ins = nc.scalar.activation(to[:, m], src[:, m], ACT.Identity,
                                                       scale=vec[:, gain + m:gain + m + 1],
                                                       bias=vec[:, bias + m:bias + m + 1])
                    ins.then_inc(xt_rdy, 1)

            def routing_logits(c):
                act.wait_ge(z_ps, c + 1)
                nc.scalar.copy(zb[:, CH * c:CH * (c + 1)], ps[0:TT, 3, 0:CH])
                nc.scalar.activation(sig[:, CH * c:CH * (c + 1)], ps[0:HALF, 3, 0:CH], ACT.Exp,
                                     scale=-1.0).then_inc(e_sb, 1)

            for j in range(3):
                act.wait_ge(h0_ps, j + 1)
                nc.scalar.copy(h0[:, 2 * j:2 * j + 2, :],
                               ps[0:TT, 4 + j, 0:2 * D].rearrange("p (i d) -> p i d", i=2)).then_inc(h0_sb, 1)
            act.wait_ge(ready, 1)
            attention(0)
            to_features(0, xt[1], 4, G1, B1)
            attention(1)
            to_features(1, xt[2], 0, G2, B2)
            for k in range(6):
                for c in range(2):
                    act.wait_ge(hid_ps, 2 * k + c + 1)
                    nc.scalar.activation(hid[:, k, CH * c:CH * (c + 1)], ps[:, 3 + (2 * k + c) % 4, 0:CH], ACT.Gelu,
                                         bias=b1[:, k:k + 1]).then_inc(hid_sb, 1)
            to_features(2, xt[3], 4)
            act.wait_ge(in_diff, 64)
            act.wait_ge(buf_rdy, 1)
            for c in range(2):
                act.wait_ge(enc1_ps, c + 1)
                nc.scalar.activation(enc1[0:ENC1, CH * c:CH * (c + 1)], ps[0:ENC1, c, 0:CH], ACT.Gelu,
                                     bias=vec[0:ENC1, FC1B:FC1B + 1]).then_inc(enc1_sb, 1)
            for j in range(2):
                act.wait_ge(k_ref_ps, j + 1)
                nc.scalar.copy(ksb[:, 2 * j:2 * j + 2, :],
                               ps[0:TT, j, 0:2 * D].rearrange("p (i d) -> p i d", i=2)).then_inc(k_ref_sb, 1)
            act.wait_ge(alike_rdy, 1)
            nc.scalar.activation(alike[:], alike[:], ACT.Tanh, scale=25.0 / (2 * REFS)).then_inc(tanh_rdy, 1)
            for s in range(3):
                for i in range(2):
                    n, b0 = 2 * s + i, 4 * i
                    act.wait_ge(xd_ps, n + 1)
                    src = ps[0:HALF, b0, 0:2 * TT].rearrange("p (m t) -> p m t", m=2)
                    to = xd[0:HALF, :, TT * i:TT * (i + 1)]
                    if s == 0:
                        ins = nc.scalar.copy(to, src)
                    else:
                        for m in range(2):
                            ins = nc.scalar.activation(to[:, m], src[:, m], ACT.Identity,
                                                       scale=vec[:, LNG + m:LNG + m + 1], bias=vec[:, LNB + m:LNB + m + 1])
                    ins.then_inc(xd_sb, 1)
                for i in range(2):
                    n, b0 = 2 * s + i, 4 * i
                    act.wait_ge(qtok_ps, n + 1)
                    nc.scalar.copy(qtok[:, i, :], ps[0:TT, b0 + 1, 0:D]).then_inc(qtok_sb, 1)
                    act.wait_ge(qd_ps, n + 1)
                    nc.scalar.copy(qd[:, :, TT * i:TT * (i + 1)],
                                   ps[0:HALF, b0 + 3, 0:2 * TT].rearrange("p (m t) -> p m t", m=2)).then_inc(qd_sb, 1)
                for i in range(2):
                    n, b0 = 2 * s + i, 4 * i
                    for h in range(2):
                        act.wait_ge(gm_ps, 2 * n + h + 1)
                        nc.scalar.copy(gmask[:, h, 3 * i:3 * i + 3, :],
                                       ps[0:HALF, b0 + 2 + h, 0:3 * HALF].rearrange("p (b f) -> p b f", b=3)).then_inc(gm_sb, 1)
                act.wait_ge(o_ps, 2 * s + 1)
                for j in range(HEADS):
                    ins = nc.scalar.copy(*folded(0, j))
                ins.then_inc(o_sb, 1)
            to_features(3, xt[4], 0)
            for c in range(2):
                act.wait_ge(key_ps, c + 1)
                nc.scalar.copy(keyT[:, CH * c:CH * (c + 1)], ps[:, c, 0:CH]).then_inc(key_sb, 1)
            for j in range(3):
                act.wait_ge(logit_ps, j + 1)
                nc.scalar.copy(logit[:, 4 * j:4 * j + 4, 0:NN],
                               ps[0:TT, 2 + j, :].rearrange("p (q n) -> p q n", n=NN)).then_inc(logit_sb, 1)
            for r in range(2):
                act.wait_ge(base_ps, r + 1)
                nc.scalar.copy(base[:, 0, r, :], ps[0:TT, 0, NN * r:NN * (r + 1)]).then_inc(base_sb, 1)
            act.wait_ge(base_ps, 3)
            nc.scalar.copy(base[:, 1].rearrange("p r n -> p (r n)"), ps[0:TT, 1, 0:2 * NN]).then_inc(base_sb, 1)
            act.wait_ge(shift_rdy, 1)
            nc.scalar.activation(expo[:], expo[:], ACT.Exp).then_inc(expo_rdy, 1)

            def turn_pairs(st):
                if st == 0:
                    act.wait_ge(moe_buf, 2)
                for n in range((10, 5)[st]):
                    act.wait_ge(turned_ps, (0, 10)[st] + n + 1)
                    if st == 0:
                        w = 2 * P if n < 9 else PLAST
                        to = xg[:, :, 2 * P * n:2 * P * n + w]
                        src = ps[0:HALF, n % 4, 0:4 * P].rearrange("p (t m c) -> p m t c", t=2, m=2)
                        if n < 9:
                            to = to.rearrange("p m (t c) -> p m t c", t=2)
                        else:
                            src = src[:, :, 0, 0:w]
                    else:
                        w = min(4 * P, PAIRS - 4 * P * n)
                        to, src = hg[:, 4 * P * n:4 * P * n + w], ps[:, n % 4, 0:w]
                    nc.scalar.copy(to, src).then_inc(turned_sb, 1)

            def neurons(st, d):
                w = (R, D)[st]

                def quad(count, bank, at):
                    act.wait_ge(product, count + (1 + ALL * st))
                    nc.scalar.copy(products[:, bank, 0:2 * w], ps[:, bank, 0:2 * w]).then_inc(taken, 1)
                    act.wait_ge(taken, count + (1 + ALL * st))
                    nc.scalar.dma_start(d[bass.ds(at * (QUAD * SLOT), QUAD * SLOT), :].rearrange("(q p) f -> p q f", p=P),
                                        products[:, bank, 0:2 * w].rearrange("p (q f) -> p q f", q=2)).then_inc(
                                            stored_rows[bank], 16)

                for j in range(AHEAD):
                    if j >= BANKS or st == 1:
                        act.wait_ge(stored_rows[j % BANKS], 16 * (j // BANKS + STORES[j % BANKS] * st))
                    quad(j, j % BANKS, j)
                with act.Fori(1, TURNS + 1) as i:
                    for p, q in enumerate(TURN):
                        uses = (AHEAD - len(TURN) + p) // BANKS + STORES[bank_of(p)] * st
                        act.wait_ge(stored_rows[bank_of(p)], 16 * (len(TURN) // BANKS) * i + 16 * uses)
                        quad(turns(i, p), bank_of(p), which(i, q))

            turn_pairs(0)
            neurons(0, hsd)
            turn_pairs(1)
            neurons(1, ysd)

        @block.vector
        def _(dve):
            steps = [0]

            def link(ins):
                steps[0] += 1
                ins.then_inc(dve_chain, 1)
                dve.wait_ge(dve_chain, steps[0])

            def embed():
                dve.wait_ge(in_vec, 16)
                pos = vec[:, POS:POS + 2 * NT].rearrange("p (m t) -> p m t", m=2)
                for m in range(2):
                    nc.vector.tensor_scalar(posb[:, m, 1:NT], pos[:, m, 1:NT], vec[:, TOKB + m:TOKB + m + 1], None, ALU.add)
                    ins = nc.vector.tensor_scalar(posb[:, m, 0:1], pos[:, m, 0:1], vec[:, CLS + m:CLS + m + 1], None,
                                                  ALU.add)
                link(ins)
                dve.wait_ge(ready, 1)
                xv = xt[0][0:HALF, :, 0:T].rearrange("p m (b t) -> p m b t", b=NB)
                for m in range(2):
                    ins = nc.vector.tensor_copy(xv[:, m, :, 0:1], posb[:, m, 0:1].unsqueeze(1).to_broadcast([HALF, NB, 1]))
                ins.then_inc(tok_xt, 1)
                for m in range(2):
                    for c in range(2):
                        dve.wait_ge(tok_ps, 2 * m + c + 1)
                        nc.vector.tensor_tensor(
                            xv[:, m, 8 * c:8 * c + 8, 1:NT],
                            ps[0:HALF, 2 * m + c, 0:8 * (NT - 1)].rearrange("p (b t) -> p b t", b=8),
                            posb[:, m, 1:NT].unsqueeze(1).to_broadcast([HALF, 8, NT - 1]), ALU.add).then_inc(tok_xt, 1)

            def attention(a):
                for j in range(4):
                    dve.wait_ge(qk_ps, 8 * a + 5 + j)
                    m, c = j // 2, j % 2
                    nc.vector.tensor_copy(kt[:, m, CH * c:CH * (c + 1)], ps[0:HALF, 4 + j, 0:CH]).then_inc(k_sb, 1)
                dve.wait_ge(k_sb, 4 * a + 4)
                for h in range(6):
                    ins = nc.vector.tensor_scalar(kx[:, :, h, :], kt[:], const("headof", HALF)[:, h:h + 1], None, ALU.mult)
                ins.then_inc(kx_sb, 1)
                for j in range(NB // 2):
                    dve.wait_ge(vrep_ps, 8 * a + j + 1)
                    nc.vector.tensor_tensor(
                        vx[:, 2 * j:2 * j + 2, :, :].rearrange("p b g f -> p (b g) f"),
                        ps[0:TT, 4 + j % 4, 0:2 * D].rearrange("p (x f) -> p x f", f=GF),
                        const("vmask", TT).unsqueeze(1).to_broadcast([TT, 2 * GROUPS, GF]), ALU.mult).then_inc(vx_sb, 1)

                def top(p):
                    n = PAIRS_OF_IMAGES * a + p
                    dve.wait_ge(score_ps, n + 1)
                    s = ps[:, p % 2, 0:HEADS * NT].rearrange("p (h k) -> p h k", h=HEADS)
                    if n >= 3:
                        dve.wait_ge(prob_sb, n - 2)
                    link(nc.vector.tensor_reduce(smax[:, n % 3, :], s, AX, ALU.max))
                    nc.vector.tensor_tensor(
                        shifted[:, n % 3, :].rearrange("p (h k) -> p h k", h=HEADS), s,
                        smax[:, n % 3, :].unsqueeze(2).to_broadcast([P, HEADS, NT]), ALU.subtract).then_inc(score_used, 1)

                def total(p):
                    n = PAIRS_OF_IMAGES * a + p
                    dve.wait_ge(exped, n + 1)
                    link(nc.vector.tensor_reduce(ssum[:, n % 3, :], shifted[:, n % 3, :].rearrange("p (h k) -> p h k", h=HEADS),
                                                 AX, ALU.add))
                    nc.vector.reciprocal(sinv[:, n % 3, :], ssum[:, n % 3, :]).then_inc(inv_rdy, 1)

                for s in range(PAIRS_OF_IMAGES + 1):
                    if s < PAIRS_OF_IMAGES:
                        top(s)
                    if s >= 1:
                        total(s - 1)
                    if a == 1 and s == 2:
                        sigmoid()
                    if a == 1 and s == 4:
                        pool_inputs()

            def sigmoid():
                dve.wait_ge(e_sb, 2)
                link(nc.vector.tensor_scalar(sig[:], sig[:], 1.0, None, ALU.add))
                nc.vector.reciprocal(sig[:], sig[:]).then_inc(sig_rdy, 1)

            def pool_inputs():
                link(nc.vector.tensor_reduce(sigsum[:], sig[:].rearrange("p (b t) -> p b t", b=NB), AX, ALU.add))
                link(nc.vector.tensor_scalar(sigsum[:], sigsum[:], 1e-6, None, ALU.add))
                nc.vector.reciprocal(sigsum[:], sigsum[:])
                dve.wait_ge(weighed_rdy, 1)
                link(nc.vector.tensor_reduce(pooled[:], weighed[:].rearrange("p m (b t) -> p m b t", b=NB), AX, ALU.add))
                nc.vector.tensor_tensor(pooled[:], pooled[:], sigsum[:].unsqueeze(1).to_broadcast([HALF, 2, NB]),
                                        ALU.mult).then_inc(pooled_rdy, 1)

            def ranks():
                for i in range(TILES):
                    ins = nc.vector.tensor_tensor_reduce(scratch[:, i, 0:TT], zb[:, TT * i:TT * (i + 1)], ident[0:TT, 0:TT], 1.0,
                                                   0.0, ALU.mult, ALU.add, zcol[:, i:i + 1])
                link(ins)
                for i in range(TILES):
                    if i == 4:
                        link(ins)
                    for n, (op, mask) in enumerate(((ALU.is_lt, "same"), (ALU.is_equal, "earlier"))):
                        ins = nc.vector.scalar_tensor_tensor(
                            out=scratch[:, (2 * i + n) % 8, 0:TT], in0=zb[:, TT * i:TT * (i + 1)], scalar=zcol[:, i:i + 1],
                            in1=const(mask, TT), op0=op, op1=ALU.mult, accum_out=below[:, n, i:i + 1])
                link(ins)
                link(nc.vector.tensor_tensor(takes[:, 0], below[:, 0], below[:, 1], ALU.add))
                link(nc.vector.tensor_scalar(takes[:, 0], takes[:, 0], ROUTED - 0.5, None, ALU.is_lt))
                link(nc.vector.tensor_scalar(takes[:, 1], takes[:, 0], -1.0, 1.0, ALU.mult, ALU.add))

            def merge():
                for i in range(TILES):
                    if i % 2 == 0:
                        dve.wait_ge(att_ps, 3 + i // 2 + 1)
                    ins = nc.vector.scalar_tensor_tensor(
                        out=hp[:, i, :], in0=ps[0:TT, i // 2, D * (i % 2):D * (i % 2 + 1)], scalar=takes[:, 0, i:i + 1],
                        in1=h1[:, i, :], op0=ALU.mult, op1=ALU.add)
                link(ins)
                for i in range(TILES):
                    if i % 2 == 0:
                        dve.wait_ge(mix_ps, i // 2 + 1)
                    nc.vector.scalar_tensor_tensor(
                        out=hp[:, i, :], in0=ps[0:TT, 3 + i // 2, D * (i % 2):D * (i % 2 + 1)], scalar=takes[:, 1, i:i + 1],
                        in1=hp[:, i, :], op0=ALU.mult, op1=ALU.add).then_inc(merged, 1)
                    if i % 2:
                        dve.wait_ge(merged, i + 1)
                        for t in range(i - 1, i + 1):
                            ins = nc.vector.bn_stats(stats[0:TT, t, :], hp[:, t, :])
                link(ins)

            def add_tokens(ready_at, base, bank, to, res):
                for j in range(3):
                    dve.wait_ge(ready_at, base + j + 1)
                    link(nc.vector.tensor_tensor(to[:, 2 * j:2 * j + 2, :],
                                                 ps[0:TT, bank + j, 0:2 * D].rearrange("p (i d) -> p i d", i=2),
                                                 res[:, 2 * j:2 * j + 2, :], ALU.add))
                    for i in range(2 * j, 2 * j + 2):
                        ins = nc.vector.bn_stats(stats[0:TT, i, :], to[:, i, :])
                link(ins)

            def layer_norm(n, dst, src=zln, tiles=TILES, counted=False, rows=TT):
                src = src if src is not None else ps[0:TT, 6, 0:2 * D].rearrange("p (i d) -> p i d", i=2)
                if not counted:
                    for i in range(tiles):
                        ins = nc.vector.bn_stats(stats[0:TT, i, :], src[:, i, :])
                    link(ins)
                for i in range(tiles):
                    ins = nc.vector.bn_aggr(mv[0:rows, i, :], stats[0:rows, i, :])
                link(ins)
                nc.vector.tensor_scalar(rstd[0:rows, 0:tiles], mv[0:rows, 0:tiles, 1], EPS, None, ALU.add).then_inc(var_rdy, 1)
                dve.wait_ge(rstd_rdy, n + 1)
                for i in range(tiles):
                    nc.vector.tensor_scalar(dst[:, i, :], src[:, i, :], mv[0:rows, i, 0:1], rstd[0:rows, i:i + 1], ALU.subtract,
                                            ALU.mult).then_inc(ln_out, 1)

            def embedding_norms():
                dve.wait_ge(in_emb, 16)
                link(nc.vector.tensor_tensor(emb2[:], emb[:], emb[:], ALU.mult))
                nc.vector.tensor_reduce(emb_n[:], emb2[:], AX, ALU.add).then_inc(emb2_rdy, 1)
                dve.wait_ge(emb_root, 1)
                link(nc.vector.tensor_scalar(emb_n[:], emb_n[:], 1e-8, None, ALU.add))
                link(nc.vector.reciprocal(emb_n[:], emb_n[:]))
                nc.vector.tensor_tensor(emb2[:], emb[:], emb_n[:].unsqueeze(2).to_broadcast([P, 2, 64]),
                                        ALU.mult).then_inc(emb_rdy, 1)

            def choose(r):
                for j in range(3):
                    if r == 0:
                        dve.wait_ge(logit_sb, j + 1)
                    for q in (4 * j + r, 4 * j + 2 + r):
                        ins = nc.vector.max(top8[:, q, :], logit[:, q, 0:NN])
                link(ins)
                link(nc.vector.memset(top8[:, r::2, TOPK:8], SENTINEL))
                for q in range(r, 2 * TILES, 2):
                    ins = nc.vector.match_replace(kept[:, q, :], top8[:, q, :], logit[:, q, :], -SENTINEL)
                link(ins)
                nc.vector.tensor_tensor(chosen[:, r::2, :], logit[:, r::2, 0:NN], kept[:, r::2, 0:NN],
                                        ALU.not_equal).then_inc(chosen_rdy, 1)

            def shift():
                nc.vector.tensor_tensor(expo[:], logit[:, :, 0:NN], top8[:, :, 0:1].to_broadcast([TT, 2 * TILES, NN]),
                                        ALU.subtract).then_inc(shift_rdy, 1)

            def count(r):
                dve.wait_ge(count_ps, r + 1)
                link(nc.vector.tensor_copy(counts[:, r:r + 1], ps[:, 5, r:r + 1]))
                nc.vector.tensor_copy(count_wide[:, r, :], counts[:, r:r + 1].to_broadcast([P, TT])).then_inc(count_rdy, 1)
                link(nc.vector.tensor_scalar(over[:, r, :], const("steps64"), counts[:, r:r + 1], None, ALU.is_lt))
                nc.vector.tensor_reduce(counts[:, 2 + r:3 + r], over[:, r, :], AX, ALU.add).then_inc(over_rdy, 1)

            def further_slots():
                dve.wait_ge(over_rdy, 2)
                dve.wait_ge(first_ps, 1)
                link(nc.vector.tensor_copy(first[:], ps[:, 6, 0:4]))
                link(nc.vector.tensor_tensor(reach[:], first[:, 2:4], counts[:, 2:4], ALU.add))
                link(nc.vector.tensor_scalar(delta[:], first[:, 2:4], float(SLOT), const("delta"), ALU.mult, ALU.add))
                nc.vector.tensor_copy(delta_wide[:], delta[:].unsqueeze(2).to_broadcast([P, 2, TT])).then_inc(delta_rdy, 1)
                link(nc.vector.scalar_tensor_tensor(out=first[:, 0:2], in0=first[:, 2:4], scalar=-float(SLOT),
                                                    in1=first[:, 0:2], op0=ALU.mult, op1=ALU.add))
                for r in range(2):
                    nc.vector.tensor_scalar(owns[:, 0], const("slots"), first[:, 2 + r:3 + r], None, ALU.is_ge)
                    link(nc.vector.tensor_scalar(owns[:, 1], const("slots"), reach[:, r:r + 1], None, ALU.is_lt))
                    link(nc.vector.tensor_tensor(owns[:, 2], owns[:, 0], owns[:, 1], ALU.mult))
                    nc.vector.scalar_tensor_tensor(out=table_f[:, r, 0, :], in0=const("slots64"), scalar=first[:, r:r + 1],
                                                   in1=owns[:, 2], op0=ALU.add, op1=ALU.mult)
                    ins = nc.vector.tensor_scalar(table_f[:, r, 1, :], owns[:, 2], const("neuron"), None, ALU.mult)
                    if r == 0:
                        link(ins)
                ins.then_inc(table_in, 1)
                dve.wait_ge(table_ps, 1)
                for r in range(2):
                    nc.vector.tensor_copy(table[:, r, 0:NN], ps[0:1, 7, NN * r:NN * (r + 1)])
                    at = 2 * NN + 2 * EXTRA * r
                    nc.vector.tensor_copy(table[:, r, NN:NN + EXTRA], ps[0:1, 7, at:at + EXTRA])
                    ins = nc.vector.tensor_copy(table[:, r, NN + EXTRA:], ps[0:1, 7, at + EXTRA:at + 2 * EXTRA])
                ins.then_inc(table_rdy, 1)

            def ranks_of(j, r):
                return ps[0:TT, 2 + j, :].rearrange("p (i r n) -> p i r n", i=2, r=2)[:, :, r, :]

            def rows_in_order(r):
                dve.wait_ge(base_sb, r + 1)
                dve.wait_ge(rank_ps, 3 * r + 3)
                for j in range(3):
                    ins = nc.vector.tensor_tensor(place[:, 4 * j + r:4 * j + 4:2, :], ranks_of(j, r),
                                                  base[:, 0, r:r + 1, :].to_broadcast([TT, 2, NN]), ALU.add)
                link(ins)
                link(nc.vector.tensor_tensor(place[:, r::2, :], place[:, r::2, :], chosen[:, r::2, :], ALU.mult))
                for i in range(TILES):
                    ins = nc.vector.max(slot8[:, 2 * i + r, :], place[:, 2 * i + r, :])
                link(ins)
                nc.vector.tensor_scalar(row_in[:, r::2, :], slot8[:, r::2, 0:TOPK], -1.0, None, ALU.add).then_inc(in_rdy, 1)

            def rows_of_products():
                dve.wait_ge(base_sb, 3)
                for r in range(2):
                    for j in range(3):
                        ins = nc.vector.scalar_tensor_tensor(
                            out=place_out[:, 4 * j + r:4 * j + 4:2, :], in0=ranks_of(j, r), scalar=SLOT + 0.5,
                            in1=base[:, 1, r:r + 1, :].to_broadcast([TT, 2, NN]), op0=ALU.is_gt, op1=ALU.mult)
                link(ins)
                for r in range(2):
                    for j in range(3):
                        ins = nc.vector.tensor_tensor(place_out[:, 4 * j + r:4 * j + 4:2, :], ranks_of(j, r),
                                                      place_out[:, 4 * j + r:4 * j + 4:2, :], ALU.add)
                ins.then_inc(ranks_used, 1)
                dve.wait_ge(ranks_used, 1)
                link(nc.vector.tensor_tensor(place_out[:], place_out[:],
                                             const("rows64", TT).unsqueeze(1).to_broadcast([TT, 2 * TILES, NN]), ALU.add))
                link(nc.vector.tensor_tensor(place_out[:], place_out[:], chosen, ALU.mult))
                for q in range(2 * TILES):
                    ins = nc.vector.max(slot8[:, q, :], place_out[:, q, :])
                link(ins)
                nc.vector.tensor_scalar(row_out[:], slot8[:, :, 0:TOPK], -1.0, None, ALU.add).then_inc(out_rdy, 1)

            def weights(q):
                for k in range(TOPK):
                    ins = nc.vector.scalar_tensor_tensor(
                        out=scratch[:, TOPK * (q // 2 % 2) + k, 0:NN], in0=place_out[:, q, :], scalar=slot8[:, q, k:k + 1],
                        in1=expo[:, q, :], op0=ALU.is_equal, op1=ALU.mult, accum_out=weight[:, q, k:k + 1])
                if q // 2 % 2:
                    link(ins)

            def weights_whole(r):
                w, total = weight[:, r::2, :], esum[:, r::2]
                wide = total.unsqueeze(2).to_broadcast([TT, TILES, TOPK])
                link(nc.vector.tensor_tensor(w, w, wide, ALU.mult))
                link(nc.vector.tensor_reduce(total, w, AX, ALU.add))
                link(nc.vector.tensor_scalar(total, total, 1e-8, None, ALU.add))
                link(nc.vector.reciprocal(total, total))
                nc.vector.tensor_tensor(w, w, wide, ALU.mult).then_inc(weight_rdy, 1)

            offs = [dve.alloc_register(f"dve_first{j}") for j in range(8)]

            def neurons(st):
                dve.wait_ge(turned_sb, (10, 15)[st])
                dve.wait_ge(moe_buf, 2)

                def quad(o, bank):
                    for c in range(QUAD):
                        at = dve.snap(o[c], min_val=0, max_val=PAIRS)
                        x = staged[:, QUAD * bank + c, :]
                        if st == 0:
                            ins = nc.vector.tensor_copy(x[0:HALF].rearrange("p (m s) -> p m s", m=2), xg[:, :, bass.ds(at, SLOT)])
                        else:
                            ins = nc.vector.tensor_copy(x[:, 0:SLOT], hg[:, bass.ds(at, SLOT)])
                    ins.then_inc(staged_rdy, 1)

                for j in range(AHEAD):
                    o = offs[4 * (j % 2):4 * (j % 2) + 4]
                    dve.load(o, table[0:1, st, QUAD * j:QUAD * (j + 1)])
                    if j >= BANKS:
                        dve.wait_ge(product, j - BANKS + 1 + ALL * st)
                    quad(o, j % BANKS)
                with dve.Fori(1, TURNS + 1) as i:
                    for p, q in enumerate(TURN):
                        o = offs[4 * (p % 2):4 * (p % 2) + 4]
                        dve.load(o, table[0:1, st, bass.ds(which(i, q) * QUAD, QUAD)])
                        dve.wait_ge(product, turns(i, p) + (1 - BANKS + ALL * st))
                        quad(o, bank_of(p))

            def combine(st, got, dst, base):
                dve.wait_ge(tokens_in, 6 * 16)
                if st == 1:
                    dve.wait_ge(in_weights, 2 * 16)
                for i, n in enumerate(WIDE_ROWS):
                    dve.wait_ge(gathered[i], 16 * TOPK * (st + 1))
                    for k in range(TOPK):
                        w = weight_wide[0:n, i, TOPK * st + k:TOPK * st + k + 1]
                        if k == 0 and base is None:
                            ins = nc.vector.tensor_scalar(dst[0:n, i, :], got[0:n, i, k, :], w, None, ALU.mult)
                        else:
                            ins = nc.vector.scalar_tensor_tensor(
                                out=dst[0:n, i, :], in0=got[0:n, i, k, :], scalar=w,
                                in1=base[0:n, i, :] if k == 0 else dst[0:n, i, :], op0=ALU.mult, op1=ALU.add)
                        if st == 0 and k == TOPK - 1:
                            ins.then_inc(combined, 1)
                        else:
                            link(ins)
                    if st == 1:
                        link(nc.vector.bn_stats(stats[:, i, :], dst[:, i, :]))

            dve.wait_ge(in_const, 16)
            embedding_norms()
            embed()
            dve.wait_ge(embT_ps, 1)
            nc.vector.tensor_copy(emb2[:].rearrange("p r e -> p (r e)"), ps[:, 7, 0:P]).then_inc(emb_sb, 1)
            attention(0)
            add_tokens(att_ps, 0, 0, zln, h0)
            layer_norm(0, h1, counted=True)
            dve.wait_ge(ln_out, TILES)
            layer_norm(1, n1, h1)
            attention(1)
            ranks()
            merge()
            layer_norm(2, n1, hp, counted=True)
            dve.wait_ge(hs_rdy, 1)
            add_tokens(ffn_ps, 0, 0, zln, hs)
            layer_norm(3, h2, counted=True)
            dve.wait_ge(enc2_ps, 1)
            link(nc.vector.tensor_copy(code[:], ps[0:TT, 2, 0:TILES * ENC2].rearrange("p (i e) -> p i e", i=TILES)))
            link(nc.vector.tensor_tensor(code2[:], code[:], code[:], ALU.mult))
            link(nc.vector.tensor_reduce(norm2[:], code2[:], AX, ALU.add))
            nc.vector.tensor_scalar(norm2[:], norm2[:], 1e-16, None, ALU.max).then_inc(norm_rdy, 1)
            dve.wait_ge(inorm_rdy, 1)
            nc.vector.tensor_tensor(code2[:], code[:], norm2[:].unsqueeze(2).to_broadcast([TT, TILES, ENC2]),
                                    ALU.mult).then_inc(code_rdy, 1)
            dve.wait_ge(refsum_ps, 1)
            dve.wait_ge(code_rdy, 1)
            link(nc.vector.tensor_tensor(code[:, 0:2], code2[:, 0:2],
                                         ps[0:TT, 7, 0:ENC2].unsqueeze(1).to_broadcast([TT, 2, ENC2]), ALU.mult))
            nc.vector.tensor_reduce(alike[:], code[:, 0:2], AX, ALU.add).then_inc(alike_rdy, 1)
            dve.wait_ge(gram_ps, 1)
            nc.vector.scalar_tensor_tensor(
                out=gram[:], in0=ps[0:HALF, 3, 0:2 * HALF].rearrange("p (h f) -> p h f", h=2), scalar=1.0 / (DH * REFS),
                in1=const("headblock", HALF).unsqueeze(1).to_broadcast([HALF, 2, HALF]), op0=ALU.mult,
                op1=ALU.mult).then_inc(gram_sb, 1)
            dve.wait_ge(tanh_rdy, 1)
            nc.vector.tensor_scalar(gate[:, 0], alike[:], 0.5, 0.5, ALU.mult, ALU.add)
            link(nc.vector.tensor_scalar(gate[:, 1], alike[:], -0.5, 0.5, ALU.mult, ALU.add))
            dve.wait_ge(ln_out, 4 * TILES)
            for i in range(2):
                ins = nc.vector.tensor_scalar(n1[:, i, :], h2[:, i, :], gate[:, 0, i:i + 1], None, ALU.mult)
            ins.then_inc(gated, 1)
            for i in range(2):
                nc.vector.scalar_tensor_tensor(out=hs[:, i, :], in0=h2[:, i, :], scalar=gate[:, 1, i:i + 1],
                                               in1=h2[:, i, :], op0=ALU.mult, op1=ALU.add)
            link(nc.vector.tensor_scalar(zln[:, 2:TILES, :], h2[:, 2:TILES, :], 2.0, None, ALU.mult))
            for s in range(3):
                for i in range(2):
                    dve.wait_ge(qv_ps, 2 * s + i + 1)
                    nc.vector.tensor_tensor(
                        vmask[:, i], ps[0:TT, 4 * i + 2, 0:D].unsqueeze(1).to_broadcast([TT, 3, D]),
                        const("imageof", TT).unsqueeze(2).to_broadcast([TT, 3, D]), ALU.mult).then_inc(vmask_sb, 1)
                for i in range(2):
                    for h in range(2):
                        dve.wait_ge(m_ps, 4 * s + 2 * i + h + 1)
                        nc.vector.tensor_tensor(
                            mblock[:, h, 3 * i:3 * i + 3, :],
                            ps[0:HALF, 4 * i + h, 0:3 * HALF].rearrange("p (b f) -> p b f", b=3),
                            const("headblock", HALF).unsqueeze(1).to_broadcast([HALF, 3, HALF]), ALU.mult).then_inc(m_sb, 1)
                if s == 0:
                    for i in range(2, TILES):
                        ins = nc.vector.bn_stats(stats[0:TT, i, :], zln[:, i, :])
                    link(ins)
                    for i in range(2, TILES):
                        ins = nc.vector.bn_aggr(mv[0:TT, i, :], stats[0:TT, i, :])
                    link(ins)
                    nc.vector.tensor_scalar(rstd[0:TT, 2:TILES], mv[0:TT, 2:TILES, 1], EPS, None, ALU.add).then_inc(var_rdy, 1)
                if s == 1:
                    dve.wait_ge(rstd_rdy, 4 + 1)
                    for i in range(2, TILES):
                        nc.vector.tensor_scalar(h1[:, i, :], zln[:, i, :], mv[0:TT, i, 0:1], rstd[0:TT, i:i + 1], ALU.subtract,
                                                ALU.mult).then_inc(refs_out, 1)
                dve.wait_ge(o_sb, 2 * s + 1)
                dve.wait_ge(o_ps, 2 * s + 2)
                for j in range(HEADS):
                    ins = nc.vector.tensor_copy(*folded(1, j))
                ins.then_inc(o_sb, 1)
                for i in range(2):
                    n = 2 * s + i
                    dve.wait_ge(proj_ps, n + 1)
                    x = ps[0:TT, 4 * i + 3, 0:D]
                    link(nc.vector.bn_stats(stats[0:TT, i, :], x))
                    link(nc.vector.bn_aggr(mv[0:TT, i, :], stats[0:TT, i, :]))
                    nc.vector.tensor_scalar(rstd[0:TT, i:i + 1], mv[0:TT, i, 1:2], EPS, None, ALU.add).then_inc(var_rdy, 1)
                for i in range(2):
                    n = 2 * s + i
                    dve.wait_ge(rstd_rdy, 5 + n + 1)
                    nc.vector.tensor_scalar(n1[:, i, :], ps[0:TT, 4 * i + 3, 0:D], mv[0:TT, i, 0:1], rstd[0:TT, i:i + 1],
                                            ALU.subtract, ALU.mult).then_inc(ln_out, 1)
            dve.wait_ge(ln_out, 4 * TILES + 6)
            link(nc.vector.tensor_tensor(n1[:, 0:2], n1[:, 0:2], diff_ln[:, 0:1, :].to_broadcast([TT, 2, D]), ALU.mult))
            link(nc.vector.tensor_tensor(n1[:, 0:2], n1[:, 0:2], diff_ln[:, 1:2, :].to_broadcast([TT, 2, D]), ALU.add))
            for i in range(2):
                ins = nc.vector.scalar_tensor_tensor(out=zln[:, i, :], in0=n1[:, i, :], scalar=gate[:, 0, i:i + 1],
                                                     in1=hs[:, i, :], op0=ALU.mult, op1=ALU.add)
            link(ins)
            layer_norm(11, h1, tiles=2)
            dve.wait_ge(moe_buf, 1)
            for r in range(2):
                ins = nc.vector.tensor_copy(emb_block[64 * r:64 * (r + 1), NN * r:NN * (r + 1)],
                                            emb2[64 * r:64 * (r + 1)].rearrange("p r e -> p (r e)"))
            ins.then_inc(emb_sb, 1)
            for r in range(2):
                choose(r)
                count(r)
                if r == 1:
                    shift()
                    further_slots()
                rows_in_order(r)
            rows_of_products()
            dve.wait_ge(expo_rdy, 1)
            link(nc.vector.tensor_reduce(esum[:], expo[:], AX, ALU.add))
            link(nc.vector.reciprocal(esum[:], esum[:]))
            for q in range(0, 2 * TILES, 2):
                weights(q)
            weights_whole(0)
            neurons(0)
            for q in range(1, 2 * TILES, 2):
                weights(q)
            weights_whole(1)
            dve.wait_ge(weight_rdy, 2)
            nc.vector.memset(z_wide[64:P, WIDE - 1, :], 0.0).then_inc(zero_rdy, 1)
            dve.wait_ge(zero_rdy, 1)
            combine(0, got_h, mixed_h, None)
            neurons(1)
            combine(1, got_y, z_wide, h1_wide)
            layer_norm(12, out_wide, z_wide, WIDE, True, P)


def kernel(**inputs):
    import numpy as np
    import concourse.bacc as bacc
    from concourse import mybir
    from concourse.bass_utils import run_bass_kernel_spmd

    a = {k: np.asarray(v) for k, v in inputs.items()}
    f32 = np.float32

    def halves(w, bias=None, width=None):
        out = np.zeros((HALF + 1, 2, w.shape[1]), f32)
        out[:HALF] = w.reshape(2, HALF, -1).transpose(1, 0, 2)
        if bias is not None:
            out[HALF, 0] = bias
        return out

    def context_rows(w, bias):
        out = np.zeros((P, 2, D), f32)
        for g in range(GROUPS):
            out[64 * (g % 2):64 * (g % 2) + GF, g // 2] = w[GF * g:GF * (g + 1)]
        out[GF, 0] = bias
        return out

    def columns(v):
        return v.reshape(2, HALF).T

    pos = a["L0_tok_pos_embedding"][0].T.reshape(2, HALF, NT).transpose(1, 0, 2).reshape(HALF, 2 * NT)
    fc1_b = np.zeros((HALF, 1), f32)
    fc1_b[:ENC1, 0] = a["L1_attn_fc1_b"]
    vectors = np.concatenate(
        [columns(a["L0_ffn_g1"]), columns(a["L0_ffn_b1"]), columns(a["L0_ffn_g2"]), columns(a["L0_ffn_b2"]),
         columns(a["L1_attn_ln_g"]), columns(a["L1_attn_ln_b"]), columns(a["L0_tok_proj_b"]),
         columns(a["L0_tok_cls_token"][0, 0]), pos, fc1_b], axis=1)
    proj = np.zeros((P, 3, D), f32)
    for j in range(HEADS):
        proj[32 * (j % 4):32 * (j % 4) + DH, j // 4] = a["L1_attn_proj_w"][DH * j:DH * (j + 1)]
    proj[DH, 0] = a["L1_attn_proj_b"]
    fc2 = np.zeros((65, ENC2), f32)
    fc2[:ENC1] = a["L1_attn_fc2_w"]
    fc2[64] = a["L1_attn_fc2_b"]
    patches = a["x"].reshape(NB, 3, 6, 16, 6, 16).transpose(1, 3, 5, 0, 2, 4).reshape(6, P, NB * (NT - 1))
    wr = a["L0_ffn_Wr"].reshape(D, 1)
    arrays = {
        "constants": constants(),
        "vectors": vectors,
        "patches": patches.transpose(1, 0, 2),
        "token_w": a["L0_tok_proj_w"].T.reshape(6, P, D).transpose(1, 0, 2),
        "attn1_w": np.concatenate([halves(a[f"L0_attn_W{c}"].T, a[f"L0_attn_b{c}"]) for c in "qkv"], axis=2),
        "attn1_wo": context_rows(a["L0_attn_Wo"].T, a["L0_attn_bo"]),
        "attn2_w": np.concatenate(
            [halves(a[f"L0_ffn_W{c}"], a[f"L0_ffn_b{c}"]) for c in "qkvm"]
            + [halves(np.repeat(wr, TT, axis=1), a["L0_ffn_br"])], axis=2),
        "attn2_wo": context_rows(a["L0_ffn_Wo"], a["L0_ffn_bo"]),
        "ffn_w1": halves(a["L0_ffn_W1"])[:HALF],
        "ffn_b1": a["L0_ffn_bf1"].reshape(6, P).T,
        "ffn_w2": a["L0_ffn_W2"].reshape(6, P, D).transpose(1, 0, 2),
        "ffn_b2": a["L0_ffn_bf2"].reshape(1, D),
        "diff_w": np.concatenate(
            [halves(a["L1_attn_qv_w"]), halves(a["L1_attn_k_w"]),
             halves(a["L1_attn_fc1_w"]), halves(a["L1_ffn_W_fk"], a["L1_ffn_b_fk"]),
             halves(a["L1_ffn_W_rk"], a["L1_ffn_b_rk"])], axis=2),
        "diff_ln": np.stack([np.broadcast_to(a["L1_attn_ln_g"], (TT, D)), np.broadcast_to(a["L1_attn_ln_b"], (TT, D))], 1),
        "enc_w2": fc2,
        "proj_w": proj,
        "emb": np.stack([a["L1_ffn_emb_fk"], a["L1_ffn_emb_rk"]], axis=1),
        "feature_w": a["L1_ffn_f_know"].reshape(NN, 2, HALF, R).transpose(2, 0, 1, 3).reshape(HALF, NN, 2 * R),
        "restore_w": a["L1_ffn_r_know"].transpose(1, 0, 2),
    }
    arrays = {k: np.ascontiguousarray(v) for k, v in arrays.items()}
    nc = bacc.Bacc("TRN2", target_bir_lowering=False, num_devices=1)
    handles = {k: nc.dram_tensor(f"in_{k}", v.shape, mybir.dt.float32, kind="ExternalInput").ap() for k, v in arrays.items()}
    out = nc.dram_tensor("tower", (NB, NT, D), mybir.dt.float32, kind="ExternalOutput").ap()
    vit_tower(nc, handles, out)
    r = run_bass_kernel_spmd(nc, [{f"in_{k}": v for k, v in arrays.items()}], core_ids=[0])
    return r.results[0]["tower"]
```
